# Optimizing a Trainium2 kernel written in Bass

```python
import numpy as np
import jax
import jax.numpy as jnp

def _softmax(x, axis=-1):
    return jax.nn.softmax(x, axis=axis)

def _gelu(x):
    return jax.nn.gelu(x, approximate=True)

def _silu(x):
    return jax.nn.silu(x)

def _sigmoid(x):
    return jax.nn.sigmoid(x)

def _layernorm(x, axis=-1, eps=1e-05):
    m = jnp.mean(x, axis=axis, keepdims=True)
    v = jnp.var(x, axis=axis, keepdims=True)
    return (x - m) / jnp.sqrt(v + eps)

def _scatter_add(tgt, idx, src, axis=0):
    return tgt.at[idx].add(src)

def _segment_sum(src, seg, n):
    return jax.ops.segment_sum(src, seg, n)
kernel_name = 'mk_gnn_resnorm_d4_gnn_r8_88633e'

def setup_inputs(seed: int=0):
    np.random.seed(seed)
    _w = jnp.asarray

    def _rec_inputs():
        import jax
        import jax.numpy as jnp
        _gk = jax.random.key(seed)
        x = -0.0007083 + 1.001 * jax.random.normal(jax.random.fold_in(_gk, 1), (6250, 48), jnp.float32)
        src = jax.random.randint(jax.random.fold_in(_gk, 2), (200000,), 0, 6250, jnp.int32)
        dst = jnp.minimum((6250 * jax.random.uniform(jax.random.fold_in(_gk, 3), (200000,)) ** 2.0).astype(jnp.int32), 49999)
        _o = jnp.argsort(dst, stable=True)
        src = src[_o]
        dst = dst[_o]
        edge_attr_16 = 0.000196303 + 1.00016 * jax.random.normal(jax.random.fold_in(_gk, 12), (200000, 16), jnp.float32)
        edge_attr_40 = jax.random.uniform(jax.random.fold_in(_gk, 13), (200000, 40), jnp.float32, 0.0, 1)
        edge_weight = jax.random.uniform(jax.random.fold_in(_gk, 15), (200000,), jnp.float32, 0.0, 7.99999)
        node_type_119 = jax.random.randint(jax.random.fold_in(_gk, 16), (6250,), 0, 119, jnp.int32)
        node_vec = jax.random.uniform(jax.random.fold_in(_gk, 17), (6250,), jnp.float32, 0.0, 3.99996)
        return (x, src, dst, edge_attr_16, edge_attr_40, edge_weight, node_type_119, node_vec)
    x, src, dst, edge_attr_16, edge_attr_40, edge_weight, node_type_119, node_vec = _rec_inputs()

    def _L0_gnn_setup():
        import jax, jax.numpy as jnp
        import numpy as np
        N = 6250
        E = 150000
        H = 48
        RBF = 40
        L = 4
        NELEM = 119
        G = 32
        CUT = 6.0

        def _ln(x, g, b):
            m = x.mean(-1, keepdims=True)
            v = ((x - m) ** 2).mean(-1, keepdims=True)
            return (x - m) * jax.lax.rsqrt(v + 1e-05) * g + b
        key = jax.random.key(seed)
        k = jax.random.split(key, 16)
        s = 0.1
        return {'h': jax.random.normal(k[0], (N, H), jnp.float32), 'edge_index': jax.random.randint(k[1], (2, E), 0, N), 'edge_attr': jax.random.uniform(k[2], (E, RBF), dtype=jnp.float32), 'distances': jax.random.uniform(k[3], (E,), dtype=jnp.float32) * 8.0, 'atom_z': jax.random.randint(k[4], (N,), 0, NELEM), 'node_mult': jax.random.uniform(k[5], (N,), dtype=jnp.float32) * 3.0 + 1.0, 'batch': jnp.sort(jax.random.randint(k[6], (N,), 0, 64)), 'Wq': jax.random.normal(k[7], (L, H, H), jnp.float32) * s, 'gq': jnp.ones((L, H), jnp.float32), 'bq': jnp.zeros((L, H), jnp.float32), 'Wk': jax.random.normal(k[8], (L, H, H), jnp.float32) * s, 'gk': jnp.ones((L, H), jnp.float32), 'bk': jnp.zeros((L, H), jnp.float32), 'Wm': jax.random.normal(k[9], (L, H, H), jnp.float32) * s, 'Wu': jax.random.normal(k[10], (L, 2 * H, H), jnp.float32) * s, 'go': jnp.ones((L, H), jnp.float32), 'bo': jnp.zeros((L, H), jnp.float32), 'F1W': jax.random.normal(k[11], (RBF, H), jnp.float32) * s, 'F1b': jnp.zeros((H,), jnp.float32), 'F2W': jax.random.normal(k[12], (H, H), jnp.float32) * s, 'F2b': jnp.zeros((H,), jnp.float32), 'gn': jnp.ones((H,), jnp.float32), 'bn': jnp.zeros((H,), jnp.float32), 'emb': jax.random.normal(k[13], (NELEM, G), jnp.float32) * 0.01, 'adapt': jax.random.normal(k[14], (G, G), jnp.float32) * 0.01}
    _L0_gnn_all = _L0_gnn_setup()
    _L0_gnn_in = {k: v for k, v in _L0_gnn_all.items() if k in ('Wq', 'gq', 'bq', 'Wk', 'gk', 'bk', 'Wm', 'Wu', 'go', 'bo', 'F1W', 'F1b', 'F2W', 'F2b', 'gn', 'bn', 'emb', 'adapt')}
    del _L0_gnn_all

    def _L1_gnn_setup():
        import jax, jax.numpy as jnp
        import numpy as np
        N_NODES = 12500
        N_EDGES = 200000
        N_FEAT = 48
        N_EDGE_FEAT = 16
        HIDDEN = 128
        key = jax.random.key(seed)
        ks = jax.random.split(key, 8)
        tot = 2 * N_FEAT + N_EDGE_FEAT
        s1 = 1.0 / np.sqrt(tot)
        s2 = 1.0 / np.sqrt(HIDDEN)
        return {'x': jax.random.normal(ks[0], (N_NODES, N_FEAT), dtype=jnp.float32), 'edge_index': jax.random.randint(ks[1], (2, N_EDGES), 0, N_NODES, dtype=jnp.int64), 'edge_feat': jax.random.normal(ks[2], (N_EDGES, N_EDGE_FEAT), dtype=jnp.float32), 'W1': jax.random.normal(ks[3], (tot, HIDDEN), dtype=jnp.float32) * s1, 'b1': jnp.zeros((HIDDEN,), dtype=jnp.float32), 'W2': jax.random.normal(ks[4], (HIDDEN, HIDDEN), dtype=jnp.float32) * s2, 'b2': jnp.zeros((HIDDEN,), dtype=jnp.float32), 'W3': jax.random.normal(ks[5], (HIDDEN, N_FEAT), dtype=jnp.float32) * s2, 'b3': jnp.zeros((N_FEAT,), dtype=jnp.float32)}
    _L1_gnn_all = _L1_gnn_setup()
    _L1_gnn_in = {k: v for k, v in _L1_gnn_all.items() if k in ('W1', 'b1', 'W2', 'b2', 'W3', 'b3')}
    del _L1_gnn_all

    def _L2_gnn_setup():
        import jax, jax.numpy as jnp
        import numpy as np
        N_NODES = 12500
        N_EDGES = 200000
        D_FEAT = 48
        key = jax.random.key(seed)
        k1, k2, k3 = jax.random.split(key, 3)
        x = jax.random.normal(k1, (N_NODES, D_FEAT), dtype=jnp.float32)
        edge_index = jax.random.randint(k2, (2, N_EDGES), 0, N_NODES, dtype=jnp.int64)
        edge_weights = jax.random.uniform(k3, (N_EDGES,), dtype=jnp.float32)
        return {'x': x, 'edge_index': edge_index, 'edge_weights': edge_weights}
    _L2_gnn_all = _L2_gnn_setup()
    _L2_gnn_in = {k: v for k, v in _L2_gnn_all.items() if k in ()}
    del _L2_gnn_all

    def _L3_gnn_setup():
        import jax, jax.numpy as jnp
        import numpy as np
        key = jax.random.key(seed)
        k1, k2 = jax.random.split(key)
        N, C, E = (12500, 48, 200000)
        label_mat = jax.random.uniform(k1, (N, C), dtype=jnp.float32)
        edge_index = jax.random.randint(k2, (2, E), 0, N, dtype=jnp.int64)
        return {'label_mat': label_mat, 'edge_index': edge_index, 'num_nodes': N}
    _L3_gnn_all = _L3_gnn_setup()
    _L3_gnn_in = {k: v for k, v in _L3_gnn_all.items() if k in ()}
    del _L3_gnn_all
    return {'x': x, 'src': src, 'dst': dst, 'edge_attr_16': edge_attr_16, 'edge_attr_40': edge_attr_40, 'edge_weight': edge_weight, 'node_type_119': node_type_119, 'node_vec': node_vec, 'L0_gnn_Wq': _L0_gnn_in['Wq'], 'L0_gnn_gq': _L0_gnn_in['gq'], 'L0_gnn_bq': _L0_gnn_in['bq'], 'L0_gnn_Wk': _L0_gnn_in['Wk'], 'L0_gnn_gk': _L0_gnn_in['gk'], 'L0_gnn_bk': _L0_gnn_in['bk'], 'L0_gnn_Wm': _L0_gnn_in['Wm'], 'L0_gnn_Wu': _L0_gnn_in['Wu'], 'L0_gnn_go': _L0_gnn_in['go'], 'L0_gnn_bo': _L0_gnn_in['bo'], 'L0_gnn_F1W': _L0_gnn_in['F1W'], 'L0_gnn_F1b': _L0_gnn_in['F1b'], 'L0_gnn_F2W': _L0_gnn_in['F2W'], 'L0_gnn_F2b': _L0_gnn_in['F2b'], 'L0_gnn_gn': _L0_gnn_in['gn'], 'L0_gnn_bn': _L0_gnn_in['bn'], 'L0_gnn_emb': _L0_gnn_in['emb'], 'L0_gnn_adapt': _L0_gnn_in['adapt'], 'L1_gnn_W1': _L1_gnn_in['W1'], 'L1_gnn_b1': _L1_gnn_in['b1'], 'L1_gnn_W2': _L1_gnn_in['W2'], 'L1_gnn_b2': _L1_gnn_in['b2'], 'L1_gnn_W3': _L1_gnn_in['W3'], 'L1_gnn_b3': _L1_gnn_in['b3']}

def reference(x, src, dst, edge_attr_16, edge_attr_40, edge_weight, node_type_119, node_vec, L0_gnn_Wq, L0_gnn_gq, L0_gnn_bq, L0_gnn_Wk, L0_gnn_gk, L0_gnn_bk, L0_gnn_Wm, L0_gnn_Wu, L0_gnn_go, L0_gnn_bo, L0_gnn_F1W, L0_gnn_F1b, L0_gnn_F2W, L0_gnn_F2b, L0_gnn_gn, L0_gnn_bn, L0_gnn_emb, L0_gnn_adapt, L1_gnn_W1, L1_gnn_b1, L1_gnn_W2, L1_gnn_b2, L1_gnn_W3, L1_gnn_b3):
    import jax
    import jax.numpy as jnp

    def _L0_gnn_ref(h, edge_index, edge_attr, distances, atom_z, node_mult, batch, Wq, gq, bq, Wk, gk, bk, Wm, Wu, go, bo, F1W, F1b, F2W, F2b, gn, bn, emb, adapt):
        import jax, jax.numpy as jnp
        import numpy as np
        N = 6250
        E = 150000
        H = 48
        RBF = 40
        L = 4
        NELEM = 119
        G = 32
        CUT = 6.0

        def _ln(x, g, b):
            m = x.mean(-1, keepdims=True)
            v = ((x - m) ** 2).mean(-1, keepdims=True)
            return (x - m) * jax.lax.rsqrt(v + 1e-05) * g + b
        src, dst = (edge_index[0], edge_index[1])
        gate = jax.nn.silu(edge_attr @ F1W + F1b) @ F2W + F2b
        ei = emb[atom_z[src]]
        ej = emb[atom_z[dst]]
        gate = gate + (ei * (ej @ adapt)).sum(-1, keepdims=True)
        cw = jnp.where(distances < CUT, 0.5 * (jnp.cos(jnp.pi * distances / CUT) + 1.0), 0.0)
        mj = node_mult[dst]
        msg = gate * h[dst] * (cw * mj)[:, None]
        agg = jax.ops.segment_sum(msg, src, num_segments=N)
        tot = jnp.clip(jax.ops.segment_sum(mj, src, num_segments=N), 1e-08, None)
        h = _ln(h + agg / tot[:, None], gn, bn)
        logm = jnp.log(jnp.clip(node_mult, 1.0, None))
        for i in range(L):
            Q = _ln(h @ Wq[i], gq[i], bq[i])
            K = _ln(h @ Wk[i], gk[i], bk[i])
            qi = Q[src]
            kj = K[dst]
            score = (qi * kj).sum(-1) + 0.1 * (edge_attr * qi[:, :RBF]).sum(-1) + logm[dst]
            smax = jax.ops.segment_max(score, src, num_segments=N)
            es = jnp.exp(jnp.minimum(score - smax[src], 20.0))
            denom = jax.ops.segment_sum(es, src, num_segments=N)
            alpha = es / (denom[src] + 1e-10)
            m = h[dst] @ Wm[i]
            aggi = jax.ops.segment_sum(alpha[:, None] * m, src, num_segments=N)
            z = jnp.concatenate([h, aggi], axis=-1) @ Wu[i]
            z = jnp.where(z > 0, z, 0.01 * z)
            h = _ln(h + z, go[i], bo[i])
        return h

    def _L1_gnn_ref(x, edge_index, edge_feat, W1, b1, W2, b2, W3, b3):
        import jax, jax.numpy as jnp
        import numpy as np
        N_NODES = 12500
        N_EDGES = 200000
        N_FEAT = 48
        N_EDGE_FEAT = 16
        HIDDEN = 128
        source = edge_index[0]
        target = edge_index[1]
        edge = jnp.concatenate([x[source], x[target], edge_feat], axis=-1)
        h = jax.nn.relu(edge @ W1 + b1)
        h = jax.nn.relu(h @ W2 + b2)
        message = h @ W3 + b3
        n = x.shape[0]
        msum = jax.ops.segment_sum(message, target, num_segments=n)
        cnt = jax.ops.segment_sum(jnp.ones((target.shape[0],), dtype=x.dtype), target, num_segments=n)
        update = msum / jnp.maximum(cnt, 1.0)[:, None]
        return x + update

    def _L2_gnn_ref(x, edge_index, edge_weights):
        import jax, jax.numpy as jnp
        import numpy as np
        N_NODES = 12500
        N_EDGES = 200000
        D_FEAT = 48
        N = x.shape[0]
        row, col = (edge_index[0], edge_index[1])
        deg = jnp.zeros((N,), dtype=x.dtype).at[row].add(1.0)
        deg = jnp.maximum(deg, 1.0)
        norm = edge_weights / jnp.sqrt(deg[row] * deg[col])
        msg = x[row] * norm[:, None]
        out = jax.ops.segment_sum(msg, col, num_segments=N)
        return out

    def _L3_gnn_ref(label_mat, edge_index, num_nodes):
        import jax, jax.numpy as jnp
        import numpy as np
        row, col = (edge_index[0], edge_index[1])
        self_loop = jnp.arange(num_nodes, dtype=row.dtype)
        row = jnp.concatenate([row, self_loop])
        col = jnp.concatenate([col, self_loop])
        ones = jnp.ones_like(row, dtype=label_mat.dtype)
        deg = jax.ops.segment_sum(ones, row, num_segments=num_nodes)
        deg_inv_sqrt = jnp.where(deg > 0, jax.lax.rsqrt(deg), 0.0)
        norm = deg_inv_sqrt[row] * deg_inv_sqrt[col]
        msgs = label_mat[row] * norm[:, None]
        out = jax.ops.segment_sum(msgs, col, num_segments=num_nodes)
        return out
    edge_index = jnp.stack([src, dst])
    batch0 = jnp.zeros((6250,), jnp.int32)
    x = _layernorm(x + _L0_gnn_ref(x, edge_index, edge_attr_40, edge_weight, node_type_119, node_vec, batch0, L0_gnn_Wq, L0_gnn_gq, L0_gnn_bq, L0_gnn_Wk, L0_gnn_gk, L0_gnn_bk, L0_gnn_Wm, L0_gnn_Wu, L0_gnn_go, L0_gnn_bo, L0_gnn_F1W, L0_gnn_F1b, L0_gnn_F2W, L0_gnn_F2b, L0_gnn_gn, L0_gnn_bn, L0_gnn_emb, L0_gnn_adapt), axis=-1)
    x = _layernorm(x + _L1_gnn_ref(x, edge_index, edge_attr_16, L1_gnn_W1, L1_gnn_b1, L1_gnn_W2, L1_gnn_b2, L1_gnn_W3, L1_gnn_b3), axis=-1)
    x = _layernorm(x + _L2_gnn_ref(x, edge_index, edge_weight), axis=-1)
    x = _layernorm(x + _L3_gnn_ref(x, edge_index, 6250), axis=-1)
    return x

_drawn_inputs = setup_inputs


def setup_inputs(seed=0):
    import zlib

    import numpy as np

    out = dict(_drawn_inputs(seed))
    spreads = {'L0_gnn_gq': (1.0, 0.2),
     'L0_gnn_bq': (0.0, 0.1),
     'L0_gnn_gk': (1.0, 0.2),
     'L0_gnn_bk': (0.0, 2.0),
     'L0_gnn_go': (1.0, 0.2),
     'L0_gnn_bo': (0.0, 0.1),
     'L0_gnn_F1b': (0.0, 0.8),
     'L0_gnn_F2b': (0.0, 0.706),
     'L0_gnn_gn': (1.0, 0.2),
     'L0_gnn_bn': (0.0, 0.1),
     'L1_gnn_b1': (0.0, 0.1),
     'L1_gnn_b2': (0.0, 0.1),
     'L1_gnn_b3': (0.0, 0.1)}
    factors = {'edge_attr_16': 4.57,
     'edge_attr_40': 2.999,
     'L0_gnn_F1W': 3.167,
     'L0_gnn_F2W': 3.373,
     'L0_gnn_emb': 64.0,
     'L0_gnn_adapt': 64.0}
    for name, (base, spread) in spreads.items():
        noise = np.random.default_rng([zlib.crc32(name.encode()), seed]).standard_normal(out[name].shape)
        drawn = base * np.exp(spread * noise) if base else spread * noise
        out[name] = jnp.asarray(drawn.astype(out[name].dtype))
    for name, factor in factors.items():
        out[name] = (out[name] * factor).astype(out[name].dtype)
    return out
```

```python
from contextlib import ExitStack

import numpy as np
import concourse.bass as bass
from concourse import mybir

F32, I32, BF16 = mybir.dt.float32, mybir.dt.int32, mybir.dt.bfloat16
ALU = mybir.AluOpType
ACT = mybir.ActivationFunctionType
AX = mybir.AxisListType.X

P = 128
N = 6250
E = 200000
NT = -(-N // P)
NP = NT * P
J = 1564
EP = P * J
SORT_J = 2048
SORT_N = P * SORT_J
ORDERS = 2
IDX_BITS = 18
KEY_BIAS = 32


C = 34
CHUNKS = J // C
PAIRS = CHUNKS // 2
F = 48
RBF = 40
EF = 16
G = 32
HID = 128
LAYERS = 4
EPS = 1e-5
FAR = 3.0e38
SKIP = 1 << 20
REC_S = RBF + 2
REC_D = EF + 2
FILL_S = F + RBF + 1
ACC = F + 2
GRP = 7
ROUND = 12582912.0
COLS = 4
PAD_P = (EP - E) // 2
STEPS = -(-C // COLS)


class Chain:

    def __init__(self, eng, sem):
        self.eng, self.sem, self.n, self.base = eng, sem, 0, 0

    def step(self, ins):
        ins.then_inc(self.sem, 1)
        self.n += 1

    def wait(self):
        self.eng.wait_ge(self.sem, self.base + self.n)

    def done(self, ins):
        self.step(ins)
        self.wait()


def column(ap):
    return ap.rearrange("(n a) -> n a", a=1)


def sort_edges(nc, i, k):
    keys, sorted_bits, ident = (i["dst"], i["src"]), k.sorted, k.ident
    with ExitStack() as ctx:
        ph = Phase(nc, ctx, "sort")
        sb, sem = ph.sb, ph.sem
        W = ORDERS * SORT_J
        buf = [sb("a", [P, W], F32), sb("b", [P, W], F32)]
        pos = sb("pos", [P, SORT_J], I32)
        prow = sb("prow", [P, 1], I32)
        pbit = sb("pbit", [P, 9], I32)
        sgn = sb("sgn", [P, 9], F32)
        flip = sb("flip", [P, 9], F32)
        zero = sb("zero", [1, ORDERS], I32)
        turned = ph.ps("turned", [P, W])
        s_keys, s_pad, s_pos = sem("s_keys"), sem("s_pad"), sem("s_pos")
        s_step, s_ready, s_turned, s_out = sem("s_step"), sem("s_ready"), sem("s_turned"), sem("s_out")
        zeros = sb("sort_zeros", [P, C * FILL_S], F32)
        pad = sb("sort_pad", [PAD_P, 2, REC_S], F32)
        s_zeros, s_records = sem("s_zeros"), sem("s_records")
        full, rest = E // SORT_J, E % SORT_J
        block = ph.block()

        @block.gpsimd
        def _(pool):
            nc.gpsimd.iota(pos[:], [[1, SORT_J]], base=0, channel_multiplier=SORT_J).then_inc(s_pos, 1)
            nc.gpsimd.iota(prow[:], [[0, 1]], base=0, channel_multiplier=1).then_inc(s_pos, 1)

        @block.sync
        def _(sp):
            sp.wait_ge(s_pad, 1)
            for o, key in enumerate(keys):
                into = buf[1][:, o * SORT_J:(o + 1) * SORT_J].bitcast(I32)
                sp.dma_start(into[0:full, :], key[0:full * SORT_J].rearrange("(p j) -> p j", j=SORT_J)).then_inc(s_keys, 16)
                sp.dma_start(into[full:full + 1, 0:rest], key[full * SORT_J:E].rearrange("(p j) -> p j", p=1)).then_inc(s_keys, 16)
            sp.wait_ge(s_ready, 15)
            for o in range(ORDERS):
                sp.dma_start(sorted_bits[o, 1:1 + SORT_N].rearrange("(p j) -> p j", p=P),
                             buf[0][:, o * SORT_J:(o + 1) * SORT_J].bitcast(I32)).then_inc(s_out, 16)
                sp.dma_start(sorted_bits[o:o + 1, 0:1], zero[:, o:o + 1]).then_inc(s_out, 16)
            sp.wait_ge(s_out, 32 * ORDERS)

        @block.scalar
        def _(act):
            def put(into, cols, src):
                act.dma_start(into[0:E, cols], src, allow_slow_non_contiguous=True).then_inc(s_records, 16)

            put(k.raw_s, slice(0, RBF), i["edge_attr_40"])
            put(k.raw_s, slice(RBF, RBF + 1), column(i["edge_weight"]))
            put(k.raw_s.bitcast(I32), slice(RBF + 1, RBF + 2), column(i["dst"]))
            put(k.raw_d, slice(0, EF), i["edge_attr_16"])
            put(k.raw_d, slice(EF, EF + 1), column(i["edge_weight"]))
            put(k.raw_d.bitcast(I32), slice(EF + 1, EF + 2), column(i["src"]))
            act.wait_ge(s_zeros, 1)
            for raw, w in ((k.raw_s, REC_S), (k.raw_d, REC_D)):
                act.dma_start(raw[E:EP].rearrange("(p r) w -> p r w", r=2), pad[:, :, REC_S - w:]).then_inc(s_records, 16)
            with act.Fori(0, CHUNKS) as n:
                for table, w in ((k.fill_s, FILL_S), (k.fill_d, F)):
                    act.dma_start(table.rearrange("(p j) w -> p j w", p=P)[:, bass.ds(n * C, C), :],
                                  zeros[:, 0:C * w].rearrange("p (j w) -> p j w", w=w)).then_inc(s_records, 16)
            act.wait_ge(s_records, 16 * (8 + 2 * CHUNKS))

        @block.tensor
        def _(pe):
            for n in range(14):
                pe.wait_ge(s_ready, n + 1)
                for b in range(W // P):
                    ins = nc.tensor.transpose(turned[:, b * P:(b + 1) * P], buf[0][:, b * P:(b + 1) * P], ident[:])
                ins.then_inc(s_turned, 1)

        @block.vector
        def _(dve):
            ch = Chain(dve, s_step)
            nc.vector.memset(zero[:], 0.0)
            ch.done(nc.vector.memset(pad[:], 0.0))
            nc.vector.memset(pad[:, :, REC_S - 1].bitcast(I32), N)
            nc.vector.memset(zeros[:], 0.0).then_inc(s_zeros, 1)
            nc.vector.memset(buf[1][:].bitcast(I32), N).then_inc(s_pad, 1)
            dve.wait_ge(s_pos, 2)
            for m in range(11, 18):
                ch.done(nc.vector.tensor_scalar(pbit[:, m - 10:m - 9], prow[:], m - 11, 1, ALU.logical_shift_right, ALU.bitwise_and))
            ch.step(nc.vector.memset(sgn[:], 1.0))
            ch.done(nc.vector.memset(flip[:], 1.0))
            ch.done(nc.vector.tensor_scalar(sgn[:, 1:8], pbit[:, 1:8], -2.0, 1.0, ALU.mult, ALU.add))
            ch.done(nc.vector.tensor_tensor(flip[:, 1:9], sgn[:, 1:9], sgn[:, 0:8], ALU.mult))
            dve.wait_ge(s_keys, 16 * 2 * ORDERS)
            key = buf[1][:].bitcast(I32)
            rec = buf[0][:].bitcast(I32)
            ch.done(nc.vector.tensor_scalar(key, key, float(KEY_BIAS), None, ALU.add))
            ch.done(nc.vector.tensor_scalar(rec, key, IDX_BITS, None, ALU.logical_shift_left))
            for o in range(ORDERS):
                at = slice(o * SORT_J, (o + 1) * SORT_J)
                ch.step(nc.vector.tensor_tensor(rec[:, at], rec[:, at], pos[:], ALU.bitwise_or))
            ch.wait()
            cur = 0

            def compare(m, d, up_only):
                nonlocal cur
                a, b = buf[cur], buf[1 - cur]
                if up_only:
                    va = a[:].rearrange("p (n s d) -> p s n d", s=2, d=d)
                    vb = b[:].rearrange("p (n s d) -> p s n d", s=2, d=d)
                    ch.step(nc.vector.tensor_tensor(vb[:, 0], va[:, 0], va[:, 1], ALU.min))
                    ch.step(nc.vector.tensor_tensor(vb[:, 1], va[:, 0], va[:, 1], ALU.max))
                else:
                    for down in range(2):
                        k = 2 ** m
                        va = a[:].rearrange("p (g w r) -> p w g r", w=2, r=k)[:, down].rearrange("p g (n s d) -> p s g n d", s=2, d=d)
                        vb = b[:].rearrange("p (g w r) -> p w g r", w=2, r=k)[:, down].rearrange("p g (n s d) -> p s g n d", s=2, d=d)
                        ch.step(nc.vector.tensor_tensor(vb[:, down], va[:, 0], va[:, 1], ALU.min))
                        ch.step(nc.vector.tensor_tensor(vb[:, 1 - down], va[:, 0], va[:, 1], ALU.max))
                ch.wait()
                cur = 1 - cur

            turns = 0

            def turn():
                nonlocal cur, turns
                if cur == 1:
                    ch.done(nc.vector.tensor_copy(buf[0][:], buf[1][:]))
                dve.sem_inc(s_ready, 1)
                turns += 1
                dve.wait_ge(s_turned, turns)
                ch.done(nc.vector.tensor_copy(buf[0][:], turned[:]))
                cur = 0

            for m in range(1, 19):
                if m >= 11:
                    ch.done(nc.vector.tensor_scalar(buf[cur][:], buf[cur][:], flip[:, m - 10:m - 9], None, ALU.mult))
                if m >= 12:
                    turn()
                    for b in range(m - 12, -1, -1):
                        compare(m, 2 ** b, True)
                    turn()
                for b in range(min(m, 11) - 1, -1, -1):
                    compare(m, 2 ** b, m >= 11)
            if cur == 1:
                ch.done(nc.vector.tensor_copy(buf[0][:], buf[1][:]))
            dve.sem_inc(s_ready, 1)


assert CHUNKS * C == J and PAIRS * 2 == CHUNKS and NT % GRP == 0


def bc(ap, n):
    return ap.unsqueeze(2).to_broadcast([ap.shape[0], ap.shape[1], n])


def rows_of(ap, n):
    return ap.unsqueeze(1).to_broadcast([ap.shape[0], n, ap.shape[1]])


def clear(nc, sems):
    span = range(min(s.num for s in sems), max(s.num for s in sems) + 1)
    nc.gpsimd.dma_reset(span)
    nc.gpsimd.sem_clear(span)
    nc.all_engine_barrier()


class Phase:

    def __init__(self, nc, ctx, tag):
        self.nc, self.ctx, self.tag, self.sems = nc, ctx, tag, []

    def sb(self, name, shape, dt=F32):
        return self.ctx.enter_context(self.nc.sbuf_tensor(f"{self.tag}_{name}", shape, dt))

    def ps(self, name, shape, dt=F32):
        return self.ctx.enter_context(self.nc.psum_tensor(f"{self.tag}_{name}", shape, dt))

    def sem(self, name):
        s = self.ctx.enter_context(self.nc.semaphore(f"{self.tag}_{name}"))
        self.sems.append(s)
        return s

    def block(self):
        self.ctx.callback(clear, self.nc, self.sems)
        return self.ctx.enter_context(self.nc.Block())


def gather(nc, out, table, index):
    return nc.gpsimd.indirect_dma_start(out=out, out_offset=None, in_=table,
                                        in_offset=bass.IndirectOffsetOnAxis(ap=index, axis=0))


def scatter(nc, table, index, rows, last):
    return nc.gpsimd.indirect_dma_start(out=table, out_offset=bass.IndirectOffsetOnAxis(ap=index, axis=0), in_=rows,
                                        in_offset=None, bounds_check=last, oob_is_err=False)


def open_stores(sp, k, s_stored):
    for b in range(2):
        sp.dma_start(k.spare[b:b + 1, :], k.ones[b:b + 1, 0:1]).then_inc(s_stored[b], 16)


def pool_gathers(nc, pool, index, staged, rows, width, table, s_staged, s_rows, used, s_turn):
    with pool.Fori(0, PAIRS) as t:
        for b in range(2):
            for s, n in used[b]:
                pool.wait_ge(s, (t + 1) * n)
            nc.gpsimd.tensor_copy(staged[:, b], index[:, bass.ds((t * 2 + b) * C, C)]).then_inc(s_staged, 1)
            pool.wait_ge(s_staged, t * 2 + b + 1)
            pool.sem_inc(s_turn, 1)
            for c in range(C):
                gather(nc, rows[b][:, c, 0:width], table, staged[:, b, c:c + 1]).then_inc(s_rows[b], 16)


class Projector:

    def __init__(self, ph, ident):
        self.nc, self.ident = ph.nc, ident
        self.pst = [ph.ps(f"turn{b}", [P, GRP, P]) for b in range(2)]
        self.psp = [ph.ps(f"prod{b}", [P, GRP, P]) for b in range(2)]
        self.st = [ph.sb(f"turned{b}", [P, GRP, P]) for b in range(2)]
        self.s_t, self.s_tc, self.s_p, self.s_pc = (ph.sem(n) for n in ("s_turned", "s_turned_copied", "s_product", "s_product_copied"))
        self.npe = self.nact = self.ndve = 0

    def pe(self, pe, src, K, w, M):
        n0, groups = self.npe, NT // GRP
        for g in range(groups + 1):
            if g < groups:
                i = n0 + g
                if i >= 2:
                    pe.wait_ge(self.s_tc, i - 1)
                for k in range(GRP):
                    ins = self.nc.tensor.transpose(self.pst[i % 2][0:K, k, :], src(g * GRP + k), self.ident[:])
                ins.then_inc(self.s_t, 1)
            if g >= 1:
                i = n0 + g - 1
                pe.wait_ge(self.s_tc, i + 1)
                if i >= 2:
                    pe.wait_ge(self.s_pc, i - 1)
                for k in range(GRP):
                    ins = self.nc.tensor.matmul(self.psp[i % 2][:, k, 0:M], self.st[i % 2][0:K, k, :], w, start=True, stop=True)
                ins.then_inc(self.s_p, 1)
        self.npe += groups

    def act(self, act, K):
        for i in range(self.nact, self.nact + NT // GRP):
            act.wait_ge(self.s_t, i + 1)
            if i >= 2:
                act.wait_ge(self.s_p, i - 1)
            self.nc.scalar.activation(self.st[i % 2][0:K], self.pst[i % 2][0:K], ACT.Copy).then_inc(self.s_tc, 1)
        self.nact += NT // GRP

    def dve(self, dve, dst, M):
        for g in range(NT // GRP):
            i = self.ndve + g
            dve.wait_ge(self.s_p, i + 1)
            self.nc.vector.tensor_copy(dst[:, g * GRP:(g + 1) * GRP, 0:M], self.psp[i % 2][:, :, 0:M]).then_inc(self.s_pc, 1)
        self.ndve += NT // GRP
        dve.wait_ge(self.s_pc, self.ndve)


class Norm:

    def __init__(self, ph):
        self.nc = ph.nc
        self.stat = ph.sb("stat", [P, NT])
        self.root = ph.sb("root", [P, NT])
        self.sq = ph.sb("sq", [P, NT, F])
        self.s_var, self.s_root = ph.sem("s_var"), ph.sem("s_root")
        self.nd = self.na = 0

    def rsqrt(self, dve, ch):
        self.nd += 1
        dve.sem_inc(self.s_var, 1)
        dve.wait_ge(self.s_root, self.nd)
        ch.done(self.nc.vector.reciprocal(self.stat[:], self.root[:]))

    def variance(self, ch, centred):
        ch.done(self.nc.vector.tensor_tensor(self.sq[:], centred, centred, ALU.mult))
        ch.done(self.nc.vector.tensor_reduce(self.stat[:], self.sq[:], AX, ALU.add))
        ch.done(self.nc.vector.tensor_scalar(self.stat[:], self.stat[:], 1.0 / F, EPS, ALU.mult, ALU.add))

    def dve(self, dve, ch, x, out, gain=None, bias=None):
        v = self.nc.vector
        ch.done(v.tensor_reduce(self.stat[:], x, AX, ALU.add))
        ch.done(v.tensor_scalar(self.stat[:], self.stat[:], 1.0 / F, None, ALU.mult))
        ch.done(v.tensor_tensor(out, x, bc(self.stat[:], F), ALU.subtract))
        self.variance(ch, out)
        self.rsqrt(dve, ch)
        ch.done(v.tensor_tensor(out, out, bc(self.stat[:], F), ALU.mult))
        if gain is not None:
            ch.done(v.tensor_tensor(out, out, rows_of(gain, NT), ALU.mult))
            ch.done(v.tensor_tensor(out, out, rows_of(bias, NT), ALU.add))

    def act(self, act):
        self.na += 1
        act.wait_ge(self.s_var, self.na)
        self.nc.scalar.activation(self.root[:], self.stat[:], ACT.Sqrt).then_inc(self.s_root, 1)


def constants(nc, k):
    with ExitStack() as ctx:
        ph = Phase(nc, ctx, "const")
        s, s_i = ph.sem("s_filled"), ph.sem("s_iota")
        block = ph.block()

        @block.gpsimd
        def _(pool):
            g = nc.gpsimd
            g.iota(k.iota[:], [[1, P]], base=0, channel_multiplier=0, allow_small_or_imprecise_dtypes=True)
            g.iota(k.rowstart[:], [[0, 1]], base=0, channel_multiplier=J, allow_small_or_imprecise_dtypes=True).then_inc(s_i, 1)
            g.memset(k.ones[:], 1.0)
            g.memset(k.ident[:], 0.0).then_inc(s, 1)
            g.memset(k.below[:], 1.0).then_inc(s, 1)
            g.memset(k.above[:], 1.0).then_inc(s, 1)
            pool.wait_ge(s, 3)
            g.affine_select(out=k.ident[:], in_=k.ident[:], compare_op=ALU.not_equal, fill=1.0, base=0, pattern=[[-1, P]], channel_multiplier=1)
            g.affine_select(out=k.below[:], in_=k.below[:], compare_op=ALU.is_gt, fill=0.0, base=0, pattern=[[-1, P]], channel_multiplier=1)
            g.affine_select(out=k.above[:], in_=k.above[:], compare_op=ALU.is_gt, fill=0.0, base=0, pattern=[[1, P]], channel_multiplier=-1)


def unpack(nc, k, o):
    with ExitStack() as ctx:
        ph = Phase(nc, ctx, f"unpack{o}")
        bits, prev = ph.sb("bits", [P, J], I32), ph.sb("prev", [P, J], I32)
        prevf = ph.sb("prevf", [P, J])
        s_in, s_step = ph.sem("s_in"), ph.sem("s_step")
        keyf, perm, keep, keepr = k.keyf, k.perm[o], k.keep[o], k.keepr[o]
        block = ph.block()

        @block.sync
        def _(sp):
            sp.dma_start(bits[:], k.sorted[o, 1:1 + EP].rearrange("(p j) -> p j", p=P)).then_inc(s_in, 16)
            sp.dma_start(prev[:], k.sorted[o, 0:EP].rearrange("(p j) -> p j", p=P)).then_inc(s_in, 16)

        @block.vector
        def _(dve):
            v = nc.vector
            ch = Chain(dve, s_step)
            dve.wait_ge(s_in, 32)
            ch.done(v.tensor_scalar(perm[:], bits[:], (1 << IDX_BITS) - 1, None, ALU.bitwise_and))
            ch.step(v.tensor_scalar(bits[:], bits[:], IDX_BITS, None, ALU.logical_shift_right))
            ch.done(v.tensor_scalar(prev[:], prev[:], IDX_BITS, None, ALU.logical_shift_right))
            ch.step(v.tensor_scalar(keyf[:], bits[:], float(-KEY_BIAS), None, ALU.add))
            ch.done(v.tensor_scalar(prevf[:], prev[:], float(-KEY_BIAS), None, ALU.add))
            ch.done(v.tensor_tensor(keep[:], keyf[:], prevf[:], ALU.is_equal))
            ch.step(v.tensor_copy(k.first[o][:], keyf[:, 0:1]))
            ch.step(v.tensor_copy(k.firstf[o][:], keyf[:, 0:1]))
            ch.step(v.tensor_copy(k.lastf[o][:], keyf[:, J - 1:J]))
            ch.done(v.tensor_copy(keepr[:], keep[:]))
            ch.done(v.memset(keepr[:, 0:1], 0.0))
            if o == 1:
                ch.done(v.tensor_scalar(k.pen[:], keepr[:], -1.0, FAR, ALU.add, ALU.mult))


def records(nc, k, o):
    with ExitStack() as ctx:
        ph = Phase(nc, ctx, f"records{o}")
        W = REC_S if o else REC_D
        raw, arranged = (k.raw_s, k.edges_s) if o else (k.raw_d, k.edges_d)
        other = k.other[o]
        staged = ph.sb("staged", [P, 2, C], I32)
        rows = [ph.sb(f"rows{b}", [P, C, W]) for b in range(2)]
        quot, rem = ph.sb("quot", [P, C]), ph.sb("rem", [P, C])
        hot_p = [ph.sb(f"hot_p{b}", [P, C, P], BF16) for b in range(2)]
        hot_t = [ph.sb(f"hot_t{b}", [P, C, NT], BF16) for b in range(2)]
        part = [ph.ps(f"part{b}", [P, 512]) for b in range(2)]
        s_staged, s_step, s_ready = ph.sem("s_staged"), ph.sem("s_step"), ph.sem("s_ready")
        s_rows, s_stored, s_kept = ([ph.sem(f"{n}{b}") for b in range(2)] for n in ("s_rows", "s_stored", "s_kept"))
        s_hot, s_part = ph.sem("s_hot"), ph.sem("s_part")
        block = ph.block()

        @block.gpsimd
        def _(pool):
            pool.wait_ge(s_ready, 1)
            pool_gathers(nc, pool, k.perm[o], staged, rows, W, raw, s_staged, s_rows,
                         [[(s_stored[b], 16), (s_kept[b], 1)] for b in range(2)], ph.sem("s_turn"))

        @block.sync
        def _(sp):
            open_stores(sp, k, s_stored)
            sp.sem_inc(s_ready, 1)
            with sp.Fori(0, PAIRS) as t:
                for b in range(2):
                    sp.wait_ge(s_rows[b], (t + 1) * (16 * C))
                    sp.dma_start(arranged.rearrange("(p j) w -> p j w", p=P)[:, bass.ds((t * 2 + b) * C, C), :], rows[b][:]).then_inc(s_stored[b], 16)
            for b in range(2):
                sp.wait_ge(s_stored[b], 16 * (PAIRS + 1))

        @block.tensor
        def _(pe):
            with pe.Fori(0, PAIRS) as t:
                for b in range(2):
                    pe.wait_ge(s_hot, t * 2 + b + 1)
                    for c in range(C):
                        ins = nc.tensor.matmul(part[b][:, 0:NT], hot_p[b][:, c, :], hot_t[b][:, c, :], start=(c == 0), stop=(c == C - 1))
                    ins.then_inc(s_part, 1)

        @block.vector
        def _(dve):
            v = nc.vector
            ch = Chain(dve, s_step)
            ch.done(v.memset(k.count[o][:], 0.0))
            for b in range(2):
                dve.sem_inc(s_kept[b], 1)
            PER = 10 + 2 * o * 0 + (0 if o else 2)
            with dve.Fori(0, PAIRS) as t:
                ch.n, ch.base = 1, t * PER
                for b in range(2):
                    at = bass.ds((t * 2 + b) * C, C)
                    ch.done(v.tensor_scalar(quot[:], k.keyf[:, at], float(-(NT // 2)), 1.0 / NT, ALU.add, ALU.mult))
                    ch.done(v.tensor_scalar(quot[:], quot[:], ROUND, -ROUND, ALU.add, ALU.add))
                    ch.done(v.scalar_tensor_tensor(out=rem[:], in0=quot[:], scalar=float(-NT), in1=k.keyf[:, at], op0=ALU.mult, op1=ALU.add))
                    v.tensor_tensor(hot_p[b][:], bc(quot[:], P), rows_of(k.iota[:], C), ALU.is_equal)
                    v.tensor_tensor(hot_t[b][:], bc(rem[:], NT), rows_of(k.iota[:, 0:NT], C), ALU.is_equal).then_inc(s_hot, 1)
                    dve.wait_ge(s_part, t * 2 + b + 1)
                    ch.done(v.tensor_tensor(k.count[o][:], k.count[o][:], part[b][:, 0:NT], ALU.add))
                    dve.wait_ge(s_rows[b], (t + 1) * (16 * C))
                    if o == 0:
                        ch.done(v.tensor_copy(k.weight[:, at], rows[b][:, :, EF]))
                    ch.done(v.tensor_copy(other[:, at], rows[b][:, :, W - 1].bitcast(I32)))
                    dve.sem_inc(s_kept[b], 1)
            assert ch.n - 1 == PER


def segments(nc, k, o):
    with ExitStack() as ctx:
        ph = Phase(nc, ctx, f"segments{o}")
        cum, tot, pre = ph.sb("cum", [P, NT]), ph.sb("tot", [P, 1]), ph.sb("pre", [P, 1])
        one = ph.sb("one", [P, NT])
        flag, tmp = ph.sb("flag", [P, NT]), ph.sb("tmp", [P, NT])
        lastpos = ph.sb("lastpos", [P, NT])
        at1, f1, g1 = ph.sb("at1", [P, 1]), ph.sb("f1", [P, 1]), ph.sb("g1", [P, 1])
        diag = ph.sb("diag", [P, P])
        ps1, ps2 = ph.ps("ps1", [P, 512]), ph.ps("ps2", [P, 512])
        s_step, s_tot, s_pre, s_pos, s_put, s_got, s_diag, s_row = (ph.sem(n) for n in ("s_step", "s_tot", "s_pre", "s_pos", "s_put", "s_got", "s_diag", "s_row"))
        block = ph.block()

        @block.tensor
        def _(pe):
            pe.wait_ge(s_tot, 1)
            nc.tensor.matmul(ps1[:, 0:1], k.above[:], tot[:], start=True, stop=True).then_inc(s_pre, 1)
            pe.wait_ge(s_diag, 1)
            nc.tensor.matmul(ps2[:, 0:P], k.ones[:], diag[:], start=True, stop=True).then_inc(s_row, 1)

        @block.sync
        def _(sp):
            sp.wait_ge(s_pos, 1)
            sp.dma_start(k.lastpos[o].rearrange("(p t) a -> p (t a)", p=P), lastpos[:]).then_inc(s_put, 16)

        @block.gpsimd
        def _(pool):
            pool.wait_ge(s_put, 16)
            gather(nc, at1[:, 0:1], k.lastpos[o], k.first[o][:, 0:1]).then_inc(s_got, 16)

        @block.vector
        def _(dve):
            v = nc.vector
            ch = Chain(dve, s_step)
            ch.done(v.memset(one[:], 1.0))
            ch.done(v.tensor_tensor_scan(cum[:], one[:], k.count[o][:], 0.0, ALU.mult, ALU.add))
            ch.done(v.tensor_copy(tot[:], cum[:, NT - 1:NT]))
            dve.sem_inc(s_tot, 1)
            dve.wait_ge(s_pre, 1)
            ch.done(v.tensor_copy(pre[:], ps1[:, 0:1]))
            ch.done(v.tensor_scalar(cum[:], cum[:], pre[:], None, ALU.add))
            ch.step(v.tensor_scalar(flag[:], k.count[o][:], 0.0, None, ALU.is_equal))
            ch.step(v.tensor_tensor(tmp[:], cum[:], k.count[o][:], ALU.subtract))
            ch.done(v.tensor_scalar(lastpos[:], cum[:], -1.0, None, ALU.add))
            dve.sem_inc(s_pos, 1)
            ch.done(v.scalar_tensor_tensor(out=k.start[o][:], in0=flag[:], scalar=float(SKIP), in1=tmp[:], op0=ALU.mult, op1=ALU.add))
            ch.done(v.tensor_scalar(tmp[:], lastpos[:], -1.0, float(EP), ALU.mult, ALU.add))
            ch.done(v.tensor_tensor(tmp[:], tmp[:], flag[:], ALU.mult))
            ch.done(v.tensor_tensor(k.end[o][:], tmp[:], lastpos[:], ALU.add))
            ch.done(v.tensor_scalar(diag[:], k.ident[:], k.lastf[o][:], None, ALU.mult))
            dve.sem_inc(s_diag, 1)
            dve.wait_ge(s_row, 1)
            ch.done(v.tensor_scalar(diag[:], ps2[:, 0:P], k.firstf[o][:], None, ALU.is_equal))
            ch.done(v.tensor_tensor(k.mask[o][:], diag[:], k.below[:], ALU.mult))
            dve.wait_ge(s_got, 16)
            ch.done(v.tensor_tensor(f1[:], at1[:], k.rowstart[:], ALU.subtract))
            ch.done(v.tensor_scalar(f1[:], f1[:], float(J), None, ALU.is_lt))
            ch.done(v.tensor_tensor(f1[:], f1[:], k.keep[o][:, 0:1], ALU.mult))
            ch.done(v.tensor_scalar(g1[:], f1[:], -1.0, 1.0, ALU.mult, ALU.add))
            ch.done(v.tensor_tensor(at1[:], at1[:], f1[:], ALU.mult))
            ch.step(v.scalar_tensor_tensor(out=k.cread[o][:], in0=g1[:], scalar=float(EP), in1=at1[:], op0=ALU.mult, op1=ALU.add))
            ch.done(v.scalar_tensor_tensor(out=k.cwrite[o][:], in0=g1[:], scalar=float(SKIP), in1=at1[:], op0=ALU.mult, op1=ALU.add))


def collect(nc, k, o, res, W, tail, out, softmax, tag):
    with ExitStack() as ctx:
        ph = Phase(nc, ctx, tag)
        here, fixed = ph.sb("here", [P, W]), ph.sb("fixed", [P, W])
        diag, wt, wtT = ph.sb("diag", [P, P]), ph.sb("wt", [P, P]), ph.sb("wtT", [P, P])
        cm, m2, ex = ph.sb("cm", [P, 1]), ph.sb("m2", [P, 1]), ph.sb("ex", [P, 2])
        psr, pst, psc = ph.ps("psr", [P, 512]), ph.ps("pst", [P, 512]), ph.ps("psc", [P, 512])
        s_step, s_here, s_diag, s_row, s_arg, s_exp, s_w, s_wT, s_wTc, s_c, s_fixed, s_put, s_got = (
            ph.sem(n) for n in ("s_step", "s_here", "s_diag", "s_row", "s_arg", "s_exp", "s_w", "s_wT", "s_wTc", "s_c", "s_fixed", "s_put", "s_got"))
        with nc.Block() as block:
            @block.gpsimd
            def _(pool):
                gather(nc, here[:], res, k.cread[o][:, 0:1]).then_inc(s_here, 16)
                pool.wait_ge(s_fixed, 1)
                scatter(nc, res, k.cwrite[o][:, 0:1], fixed[:], EP - 1).then_inc(s_put, 16)
                pool.wait_ge(s_put, 16)
                for t in range(NT):
                    gather(nc, out[:, t, :], res, k.end[o][:, t:t + 1]).then_inc(s_got, 16)
                pool.wait_ge(s_got, 16 * NT)

            @block.tensor
            def _(pe):
                if softmax:
                    pe.wait_ge(s_diag, 1)
                    nc.tensor.matmul(psr[:, 0:P], k.ones[:], diag[:], start=True, stop=True).then_inc(s_row, 1)
                pe.wait_ge(s_w, 1)
                nc.tensor.transpose(pst[:, 0:P], wt[:], k.ident[:]).then_inc(s_wT, 1)
                pe.wait_ge(s_wTc, 1)
                nc.tensor.matmul(psc[:, 0:W], wtT[:], tail, start=True, stop=True).then_inc(s_c, 1)

            @block.scalar
            def _(act):
                if softmax:
                    act.wait_ge(s_arg, 1)
                    nc.scalar.activation(wt[:], wt[:], ACT.Exp).then_inc(s_exp, 1)
                    act.wait_ge(s_arg, 2)
                    nc.scalar.activation(ex[:], ex[:], ACT.Exp).then_inc(s_exp, 1)

            @block.vector
            def _(dve):
                v = nc.vector
                ch = Chain(dve, s_step)
                if softmax:
                    ch.done(v.tensor_scalar(diag[:], k.ident[:], tail[:, F + 1:F + 2], None, ALU.mult))
                    dve.sem_inc(s_diag, 1)
                    ch.done(v.tensor_scalar(wt[:], k.mask[o][:], -1.0, FAR, ALU.add, ALU.mult))
                    dve.wait_ge(s_row, 1)
                    ch.done(v.tensor_tensor(wt[:], wt[:], psr[:, 0:P], ALU.add))
                    ch.done(v.tensor_reduce(cm[:], wt[:], AX, ALU.max))
                    ch.done(v.tensor_scalar(wt[:], wt[:], cm[:], None, ALU.subtract))
                    dve.sem_inc(s_arg, 1)
                    dve.wait_ge(s_exp, 1)
                    ch.done(v.tensor_tensor(wt[:], wt[:], k.mask[o][:], ALU.mult))
                else:
                    ch.done(v.tensor_copy(wt[:], k.mask[o][:]))
                dve.sem_inc(s_w, 1)
                dve.wait_ge(s_wT, 1)
                ch.done(v.tensor_copy(wtT[:], pst[:, 0:P]))
                dve.sem_inc(s_wTc, 1)
                dve.wait_ge(s_c, 1)
                dve.wait_ge(s_here, 16)
                if softmax:
                    ch.done(v.tensor_tensor(m2[:], here[:, F + 1:F + 2], cm[:], ALU.max))
                    ch.step(v.tensor_tensor(ex[:, 0:1], here[:, F + 1:F + 2], m2[:], ALU.subtract))
                    ch.done(v.tensor_tensor(ex[:, 1:2], cm[:], m2[:], ALU.subtract))
                    dve.sem_inc(s_arg, 1)
                    dve.wait_ge(s_exp, 2)
                    ch.done(v.tensor_scalar(here[:], here[:], ex[:, 0:1], None, ALU.mult))
                    ch.done(v.scalar_tensor_tensor(out=fixed[:], in0=psc[:, 0:W], scalar=ex[:, 1:2], in1=here[:], op0=ALU.mult, op1=ALU.add))
                    ch.done(v.tensor_copy(fixed[:, F + 1:F + 2], m2[:]))
                else:
                    ch.done(v.tensor_tensor(fixed[:], here[:], psc[:, 0:W], ALU.add))
                dve.sem_inc(s_fixed, 1)

        clear(nc, ph.sems)


def load_nodes(sp, ins, into, width, sem):
    full, rest = N // NT, N % NT
    sp.dma_start(into[0:full], ins[0:full * NT].rearrange("(p t) f -> p t f", t=NT)).then_inc(sem, 16)
    sp.dma_start(into[full:full + 1, 0:rest], ins[full * NT:N].rearrange("(p t) f -> p t f", p=1)).then_inc(sem, 16)


def scan_columns(nc, out, keep, val, before, width):
    for f in range(width):
        ins = nc.vector.tensor_tensor_scan(out[:, :, f], keep, val[:, :, f], before[:, f:f + 1], ALU.mult, ALU.add)
    return ins


def stream(sp, load, store):
    for b in range(2):
        load(0, b)
    with sp.Fori(0, PAIRS - 1) as t:
        for b in range(2):
            store(t, b)
            load(t + 1, b)
    for b in range(2):
        store(PAIRS - 1, b)


def store_sums(sp, k, res, sums, s_sums, s_stored):
    open_stores(sp, k, s_stored)

    def store(t, b):
        sp.wait_ge(s_sums[b], t + 1)
        sp.dma_start(res[0:EP].rearrange("(p j) w -> p j w", p=P)[:, bass.ds((t * 2 + b) * C, C), :], sums[b][:]).then_inc(s_stored[b], 16)
    return store


def node_inputs(nc, k, i):
    with ExitStack() as ctx:
        ph = Phase(nc, ctx, "nodes")
        emb, embT, adapt = ph.sb("emb", [P, G]), ph.sb("embT", [G, P]), ph.sb("adapt", [G, G])
        both = ph.sb("both", [P, 2 * G])
        z = ph.sb("z", [P, NT, 1], I32)
        zrow = ph.sb("zrow", [P, NT, 2 * G])
        mult = ph.sb("mult", [P, NT, 1])
        table = ph.sb("table", [P, NT, F + G + 1])
        fill = ph.sb("fill", [P, NT, FILL_S])
        low = ph.sb("low", [P, NT])
        neutral = ph.sb("neutral", [1, ACC])
        ps = ph.ps("ps", [P, 512])
        s_in, s_zero, s_step, s_t, s_tc, s_m, s_both, s_z, s_tab, s_out, s_fill, s_low, s_log = (
            ph.sem(n) for n in ("s_in", "s_zero", "s_step", "s_t", "s_tc", "s_m", "s_both", "s_z", "s_tab", "s_out", "s_fill", "s_low", "s_log"))
        NIN = 16 * 8
        NE = i["L0_gnn_emb"].shape[0]
        block = ph.block()

        @block.sync
        def _(sp):
            sp.wait_ge(s_zero, 1)
            load_nodes(sp, i["x"], k.x, F, s_in)
            load_nodes(sp, column(i["node_type_119"]), z, 1, s_in)
            load_nodes(sp, column(i["node_vec"]), mult, 1, s_in)
            sp.dma_start(emb[0:NE, :], i["L0_gnn_emb"]).then_inc(s_in, 16)
            sp.dma_start(adapt[:], i["L0_gnn_adapt"]).then_inc(s_in, 16)
            sp.wait_ge(s_both, 1)
            sp.dma_start(k.by_type, both[:]).then_inc(s_out, 16)
            sp.wait_ge(s_tab, 1)
            sp.dma_start(k.table0.rearrange("(p t) w -> p t w", p=P), table[:]).then_inc(s_out, 16)
            sp.dma_start(k.fillrows.rearrange("(p t) w -> p t w", p=P), fill[:]).then_inc(s_out, 16)
            sp.dma_start(k.acc[EP:EP + 1, :], neutral[:]).then_inc(s_out, 16)
            sp.dma_start(k.sum[EP:EP + 1, :], neutral[:, 0:F]).then_inc(s_out, 16)
            sp.wait_ge(s_out, 16 * 5)

        @block.tensor
        def _(pe):
            pe.wait_ge(s_in, NIN)
            nc.tensor.transpose(ps[0:G, 0:P], emb[:], k.ident[:]).then_inc(s_t, 1)
            pe.wait_ge(s_tc, 1)
            nc.tensor.matmul(ps[:, P:P + G], embT[:], adapt[:], start=True, stop=True).then_inc(s_m, 1)

        @block.gpsimd
        def _(pool):
            pool.wait_ge(s_in, NIN)
            pool.wait_ge(s_out, 16)
            for t in range(NT):
                gather(nc, zrow[:, t, :], k.by_type, z[:, t, :]).then_inc(s_z, 16)
            pool.wait_ge(s_tab, 1)
            for t in range(NT):
                scatter(nc, k.fill_s, k.start[1][:, t:t + 1], fill[:, t, :], EP - 1).then_inc(s_fill, 16)
            pool.wait_ge(s_fill, 16 * NT)

        @block.scalar
        def _(act):
            act.wait_ge(s_low, 1)
            nc.scalar.activation(k.logm[:], low[:], ACT.Ln).then_inc(s_log, 1)

        @block.vector
        def _(dve):
            v = nc.vector
            ch = Chain(dve, s_step)
            for m in (k.x, z, mult, emb, neutral):
                v.memset(m[:], 0)
            ch.done(v.memset(fill[:], 0.0))
            ch.done(v.memset(neutral[:, F + 1:F + 2], -FAR))
            dve.sem_inc(s_zero, 1)
            dve.wait_ge(s_t, 1)
            ch.done(v.tensor_copy(embT[:], ps[0:G, 0:P]))
            dve.sem_inc(s_tc, 1)
            dve.wait_ge(s_m, 1)
            ch.step(v.tensor_copy(both[:, 0:G], emb[:]))
            ch.done(v.tensor_copy(both[:, G:], ps[:, P:P + G]))
            dve.sem_inc(s_both, 1)
            dve.wait_ge(s_in, NIN)
            ch.done(v.tensor_scalar(low[:], mult[:, :, 0], 1.0, None, ALU.max))
            dve.sem_inc(s_low, 1)
            ch.step(v.tensor_copy(table[:, :, 0:F], k.x[:]))
            ch.step(v.tensor_copy(table[:, :, F + G], mult[:, :, 0]))
            dve.wait_ge(s_z, 16 * NT)
            ch.step(v.tensor_copy(table[:, :, F:F + G], zrow[:, :, G:]))
            ch.done(v.tensor_copy(fill[:, :, 0:G], zrow[:, :, 0:G]))
            dve.sem_inc(s_tab, 1)
            dve.wait_ge(s_log, 1)


def first_pass(nc, k, i):
    W = F + G + 1
    with ExitStack() as ctx:
        ph = Phase(nc, ctx, "first")
        staged = ph.sb("staged", [P, 2, C], I32)
        rows = [ph.sb(f"rows{b}", [P, C, W]) for b in range(2)]
        fin = [ph.sb(f"fin{b}", [P, C, FILL_S]) for b in range(2)]
        edge = [ph.sb(f"edge{b}", [P, C, REC_S]) for b in range(2)]
        fo = [ph.sb(f"fo{b}", [P, C, G]) for b in range(2)]
        sums = [ph.sb(f"sums{b}", [P, C, ACC]) for b in range(2)]
        init = ph.sb("init", [P, FILL_S])
        val = ph.sb("val", [P, C, F + 1])
        dot, gate = ph.sb("dot", [P, C, G]), ph.sb("gate", [P, C, F])
        near, phase_, turn, cw, wgt = (ph.sb(n, [P, C]) for n in ("near", "phase", "turn", "cw", "wgt"))
        w1, w2, b1 = ph.sb("w1", [RBF, F]), ph.sb("w2", [F + 1, F]), ph.sb("b1", [F, 1])
        half = ph.sb("half", [P, 1])
        eT = [ph.sb(f"eT{b}", [RBF, COLS * P]) for b in range(2)]
        act1 = [ph.sb(f"act1{b}", [64, COLS * P]) for b in range(2)]
        ps_t, ps_1, ps_2 = ([ph.ps(f"{n}{b}", [P, 512]) for b in range(2)] for n in ("ps_t", "ps_1", "ps_2"))
        s_w, s_ones, s_init, s_staged, s_step, s_turn, s_pe_turn = (ph.sem(n) for n in ("s_w", "s_ones", "s_init", "s_staged", "s_step", "s_turn", "s_pe_turn"))
        s_rows, s_load, s_used, s_sums, s_stored = ([ph.sem(f"{n}{b}") for b in range(2)] for n in ("s_rows", "s_load", "s_used", "s_sums", "s_stored"))
        s_t, s_tc, s_1, s_1a, s_2, s_2c, s_arg, s_cos = (ph.sem(n) for n in ("s_t", "s_tc", "s_1", "s_1a", "s_2", "s_2c", "s_arg", "s_cos"))
        cols = lambda g: min(COLS, C - g * COLS)
        block = ph.block()

        @block.gpsimd
        def _(pool):
            gather(nc, init[:], k.fillrows, k.first[1][:, 0:1]).then_inc(s_init, 16)
            pool.wait_ge(s_init, 16)
            pool_gathers(nc, pool, k.other[1], staged, rows, W, k.table0, s_staged, s_rows,
                         [[(s_used[b], 1)] for b in range(2)], s_turn)

        @block.sync
        def _(sp):
            sp.wait_ge(s_ones, 1)
            sp.dma_start(w1[:], i["L0_gnn_F1W"]).then_inc(s_w, 16)
            sp.dma_start(w2[0:F, :], i["L0_gnn_F2W"]).then_inc(s_w, 16)
            sp.dma_start(w2[F:F + 1, :], i["L0_gnn_F2b"].rearrange("(a n) -> a n", a=1)).then_inc(s_w, 16)
            sp.dma_start(b1[:], column(i["L0_gnn_F1b"])).then_inc(s_w, 16)
            def load(t, b):
                at = bass.ds((t * 2 + b) * C, C)
                sp.wait_ge(s_used[b], t + 1)
                sp.dma_start(edge[b][:], k.edges_s.rearrange("(p j) w -> p j w", p=P)[:, at, :]).then_inc(s_load[b], 16)
                sp.dma_start(fin[b][:], k.fill_s.rearrange("(p j) w -> p j w", p=P)[:, at, :]).then_inc(s_load[b], 16)

            stream(sp, load, store_sums(sp, k, k.acc, sums, s_sums, s_stored))
            for b in range(2):
                sp.wait_ge(s_stored[b], 16 * (PAIRS + 1))

        @block.tensor
        def _(pe):
            pe.wait_ge(s_w, 64)
            with pe.Fori(0, PAIRS) as t:
                for b in range(2):
                    pe.wait_ge(s_load[b], (t + 1) * 32)
                    for s in range(STEPS + 2):
                        n = (t * 2 + b) * STEPS + s
                        q = (b * STEPS + s) % 2
                        if s < STEPS:
                            pe.wait_ge(s_tc, n + 1)
                            pe.sem_inc(s_pe_turn, 1)
                            for c in range(cols(s)):
                                ins = nc.tensor.transpose(ps_t[q][0:RBF, c * P:(c + 1) * P], edge[b][:, s * COLS + c, 0:RBF], k.ident[:])
                            ins.then_inc(s_t, 1)
                        if 1 <= s < STEPS + 1:
                            g = s - 1
                            pe.wait_ge(s_tc, n + 2)
                            pe.wait_ge(s_1a, n)
                            pe.sem_inc(s_pe_turn, 1)
                            w = cols(g) * P
                            nc.tensor.matmul(ps_1[1 - q][0:F, 0:w], w1[:], eT[1 - q][:, 0:w], start=True, stop=True).then_inc(s_1, 1)
                        if s >= 2:
                            g = s - 2
                            pe.wait_ge(s_1a, n + 1)
                            pe.wait_ge(s_2c, n - 1)
                            for c in range(cols(g)):
                                ins = nc.tensor.matmul(ps_2[q][:, c * F:(c + 1) * F], act1[q][0:F + 1, c * P:(c + 1) * P], w2[:], start=True, stop=True)
                            ins.then_inc(s_2, 1)

        @block.scalar
        def _(act):
            act.sem_inc(s_tc, 2)
            act.sem_inc(s_1a, 2)
            act.wait_ge(s_w, 64)
            with act.Fori(0, PAIRS) as t:
                for b in range(2):
                    ch0 = (t * 2 + b) * STEPS
                    act.wait_ge(s_arg, t * 2 + b + 1)
                    nc.scalar.activation(cw[:], phase_[:], ACT.Sin, bias=half[:], scale=-np.pi / 6.0).then_inc(s_cos, 1)
                    for g in range(STEPS + 1):
                        if g < STEPS:
                            w = cols(g) * P
                            act.wait_ge(s_t, ch0 + g + 1)
                            q = (b * STEPS + g) % 2
                            nc.scalar.activation(eT[q][:, 0:w], ps_t[q][0:RBF, 0:w], ACT.Copy).then_inc(s_tc, 1)
                        if g >= 1:
                            w = cols(g - 1) * P
                            act.wait_ge(s_1, ch0 + g)
                            q = (b * STEPS + g - 1) % 2
                            nc.scalar.activation(act1[q][0:F, 0:w], ps_1[q][0:F, 0:w], ACT.Silu, bias=b1[:]).then_inc(s_1a, 1)

        @block.vector
        def _(dve):
            v = nc.vector
            ch = Chain(dve, s_step)
            v.memset(half[:], float(np.pi / 2))
            for m in (*act1,):
                v.memset(m[:], 1.0)
            v.memset(sums[0][:], 0.0)
            ch.done(v.memset(sums[1][:], 0.0))
            dve.sem_inc(s_ones, 1)
            dve.sem_inc(s_2c, 2)
            for b in range(2):
                dve.sem_inc(s_used[b], 1)
            dve.wait_ge(s_init, 16)
            ch.done(v.tensor_copy(fo[1][:, C - 1, :], init[:, 0:G]))
            PER, n0 = 24, ch.n
            with dve.Fori(0, PAIRS) as t:
                ch.n, ch.base = n0, t * PER
                for b in range(2):
                    at = bass.ds((t * 2 + b) * C, C)
                    dve.wait_ge(s_load[b], (t + 1) * 32)
                    d = edge[b][:, :, RBF]
                    ch.step(v.tensor_scalar(near[:], d, 6.0, 0.5, ALU.is_lt, ALU.mult))
                    ch.done(v.tensor_scalar(turn[:], d, 1.0 / 12.0, ROUND, ALU.mult, ALU.add))
                    ch.done(v.tensor_scalar(turn[:], turn[:], -ROUND, -12.0, ALU.add, ALU.mult))
                    ch.done(v.tensor_tensor(turn[:], turn[:], d, ALU.add))
                    ch.done(v.scalar_tensor_tensor(out=phase_[:], in0=turn[:], scalar=-1.0, in1=turn[:], op0=ALU.mult, op1=ALU.max))
                    dve.sem_inc(s_arg, 1)
                    ch.done(scan_columns(nc, fo[b], k.keep[1][:, at], fin[b][:], fo[1 - b][:, C - 1, :], G))
                    dve.wait_ge(s_rows[b], (t + 1) * (16 * C))
                    ch.done(v.tensor_tensor(dot[:], fo[b][:], rows[b][:, :, F:F + G], ALU.mult))
                    ch.done(v.tensor_reduce(wgt[:], dot[:], AX, ALU.add))
                    for g in range(STEPS):
                        dve.wait_ge(s_2, (t * 2 + b) * STEPS + g + 1)
                        c0, w = g * COLS, cols(g)
                        v.tensor_tensor(gate[:, c0:c0 + w, :], ps_2[(b * STEPS + g) % 2][:, 0:w * F].rearrange("p (c f) -> p c f", f=F),
                                        bc(wgt[:, c0:c0 + w], F), ALU.add).then_inc(s_2c, 1)
                    dve.wait_ge(s_2c, (t * 2 + b + 1) * STEPS + 2)
                    dve.wait_ge(s_cos, t * 2 + b + 1)
                    ch.done(v.tensor_scalar(cw[:], cw[:], 1.0, None, ALU.add))
                    ch.done(v.tensor_tensor(cw[:], cw[:], near[:], ALU.mult))
                    ch.step(v.tensor_tensor(cw[:], cw[:], rows[b][:, :, W - 1], ALU.mult))
                    ch.done(v.tensor_tensor(gate[:], gate[:], rows[b][:, :, 0:F], ALU.mult))
                    v.tensor_copy(val[:, :, F], rows[b][:, :, W - 1])
                    v.tensor_tensor(val[:, :, 0:F], gate[:], bc(cw[:], F), ALU.mult).then_inc(s_used[b], 1)
                    dve.wait_ge(s_used[b], t + 2)
                    dve.wait_ge(s_stored[b], (t + 1) * 16)
                    scan_columns(nc, sums[b], k.keepr[1][:, at], val[:], sums[1 - b][:, C - 1, :], F + 1).then_inc(s_sums[b], 1)
                    dve.wait_ge(s_sums[b], t + 1)
            assert ch.n - n0 == PER, ch.n - n0
            dve.wait_ge(s_sums[1], PAIRS)
            v.tensor_copy(k.tail[:], sums[1][:, C - 1, :]).then_inc(s_step, 1)


def after_first(nc, k, i):
    with ExitStack() as ctx:
        ph = Phase(nc, ctx, "afterfirst")
        norm = Norm(ph)
        gain, bias = ph.sb("gain", [P, F]), ph.sb("bias", [P, F])
        tot, t1 = ph.sb("tot", [P, NT]), ph.sb("t1", [P, NT, F])
        s_step, s_w = ph.sem("s_step"), ph.sem("s_w")
        block = ph.block()

        @block.sync
        def _(sp):
            sp.dma_start(gain[:], i["L0_gnn_gn"].partition_broadcast(P)).then_inc(s_w, 16)
            sp.dma_start(bias[:], i["L0_gnn_bn"].partition_broadcast(P)).then_inc(s_w, 16)

        @block.scalar
        def _(act):
            norm.act(act)

        @block.vector
        def _(dve):
            v = nc.vector
            ch = Chain(dve, s_step)
            ch.done(v.tensor_scalar(tot[:], k.agg[:, :, F], 1e-8, None, ALU.max))
            ch.done(v.reciprocal(tot[:], tot[:]))
            ch.done(v.tensor_tensor(t1[:], k.agg[:, :, 0:F], bc(tot[:], F), ALU.mult))
            ch.done(v.tensor_tensor(t1[:], t1[:], k.x[:], ALU.add))
            dve.wait_ge(s_w, 32)
            norm.dve(dve, ch, t1[:], k.h[:], gain[:], bias[:])


def layer_tables(nc, k, i, layer):
    with ExitStack() as ctx:
        ph = Phase(nc, ctx, "tables")
        proj_, norm = Projector(ph, k.ident), Norm(ph)
        wqk, wu = ph.sb("wqk", [F, 2 * F]), ph.sb("wu", [F, F + 1])
        mean, gk = ph.sb("mean", [F, 1]), ph.sb("gk", [F, 1])
        gq, bq = ph.sb("gq", [P, F]), ph.sb("bq", [P, F])
        proj, q, uc = ph.sb("proj", [P, NT, 2 * F]), ph.sb("q", [P, NT, F]), ph.sb("uc", [P, NT, F + 1])
        table, fill = ph.sb("table", [P, NT, ACC]), ph.sb("fill", [P, NT, FILL_S])
        s_w, s_step, s_wt, s_wtc, s_ready, s_tab, s_out, s_fill, s_q, s_put = (
            ph.sem(n) for n in ("s_w", "s_step", "s_wt", "s_wtc", "s_ready", "s_tab", "s_out", "s_fill", "s_q", "s_put"))
        of = lambda name: i[f"L0_gnn_{name}"][bass.ds(layer, 1)]
        row = lambda name: of(name).to_broadcast([P, F])
        with nc.Block() as block:
            @block.sync
            def _(sp):
                sp.dma_start(wqk[:, 0:F], of("Wq").rearrange("l a b -> (l a) b")).then_inc(s_w, 16)
                sp.dma_start(wqk[:, F:], of("Wk").rearrange("l a b -> (l a) b")).then_inc(s_w, 16)
                sp.dma_start(gk[:], of("gk").rearrange("l (f a) -> (l f) a", a=1)).then_inc(s_w, 16)
                sp.dma_start(wu[:, F:F + 1], of("bk").rearrange("l (f a) -> (l f) a", a=1)).then_inc(s_w, 16)
                sp.dma_start(gq[:], row("gq")).then_inc(s_w, 16)
                sp.dma_start(bq[:], row("bq")).then_inc(s_w, 16)
                sp.wait_ge(s_tab, 1)
                sp.dma_start(k.table1.rearrange("(p t) w -> p t w", p=P), table[:]).then_inc(s_out, 16)
                sp.wait_ge(s_fill, 1)
                sp.dma_start(k.fillrows.rearrange("(p t) w -> p t w", p=P), fill[:]).then_inc(s_out, 16)
                sp.wait_ge(s_out, 32)

            @block.tensor
            def _(pe):
                pe.wait_ge(s_ready, 1)
                nc.tensor.transpose(proj_.psp[1][0:F, 0, 0:F], wqk[:, F:], k.ident[0:F, 0:F]).then_inc(s_wt, 1)
                pe.wait_ge(s_wtc, 1)
                proj_.pe(pe, lambda t: k.h[:, t, :], F, wqk[:], 2 * F)
                pe.wait_ge(s_q, 1)
                proj_.pe(pe, lambda t: q[:, t, :], F, wu[:], F + 1)

            @block.scalar
            def _(act):
                proj_.act(act, F)
                norm.act(act)
                norm.act(act)
                proj_.act(act, F)

            @block.gpsimd
            def _(pool):
                pool.wait_ge(s_fill, 1)
                for t in range(NT):
                    scatter(nc, k.fill_s, k.start[1][:, t:t + 1], fill[:, t, :], EP - 1).then_inc(s_put, 16)
                pool.wait_ge(s_put, 16 * NT)

            @block.vector
            def _(dve):
                v = nc.vector
                ch = Chain(dve, s_step)
                dve.wait_ge(s_w, 96)
                ch.done(v.tensor_reduce(mean[:], wqk[:, F:], AX, ALU.add))
                ch.done(v.tensor_scalar(mean[:], mean[:], 1.0 / F, None, ALU.mult))
                ch.done(v.tensor_scalar(wqk[:, F:], wqk[:, F:], mean[:], None, ALU.subtract))
                dve.sem_inc(s_ready, 1)
                dve.wait_ge(s_wt, 1)
                ch.done(v.tensor_scalar(wu[:, 0:F], proj_.psp[1][0:F, 0, 0:F], gk[:], None, ALU.mult))
                dve.sem_inc(s_wtc, 1)
                proj_.dve(dve, proj, 2 * F)
                norm.variance(ch, proj[:, :, F:])
                norm.rsqrt(dve, ch)
                ch.step(v.tensor_copy(table[:, :, 0:F], k.h[:]))
                ch.step(v.tensor_copy(table[:, :, F], norm.stat[:]))
                ch.done(v.tensor_copy(table[:, :, F + 1], k.logm[:]))
                dve.sem_inc(s_tab, 1)
                norm.dve(dve, ch, proj[:, :, 0:F], q[:], gq[:], bq[:])
                dve.sem_inc(s_q, 1)
                proj_.dve(dve, uc, F + 1)
                ch.step(v.tensor_copy(fill[:, :, 0:F], uc[:, :, 0:F]))
                ch.step(v.tensor_scalar(fill[:, :, F:F + RBF], q[:, :, 0:RBF], 0.1, None, ALU.mult))
                ch.done(v.tensor_copy(fill[:, :, FILL_S - 1], uc[:, :, F]))
                dve.sem_inc(s_fill, 1)

        clear(nc, ph.sems)


def attend(nc, k):
    with ExitStack() as ctx:
        ph = Phase(nc, ctx, "attend")
        staged = ph.sb("staged", [P, 2, C], I32)
        rows = [ph.sb(f"rows{b}", [P, C, ACC]) for b in range(2)]
        fin = [ph.sb(f"fin{b}", [P, C, FILL_S]) for b in range(2)]
        edge = [ph.sb(f"edge{b}", [P, C, REC_S]) for b in range(2)]
        fo = [ph.sb(f"fo{b}", [P, C, FILL_S]) for b in range(2)]
        sums = [ph.sb(f"sums{b}", [P, C, ACC]) for b in range(2)]
        init = ph.sb("init", [P, FILL_S])
        val = ph.sb("val", [P, C, F + 1])
        dot_h, dot_e = ph.sb("dot_h", [P, C, F]), ph.sb("dot_e", [P, C, RBF])
        sh, se = ph.sb("sh", [P, C]), ph.sb("se", [P, C])
        top = [ph.sb(f"top{b}", [P, 1 + C]) for b in range(2)]
        arg, ex = ph.sb("arg", [P, 2, C]), ph.sb("ex", [P, 2, C])
        s_init, s_staged, s_step, s_arg, s_exp, s_turn = (ph.sem(n) for n in ("s_init", "s_staged", "s_step", "s_arg", "s_exp", "s_turn"))
        s_rows, s_load, s_used, s_sums, s_stored = ([ph.sem(f"{n}{b}") for b in range(2)] for n in ("s_rows", "s_load", "s_used", "s_sums", "s_stored"))
        with nc.Block() as block:
            @block.gpsimd
            def _(pool):
                gather(nc, init[:], k.fillrows, k.first[1][:, 0:1]).then_inc(s_init, 16)
                pool.wait_ge(s_init, 16)
                pool_gathers(nc, pool, k.other[1], staged, rows, ACC, k.table1, s_staged, s_rows,
                             [[(s_used[b], 1)] for b in range(2)], s_turn)

            @block.sync
            def _(sp):
                def load(t, b):
                    at = bass.ds((t * 2 + b) * C, C)
                    sp.wait_ge(s_used[b], t + 1)
                    sp.dma_start(edge[b][:], k.edges_s.rearrange("(p j) w -> p j w", p=P)[:, at, :]).then_inc(s_load[b], 16)
                    sp.dma_start(fin[b][:], k.fill_s.rearrange("(p j) w -> p j w", p=P)[:, at, :]).then_inc(s_load[b], 16)

                stream(sp, load, store_sums(sp, k, k.acc, sums, s_sums, s_stored))
                for b in range(2):
                    sp.wait_ge(s_stored[b], 16 * (PAIRS + 1))

            @block.scalar
            def _(act):
                with act.Fori(0, PAIRS) as t:
                    for b in range(2):
                        act.wait_ge(s_arg, t * 2 + b + 1)
                        nc.scalar.activation(ex[:], arg[:], ACT.Exp).then_inc(s_exp, 1)

            @block.vector
            def _(dve):
                v = nc.vector
                ch = Chain(dve, s_step)
                v.memset(top[1][:], 0.0)
                for b in range(2):
                    dve.sem_inc(s_used[b], 1)
                ch.done(v.memset(sums[1][:, C - 1, :], 0.0))
                dve.wait_ge(s_init, 16)
                ch.done(v.tensor_copy(fo[1][:, C - 1, :], init[:]))
                PER, n0 = 28, ch.n
                with dve.Fori(0, PAIRS) as t:
                    ch.n, ch.base = n0, t * PER
                    for b in range(2):
                        at = bass.ds((t * 2 + b) * C, C)
                        dve.wait_ge(s_load[b], (t + 1) * 32)
                        ch.done(scan_columns(nc, fo[b], k.keep[1][:, at], fin[b][:], fo[1 - b][:, C - 1, :], FILL_S))
                        ch.done(v.tensor_tensor(dot_e[:], fo[b][:, :, F:F + RBF], edge[b][:, :, 0:RBF], ALU.mult))
                        ch.done(v.tensor_reduce(se[:], dot_e[:], AX, ALU.add))
                        dve.wait_ge(s_rows[b], (t + 1) * (16 * C))
                        ch.done(v.tensor_tensor(dot_h[:], fo[b][:, :, 0:F], rows[b][:, :, 0:F], ALU.mult))
                        ch.done(v.tensor_reduce(sh[:], dot_h[:], AX, ALU.add))
                        ch.done(v.tensor_tensor(sh[:], sh[:], rows[b][:, :, F], ALU.mult))
                        ch.done(v.tensor_tensor(sh[:], sh[:], fo[b][:, :, FILL_S - 1], ALU.add))
                        ch.done(v.tensor_tensor(sh[:], sh[:], se[:], ALU.add))
                        ch.done(v.tensor_tensor(sh[:], sh[:], rows[b][:, :, F + 1], ALU.add))
                        ch.step(v.tensor_copy(top[b][:, 0:1], top[1 - b][:, C:C + 1]))
                        ch.done(v.tensor_tensor_scan(top[b][:, 1:], k.pen[:, at], sh[:], top[1 - b][:, C:C + 1], ALU.add, ALU.max))
                        ch.done(v.tensor_tensor(arg[:, 0], top[b][:, 0:C], k.pen[:, at], ALU.add))
                        ch.step(v.tensor_tensor(arg[:, 0], arg[:, 0], top[b][:, 1:], ALU.subtract))
                        ch.done(v.tensor_tensor(arg[:, 1], sh[:], top[b][:, 1:], ALU.subtract))
                        v.tensor_scalar(arg[:, 1], arg[:, 1], 20.0, None, ALU.min).then_inc(s_arg, 1)
                        dve.wait_ge(s_exp, t * 2 + b + 1)
                        v.tensor_copy(val[:, :, F], ex[:, 1])
                        v.tensor_tensor(val[:, :, 0:F], rows[b][:, :, 0:F], bc(ex[:, 1], F), ALU.mult).then_inc(s_used[b], 1)
                        dve.wait_ge(s_used[b], t + 2)
                        dve.wait_ge(s_stored[b], (t + 1) * 16)
                        v.tensor_copy(sums[b][:, :, F + 1], top[b][:, 1:])
                        scan_columns(nc, sums[b], ex[:, 0], val[:], sums[1 - b][:, C - 1, :], F + 1).then_inc(s_sums[b], 1)
                        dve.wait_ge(s_sums[b], t + 1)
                assert ch.n - n0 == PER, ch.n - n0
                dve.wait_ge(s_sums[1], PAIRS)
                v.tensor_copy(k.tail[:], sums[1][:, C - 1, :]).then_inc(s_arg, 1)

        clear(nc, ph.sems)


def layer_update(nc, k, i, layer):
    with ExitStack() as ctx:
        ph = Phase(nc, ctx, "update")
        proj_, norm = Projector(ph, k.ident), Norm(ph)
        wm, wt, wb = ph.sb("wm", [F, F]), ph.sb("wt", [F, F]), ph.sb("wb", [F, F])
        left, eye, wz = ph.sb("left", [F, 2 * F]), ph.sb("eye", [F, 2 * F]), ph.sb("wz", [2 * F, F])
        go, bo = ph.sb("go", [P, F]), ph.sb("bo", [P, F])
        ha, z, lz = ph.sb("ha", [P, NT, 2 * F]), ph.sb("z", [P, NT, F]), ph.sb("lz", [P, NT, F])
        den = ph.sb("den", [P, NT])
        s_w, s_step, s_wt, s_wtc, s_prod, s_ready = (ph.sem(n) for n in ("s_w", "s_step", "s_wt", "s_wtc", "s_prod", "s_ready"))
        of = lambda name: i[f"L0_gnn_{name}"][bass.ds(layer, 1)]
        with nc.Block() as block:
            @block.sync
            def _(sp):
                sp.dma_start(wm[:], of("Wm").rearrange("l a b -> (l a) b")).then_inc(s_w, 16)
                sp.dma_start(wt[:], of("Wu")[:, 0:F].rearrange("l a b -> (l a) b")).then_inc(s_w, 16)
                sp.dma_start(wb[:], of("Wu")[:, F:2 * F].rearrange("l a b -> (l a) b")).then_inc(s_w, 16)
                sp.dma_start(go[:], of("go").to_broadcast([P, F])).then_inc(s_w, 16)
                sp.dma_start(bo[:], of("bo").to_broadcast([P, F])).then_inc(s_w, 16)

            @block.tensor
            def _(pe):
                pe.wait_ge(s_w, 80)
                nc.tensor.transpose(proj_.psp[1][0:F, 0, 0:F], wm[:], k.ident[0:F, 0:F]).then_inc(s_wt, 1)
                pe.wait_ge(s_wtc, 1)
                nc.tensor.matmul(proj_.psp[1][0:2 * F, 0, 0:F], eye[:], wt[:], start=True, stop=False)
                nc.tensor.matmul(proj_.psp[1][0:2 * F, 0, 0:F], left[:], wb[:], start=False, stop=True).then_inc(s_prod, 1)
                pe.wait_ge(s_ready, 1)
                proj_.pe(pe, lambda t: ha[:, t, :], 2 * F, wz[:], F)

            @block.scalar
            def _(act):
                proj_.act(act, 2 * F)
                norm.act(act)

            @block.vector
            def _(dve):
                v = nc.vector
                ch = Chain(dve, s_step)
                v.memset(left[:], 0.0)
                ch.done(v.memset(eye[:], 0.0))
                ch.done(v.tensor_copy(eye[:, 0:F], k.ident[0:F, 0:F]))
                dve.wait_ge(s_wt, 1)
                ch.done(v.tensor_copy(left[:, F:], proj_.psp[1][0:F, 0, 0:F]))
                dve.sem_inc(s_wtc, 1)
                ch.done(v.tensor_scalar(den[:], k.agg[:, :, F], 1e-10, None, ALU.add))
                ch.done(v.reciprocal(den[:], den[:]))
                ch.step(v.tensor_tensor(ha[:, :, F:], k.agg[:, :, 0:F], bc(den[:], F), ALU.mult))
                ch.done(v.tensor_copy(ha[:, :, 0:F], k.h[:]))
                dve.wait_ge(s_prod, 1)
                ch.done(v.tensor_copy(wz[:], proj_.psp[1][0:2 * F, 0, 0:F]))
                dve.sem_inc(s_ready, 1)
                proj_.dve(dve, z, F)
                ch.done(v.tensor_scalar(lz[:], z[:], 0.01, None, ALU.mult))
                ch.done(v.tensor_tensor(z[:], z[:], lz[:], ALU.max))
                ch.done(v.tensor_tensor(z[:], z[:], k.h[:], ALU.add))
                dve.wait_ge(s_w, 80)
                norm.dve(dve, ch, z[:], k.h[:], go[:], bo[:])

        clear(nc, ph.sems)


def next_tables(nc, k, stage, out):
    with ExitStack() as ctx:
        ph = Phase(nc, ctx, f"next{stage}")
        norm = Norm(ph)
        t1, t2 = ph.sb("t1", [P, NT, F]), ph.sb("t2", [P, NT, F])
        cnt = ph.sb("cnt", [P, NT])
        s_step, s_tab, s_out, s_w = (ph.sem(n) for n in ("s_step", "s_tab", "s_out", "s_w"))
        y = k.y
        block = ph.block()

        @block.sync
        def _(sp):
            sp.wait_ge(s_tab, 1)
            if stage == 3:
                full, rest = N // NT, N % NT
                sp.dma_start(out[0:full * NT].rearrange("(p t) f -> p t f", t=NT), k.x[0:full]).then_inc(s_out, 16)
                sp.dma_start(out[full * NT:N].rearrange("(p t) f -> p t f", p=1), k.x[full:full + 1, 0:rest]).then_inc(s_out, 16)
                sp.wait_ge(s_out, 32)
            else:
                sp.dma_start(k.table2.rearrange("(p t) f -> p t f", p=P), y[:]).then_inc(s_out, 16)
                sp.wait_ge(s_out, 16)

        @block.gpsimd
        def _(pool):
            if stage == 0:
                pool.wait_ge(s_tab, 1)
                for t in range(NT):
                    scatter(nc, k.fill_d, k.start[0][:, t:t + 1], y[:, t, :], EP - 1).then_inc(s_w, 16)
                pool.wait_ge(s_w, 16 * NT)

        @block.scalar
        def _(act):
            norm.act(act)
            if stage in (1, 2):
                norm.act(act)

        @block.vector
        def _(dve):
            v = nc.vector
            ch = Chain(dve, s_step)
            if stage == 0:
                ch.done(v.tensor_tensor(t1[:], k.x[:], k.h[:], ALU.add))
            elif stage == 1:
                ch.done(v.tensor_tensor(t1[:], bc(k.count[0][:], F), rows_of(k.b3[:], NT), ALU.mult))
                ch.done(v.tensor_tensor(t1[:], t1[:], k.agg2[:], ALU.add))
                ch.done(v.tensor_scalar(cnt[:], k.count[0][:], 1.0, None, ALU.max))
                ch.done(v.reciprocal(cnt[:], cnt[:]))
                ch.done(v.tensor_tensor(t1[:], t1[:], bc(cnt[:], F), ALU.mult))
                ch.done(v.tensor_tensor(t1[:], t1[:], k.x[:], ALU.add))
                ch.done(v.tensor_tensor(t1[:], t1[:], k.x[:], ALU.add))
            else:
                src = k.agg2
                if stage == 3:
                    ch.done(v.tensor_tensor(t2[:], k.agg2[:], y[:], ALU.add))
                    src = t2
                ch.done(v.tensor_tensor(t1[:], src[:], bc(k.dinv[:], F), ALU.mult))
                ch.done(v.tensor_tensor(t1[:], t1[:], k.x[:], ALU.add))
            norm.dve(dve, ch, t1[:], k.x[:])
            if stage == 0:
                ch.done(v.tensor_copy(y[:], k.x[:]))
            elif stage in (1, 2):
                if stage == 1:
                    ch.done(v.tensor_scalar(norm.stat[:], k.count[1][:], 1.0, None, ALU.max))
                else:
                    ch.done(v.tensor_scalar(norm.stat[:], k.count[1][:], 1.0, None, ALU.add))
                norm.rsqrt(dve, ch)
                ch.done(v.tensor_copy(k.dinv[:], norm.stat[:]))
                ch.done(v.tensor_tensor(y[:], k.x[:], bc(k.dinv[:], F), ALU.mult))
            dve.sem_inc(s_tab, 1)


def sum_pass(nc, k, weighted):
    with ExitStack() as ctx:
        ph = Phase(nc, ctx, f"sum{int(weighted)}")
        staged = ph.sb("staged", [P, 2, C], I32)
        rows = [ph.sb(f"rows{b}", [P, C, F]) for b in range(2)]
        sums = [ph.sb(f"sums{b}", [P, C, F]) for b in range(2)]
        val = ph.sb("val", [P, C, F])
        s_go, s_staged, s_step, s_turn = (ph.sem(n) for n in ("s_go", "s_staged", "s_step", "s_turn"))
        s_rows, s_used, s_sums, s_stored = ([ph.sem(f"{n}{b}") for b in range(2)] for n in ("s_rows", "s_used", "s_sums", "s_stored"))
        block = ph.block()

        @block.gpsimd
        def _(pool):
            pool.wait_ge(s_go, 1)
            pool_gathers(nc, pool, k.other[0], staged, rows, F, k.table2, s_staged, s_rows,
                         [[(s_used[b], 1)] for b in range(2)], s_turn)

        @block.sync
        def _(sp):
            sp.sem_inc(s_go, 1)
            store = store_sums(sp, k, k.sum, sums, s_sums, s_stored)
            with sp.Fori(0, PAIRS) as t:
                for b in range(2):
                    store(t, b)
            for b in range(2):
                sp.wait_ge(s_stored[b], 16 * (PAIRS + 1))

        @block.vector
        def _(dve):
            v = nc.vector
            ch = Chain(dve, s_step)
            for b in range(2):
                dve.sem_inc(s_used[b], 1)
            ch.done(v.memset(sums[1][:, C - 1, :], 0.0))
            PER, n0 = 2 * int(weighted), ch.n
            with dve.Fori(0, PAIRS) as t:
                ch.n, ch.base = n0, t * PER
                for b in range(2):
                    at = bass.ds((t * 2 + b) * C, C)
                    dve.wait_ge(s_rows[b], (t + 1) * (16 * C))
                    src = rows[b]
                    if weighted:
                        ch.done(v.tensor_tensor(val[:], rows[b][:], bc(k.weight[:, at], F), ALU.mult))
                        src = val
                    dve.wait_ge(s_stored[b], (t + 1) * 16)
                    scan_columns(nc, sums[b], k.keepr[0][:, at], src[:], sums[1 - b][:, C - 1, :], F).then_inc(s_sums[b], 1)
                    dve.wait_ge(s_sums[b], t + 1)
                    dve.sem_inc(s_used[b], 1)
            dve.wait_ge(s_sums[1], PAIRS)
            v.tensor_copy(k.tail[:, 0:F], sums[1][:, C - 1, :]).then_inc(s_go, 1)


def mlp_pass(nc, k, i):
    X = 2 * F + EF
    with ExitStack() as ctx:
        ph = Phase(nc, ctx, "mlp")
        staged = ph.sb("staged", [P, 2, C], I32)
        xin = [ph.sb(f"xin{b}", [P, C, X]) for b in range(2)]
        fin = [ph.sb(f"fin{b}", [P, C, F]) for b in range(2)]
        edge = [ph.sb(f"edge{b}", [P, C, REC_D]) for b in range(2)]
        sums = [ph.sb(f"sums{b}", [P, C, F]) for b in range(2)]
        val = [ph.sb(f"val{b}", [P, C, F]) for b in range(2)]
        init = ph.sb("init", [P, F])
        w1, w2, w3 = ph.sb("w1", [X, HID]), ph.sb("w2", [HID, HID]), ph.sb("w3", [HID, F])
        b1, b2 = ph.sb("b1", [HID, 1]), ph.sb("b2", [HID, 1])
        xT, h1, h2 = ([ph.sb(f"{n}{b}", [P, COLS * P]) for b in range(2)] for n in ("xT", "h1", "h2"))
        ps_t, ps_1, ps_2, ps_3 = ([ph.ps(f"{n}{b}", [P, 512]) for b in range(2)] for n in ("ps_t", "ps_1", "ps_2", "ps_3"))
        s_w, s_init, s_staged, s_step, s_join, s_turn = (ph.sem(n) for n in ("s_w", "s_init", "s_staged", "s_step", "s_join", "s_turn"))
        s_rows, s_load, s_used, s_sums, s_stored = ([ph.sem(f"{n}{b}") for b in range(2)] for n in ("s_rows", "s_load", "s_used", "s_sums", "s_stored"))
        s_t, s_tc, s_1, s_1a, s_2, s_2a, s_3, s_3c = (ph.sem(n) for n in ("s_t", "s_tc", "s_1", "s_1a", "s_2", "s_2a", "s_3", "s_3c"))
        cols = lambda g: min(COLS, C - g * COLS)
        block = ph.block()

        @block.gpsimd
        def _(pool):
            gather(nc, init[:], k.table2, k.first[0][:, 0:1]).then_inc(s_init, 16)
            pool.wait_ge(s_init, 16)
            pool_gathers(nc, pool, k.other[0], staged, xin, F, k.table2, s_staged, s_rows,
                         [[(s_used[b], 1)] for b in range(2)], s_turn)

        @block.sync
        def _(sp):
            for to, name in ((w1, "W1"), (w2, "W2"), (w3, "W3")):
                sp.dma_start(to[:], i[f"L1_gnn_{name}"]).then_inc(s_w, 16)
            sp.dma_start(b1[:], column(i["L1_gnn_b1"])).then_inc(s_w, 16)
            sp.dma_start(b2[:], column(i["L1_gnn_b2"])).then_inc(s_w, 16)
            sp.dma_start(k.b3[:], i["L1_gnn_b3"].partition_broadcast(P)).then_inc(s_w, 16)

            def load(t, b):
                at = bass.ds((t * 2 + b) * C, C)
                sp.wait_ge(s_used[b], t + 1)
                sp.dma_start(edge[b][:], k.edges_d.rearrange("(p j) w -> p j w", p=P)[:, at, :]).then_inc(s_load[b], 16)
                sp.dma_start(fin[b][:], k.fill_d.rearrange("(p j) w -> p j w", p=P)[:, at, :]).then_inc(s_load[b], 16)

            stream(sp, load, store_sums(sp, k, k.sum, sums, s_sums, s_stored))
            for b in range(2):
                sp.wait_ge(s_stored[b], 16 * (PAIRS + 1))

        @block.tensor
        def _(pe):
            pe.wait_ge(s_w, 96)
            with pe.Fori(0, PAIRS) as t:
                for b in range(2):
                    pe.wait_ge(s_rows[b], (t + 1) * (16 * C))
                    pe.wait_ge(s_join, t * 2 + b + 1)
                    for s in range(STEPS + 3):
                        n = (t * 2 + b) * STEPS + s
                        q = (b * STEPS + s) % 2
                        if s < STEPS:
                            pe.wait_ge(s_tc, n + 1)
                            for c in range(cols(s)):
                                ins = nc.tensor.transpose(ps_t[q][0:X, c * P:(c + 1) * P], xin[b][:, s * COLS + c, :], k.ident[:])
                            ins.then_inc(s_t, 1)
                        if 1 <= s <= STEPS:
                            w = cols(s - 1) * P
                            pe.wait_ge(s_tc, n + 2)
                            pe.wait_ge(s_1a, n)
                            nc.tensor.matmul(ps_1[1 - q][:, 0:w], w1[:], xT[1 - q][0:X, 0:w], start=True, stop=True).then_inc(s_1, 1)
                        if 2 <= s <= STEPS + 1:
                            w = cols(s - 2) * P
                            pe.wait_ge(s_1a, n + 1)
                            pe.wait_ge(s_2a, n - 1)
                            nc.tensor.matmul(ps_2[q][:, 0:w], w2[:], h1[q][:, 0:w], start=True, stop=True).then_inc(s_2, 1)
                        if s >= 3:
                            pe.wait_ge(s_2a, n)
                            pe.wait_ge(s_3c, n - 2)
                            for c in range(cols(s - 3)):
                                ins = nc.tensor.matmul(ps_3[1 - q][:, c * F:(c + 1) * F], h2[1 - q][:, c * P:(c + 1) * P], w3[:], start=True, stop=True)
                            ins.then_inc(s_3, 1)

        @block.scalar
        def _(act):
            act.sem_inc(s_1a, 2)
            act.sem_inc(s_2a, 2)
            act.sem_inc(s_tc, 2)
            act.wait_ge(s_w, 96)
            with act.Fori(0, PAIRS) as t:
                for b in range(2):
                    for s in range(STEPS + 2):
                        n = (t * 2 + b) * STEPS + s
                        q = (b * STEPS + s) % 2
                        if s < STEPS:
                            w = cols(s) * P
                            act.wait_ge(s_t, n + 1)
                            nc.scalar.activation(xT[q][0:X, 0:w], ps_t[q][0:X, 0:w], ACT.Copy).then_inc(s_tc, 1)
                        if 1 <= s <= STEPS:
                            w = cols(s - 1) * P
                            act.wait_ge(s_1, n)
                            nc.scalar.activation(h1[1 - q][:, 0:w], ps_1[1 - q][:, 0:w], ACT.Relu, bias=b1[:]).then_inc(s_1a, 1)
                        if s >= 2:
                            w = cols(s - 2) * P
                            act.wait_ge(s_2, n - 1)
                            nc.scalar.activation(h2[q][:, 0:w], ps_2[q][:, 0:w], ACT.Relu, bias=b2[:]).then_inc(s_2a, 1)

        @block.vector
        def _(dve):
            v = nc.vector
            ch = Chain(dve, s_step)
            dve.sem_inc(s_3c, 2)
            for b in range(2):
                dve.sem_inc(s_used[b], 1)
            ch.done(v.memset(sums[1][:, C - 1, :], 0.0))
            dve.wait_ge(s_init, 16)
            ch.done(v.tensor_copy(xin[1][:, C - 1, F:2 * F], init[:]))
            with dve.Fori(0, PAIRS) as t:
                for b in range(2):
                    at = bass.ds((t * 2 + b) * C, C)
                    dve.wait_ge(s_load[b], (t + 1) * 32)
                    v.tensor_copy(xin[b][:, :, 2 * F:], edge[b][:, :, 0:EF])
                    scan_columns(nc, xin[b][:, :, F:2 * F], k.keep[0][:, at], fin[b][:], xin[1 - b][:, C - 1, F:2 * F], F).then_inc(s_join, 1)
                    for g in range(STEPS):
                        c0, w = g * COLS, cols(g)
                        dve.wait_ge(s_3, (t * 2 + b) * STEPS + g + 1)
                        v.tensor_copy(val[b][:, c0:c0 + w, :], ps_3[(b * STEPS + g) % 2][:, 0:w * F].rearrange("p (c f) -> p c f", f=F)).then_inc(s_3c, 1)
                    dve.wait_ge(s_3c, (t * 2 + b + 1) * STEPS + 2)
                    dve.sem_inc(s_used[b], 1)
                    dve.wait_ge(s_stored[b], (t + 1) * 16)
                    scan_columns(nc, sums[b], k.keepr[0][:, at], val[b][:], sums[1 - b][:, C - 1, :], F).then_inc(s_sums[b], 1)
                    dve.wait_ge(s_sums[b], t + 1)
            dve.wait_ge(s_sums[1], PAIRS)
            v.tensor_copy(k.tail[:, 0:F], sums[1][:, C - 1, :]).then_inc(s_step, 1)


class Shared:
    pass


def program(nc, i, out):
    k = Shared()
    dram = lambda name, shape, dt=F32: nc.dram_tensor(name, shape, dt).ap()
    k.sorted = dram("sorted_records", [ORDERS, 1 + SORT_N], I32)
    k.raw_s, k.raw_d = dram("raw_s", [EP, REC_S]), dram("raw_d", [EP, REC_D])
    k.edges_s, k.edges_d = dram("edges_s", [EP, REC_S]), dram("edges_d", [EP, REC_D])
    k.fill_s, k.fill_d = dram("fill_s", [EP, FILL_S]), dram("fill_d", [EP, F])
    k.lastpos = [dram(f"lastpos{o}", [NP, 1]) for o in range(ORDERS)]
    k.by_type = dram("by_type", [P, 2 * G])
    k.table0, k.table1, k.table2 = dram("table0", [NP, F + G + 1]), dram("table1", [NP, ACC]), dram("table2", [NP, F])
    k.fillrows = dram("fillrows", [NP, FILL_S])
    k.spare = dram("spare", [2, 1])
    k.acc, k.sum = dram("acc_rows", [EP + 1, ACC]), dram("sum_rows", [EP + 1, F])
    with ExitStack() as ctx:
        sb = lambda n, s, d=F32: ctx.enter_context(nc.sbuf_tensor(n, s, d))
        k.ident, k.ones, k.iota = sb("ident", [P, P]), sb("ones", [P, P]), sb("iota", [P, P])
        k.below, k.above, k.rowstart = sb("below", [P, P]), sb("above", [P, P]), sb("rowstart", [P, 1])
        constants(nc, k)
        sort_edges(nc, i, k)
        k.keep = [sb(f"keep{o}", [P, J]) for o in range(ORDERS)]
        k.keepr = [sb(f"keepr{o}", [P, J]) for o in range(ORDERS)]
        k.pen, k.weight = sb("pen", [P, J]), sb("weight", [P, J])
        k.other = [sb(f"other{o}", [P, J], I32) for o in range(ORDERS)]
        k.first = [sb(f"first{o}", [P, 1], I32) for o in range(ORDERS)]
        k.firstf, k.lastf = ([sb(f"{n}{o}", [P, 1]) for o in range(ORDERS)] for n in ("firstf", "lastf"))
        k.count = [sb(f"count{o}", [P, NT]) for o in range(ORDERS)]
        k.start, k.end = ([sb(f"{n}{o}", [P, NT], I32) for o in range(ORDERS)] for n in ("start", "end"))
        k.cread, k.cwrite = ([sb(f"{n}{o}", [P, 1], I32) for o in range(ORDERS)] for n in ("cread", "cwrite"))
        k.mask = [sb(f"mask{o}", [P, P]) for o in range(ORDERS)]
        for o in range(ORDERS):
            with ExitStack() as own:
                k.keyf = own.enter_context(nc.sbuf_tensor(f"keyf{o}", [P, J], F32))
                perm = own.enter_context(nc.sbuf_tensor(f"perm{o}", [P, J], I32))
                k.perm = {o: perm}
                unpack(nc, k, o)
                records(nc, k, o)
                segments(nc, k, o)
        k.x, k.h, k.y = sb("x", [P, NT, F]), sb("h", [P, NT, F]), sb("y", [P, NT, F])
        k.logm, k.dinv, k.b3 = sb("logm", [P, NT]), sb("dinv", [P, NT]), sb("b3", [P, F])
        k.tail = sb("tail", [P, ACC])
        with ExitStack() as own:
            k.agg = own.enter_context(nc.sbuf_tensor("agg", [P, NT, ACC], F32))
            node_inputs(nc, k, i)
            first_pass(nc, k, i)
            collect(nc, k, 1, k.acc, ACC, k.tail[:], k.agg, False, "collect_first")
            after_first(nc, k, i)
            with nc.Fori(0, LAYERS) as layer:
                layer_tables(nc, k, i, layer)
                attend(nc, k)
                collect(nc, k, 1, k.acc, ACC, k.tail[:], k.agg, True, "collect_layer")
                layer_update(nc, k, i, layer)
        k.agg2 = sb("agg2", [P, NT, F])
        next_tables(nc, k, 0, out)
        mlp_pass(nc, k, i)
        collect(nc, k, 0, k.sum, F, k.tail[:, 0:F], k.agg2, False, "collect_mlp")
        next_tables(nc, k, 1, out)
        sum_pass(nc, k, True)
        collect(nc, k, 0, k.sum, F, k.tail[:, 0:F], k.agg2, False, "collect_weighted")
        next_tables(nc, k, 2, out)
        sum_pass(nc, k, False)
        collect(nc, k, 0, k.sum, F, k.tail[:, 0:F], k.agg2, False, "collect_plain")
        next_tables(nc, k, 3, out)


_INS = ["x", "src", "dst", "edge_attr_16", "edge_attr_40", "edge_weight", "node_type_119", "node_vec",
        "L0_gnn_Wq", "L0_gnn_gq", "L0_gnn_bq", "L0_gnn_Wk", "L0_gnn_gk", "L0_gnn_bk", "L0_gnn_Wm", "L0_gnn_Wu",
        "L0_gnn_go", "L0_gnn_bo", "L0_gnn_F1W", "L0_gnn_F1b", "L0_gnn_F2W", "L0_gnn_F2b", "L0_gnn_gn", "L0_gnn_bn",
        "L0_gnn_emb", "L0_gnn_adapt", "L1_gnn_W1", "L1_gnn_b1", "L1_gnn_W2", "L1_gnn_b2", "L1_gnn_W3", "L1_gnn_b3"]


def kernel(**inputs):
    import numpy as _np
    import concourse.bacc as _bacc
    from concourse import mybir as _mybir
    from concourse.bass_utils import run_bass_kernel_spmd as _run

    nc = _bacc.Bacc("TRN2", target_bir_lowering=False, num_devices=1)
    arrays, args = {}, {}
    for name in _INS:
        a = _np.ascontiguousarray(inputs[name])
        arrays[f"in_{name}_dram"] = a
        args[name] = nc.dram_tensor(f"in_{name}_dram", a.shape, _mybir.dt.from_np(a.dtype), kind="ExternalInput").ap()
    out = nc.dram_tensor("out_0_dram", (N, F), F32, kind="ExternalOutput").ap()
    program(nc, args, out)
    r = _run(nc, [arrays], core_ids=[0])
    return r.results[0]["out_0_dram"]
```

```python
from contextlib import ExitStack

import numpy as np
import concourse.bass as bass
from concourse import mybir

F32, I32, BF16 = mybir.dt.float32, mybir.dt.int32, mybir.dt.bfloat16
ALU = mybir.AluOpType
ACT = mybir.ActivationFunctionType
AX = mybir.AxisListType.X

P = 128
N = 6250
E = 200000
NT = -(-N // P)
NP = NT * P
J = 1564
EP = P * J
SORT_J = 2048
SORT_N = P * SORT_J
ORDERS = 2
IDX_BITS = 18
KEY_BIAS = 32
C = 34
CHUNKS = J // C
PAIRS = CHUNKS // 2
F = 48
RBF = 40
EF = 16
G = 32
HID = 128
LAYERS = 4
EPS = 1e-5
FAR = 3.0e38
SKIP = 1 << 20
REC_S = RBF + 2
REC_D = EF + 2
FILL_S = F + RBF + 1
ACC = F + 2
GRP = 7
ROUND = 12582912.0
COLS = 4
PAD_P = (EP - E) // 2
LP = 80
LJ = E // LP
LC = 50
LCHUNKS = LJ // LC
STEPS = -(-C // COLS)


class Chain:

    def __init__(self, eng, sem):
        self.eng, self.sem, self.n, self.base = eng, sem, 0, 0

    def step(self, ins):
        ins.then_inc(self.sem, 1)
        self.n += 1

    def wait(self):
        self.eng.wait_ge(self.sem, self.base + self.n)

    def done(self, ins):
        self.step(ins)
        self.wait()


def column(ap):
    return ap.rearrange("(n a) -> n a", a=1)


def sort_edges(nc, i, k, order, first):
    W = SORT_J
    with ExitStack() as ctx:
        ph = Phase(nc, ctx, f"sort{order}")
        sb, sem = ph.sb, ph.sem
        buf = [sb("a", [P, W]), sb("b", [P, W])]
        prow, pbit = sb("prow", [P, 1], I32), sb("pbit", [P, 9], I32)
        sgn, flip = sb("sgn", [P, 9]), sb("flip", [P, 9])
        turned = ph.ps("turned", [P, W])
        s_keys, s_pos, s_step, s_ready, s_turned, s_out, s_records = (
            sem(n) for n in ("s_keys", "s_pos", "s_step", "s_ready", "s_turned", "s_out", "s_records"))
        pad = sb("pad", [PAD_P, 2, REC_S])
        s_pad, s_padded = sem("s_pad"), sem("s_padded")
        if first:
            dst_rec, dst_key = sb("dst_rec", [P, W], I32), sb("dst_key", [P, W], I32)
            pos = sb("pos", [P, W], I32)
            zero = sb("zero", [1, 1], I32)
            zeros = sb("zeros", [P, C * FILL_S])
            edge = [sb(f"edge{b}", [LP, LC, REC_S]) for b in range(2)]
            dist, dsts, before = sb("dist", [LP, LJ]), sb("dsts", [LP, LJ], I32), sb("before", [LP, LJ], I32)
            falls = sb("falls", [LP, 1])
            total = ph.ps("total", [P, 512])
            s_zeros, s_cols, s_before, s_falls, s_total, s_rec = (sem(n) for n in ("s_zeros", "s_cols", "s_before", "s_falls", "s_total", "s_rec"))
            s_attr, s_put, s_laid = ([sem(f"{n}{b}") for b in range(2)] for n in ("s_attr", "s_put", "s_laid"))
        full, rest = E // SORT_J, E % SORT_J
        lay = lambda a: a.rearrange("(p j) -> p j", p=LP)
        block = ph.block()

        @block.gpsimd
        def _(pool):
            nc.gpsimd.iota(prow[:], [[0, 1]], base=0, channel_multiplier=1).then_inc(s_pos, 1)
            if first:
                nc.gpsimd.iota(pos[:], [[1, SORT_J]], base=0, channel_multiplier=SORT_J).then_inc(s_pos, 1)

        @block.sync
        def _(sp):
            if first:
                sp.wait_ge(s_pad, 1)
                for into, key in ((dst_key, i["dst"]), (buf[1][:].bitcast(I32), i["src"])):
                    sp.dma_start(into[0:full, :], key[0:full * SORT_J].rearrange("(p j) -> p j", j=SORT_J)).then_inc(s_keys, 16)
                    sp.dma_start(into[full:full + 1, 0:rest], key[full * SORT_J:E].rearrange("(p j) -> p j", p=1)).then_inc(s_keys, 16)
                sp.dma_start(before[0:1, 1:], i["dst"][0:LJ - 1].rearrange("(p j) -> p j", p=1)).then_inc(s_before, 16)
                sp.dma_start(before[1:, :], i["dst"][LJ - 1:E - 1].rearrange("(p j) -> p j", p=LP - 1)).then_inc(s_before, 16)
                sp.dma_start(dsts[:], lay(i["dst"])).then_inc(s_cols, 16)
                sp.dma_start(dist[:], lay(i["edge_weight"])).then_inc(s_cols, 16)
                for o in range(ORDERS):
                    sp.dma_start(k.sorted[o:o + 1, 0:1], zero[:]).then_inc(s_out, 16)
                sp.wait_ge(s_rec, 1)
                sp.dma_start(k.sorted[0, 1:1 + SORT_N].rearrange("(p j) -> p j", p=P), dst_rec[:]).then_inc(s_out, 16)
                attrs = i["edge_attr_40"].rearrange("(p j) w -> p j w", p=LP)
                with sp.Fori(0, LCHUNKS // 2) as t:
                    for b in range(2):
                        sp.wait_ge(s_laid[b], (t + 1) * 16)
                        sp.dma_start(edge[b][:, :, 0:RBF], attrs[:, bass.ds((t * 2 + b) * LC, LC), :]).then_inc(s_attr[b], 16)
            else:
                sp.dma_start(buf[0][:].bitcast(I32), k.sorted[order, 1:1 + SORT_N].rearrange("(p j) -> p j", p=P)).then_inc(s_keys, 16)
            sp.wait_ge(s_ready, 15)
            sp.dma_start(k.sorted[order, 1:1 + SORT_N].rearrange("(p j) -> p j", p=P), buf[0][:].bitcast(I32)).then_inc(s_out, 16)
            sp.wait_ge(s_out, 16 * (4 if first else 1))

        @block.scalar
        def _(act):
            if first:
                for b in range(2):
                    act.dma_start(k.spare[b:b + 1, :], k.ones[b:b + 1, 0:1]).then_inc(s_laid[b], 16)
                act.wait_ge(s_padded, 1)
                act.dma_start(k.raw_s[E:EP].rearrange("(p r) w -> p r w", r=2), pad[:]).then_inc(s_records, 16)
                act.wait_ge(s_cols, 32)
                rows = k.raw_s[0:E].rearrange("(p j) w -> p j w", p=LP)
                with act.Fori(0, LCHUNKS // 2) as t:
                    for b in range(2):
                        at = bass.ds((t * 2 + b) * LC, LC)
                        act.wait_ge(s_attr[b], (t + 1) * 16)
                        nc.scalar.activation(edge[b][:, :, RBF], dist[:, at], ACT.Copy)
                        nc.scalar.activation(edge[b][:, :, RBF + 1].bitcast(I32), dsts[:, at], ACT.Copy).then_inc(s_put[b], 1)
                        act.wait_ge(s_put[b], t + 1)
                        act.dma_start(rows[:, at, :], edge[b][:]).then_inc(s_laid[b], 16)
                act.wait_ge(s_zeros, 1)
                with act.Fori(0, CHUNKS) as n:
                    for table, w in ((k.fill_s, FILL_S), (k.fill_d, F)):
                        act.dma_start(table.rearrange("(p j) w -> p j w", p=P)[:, bass.ds(n * C, C), :],
                                      zeros[:, 0:C * w].rearrange("p (j w) -> p j w", w=w)).then_inc(s_records, 16)
                act.wait_ge(s_records, 16 * (1 + 2 * CHUNKS))
                for b in range(2):
                    act.wait_ge(s_laid[b], 16 * (LCHUNKS // 2 + 1))
            else:
                raw = k.raw_d
                act.wait_ge(s_padded, 1)
                act.dma_start(raw[E:EP].rearrange("(p r) w -> p r w", r=2), pad[:, :, REC_S - REC_D:]).then_inc(s_records, 16)
                act.dma_start(raw[0:E, 0:EF], i["edge_attr_16"]).then_inc(s_records, 16)
                act.dma_start(raw[0:E, EF:EF + 1], column(i["edge_weight"]), allow_slow_non_contiguous=True).then_inc(s_records, 16)
                act.dma_start(raw.bitcast(I32)[0:E, EF + 1:], column(i["src"]), allow_slow_non_contiguous=True).then_inc(s_records, 16)
                act.wait_ge(s_records, 64)

        @block.tensor
        def _(pe):
            if first:
                pe.wait_ge(s_falls, 1)
                nc.tensor.matmul(total[0:1, 0:1], falls[:], k.ones[0:LP, 0:1], start=True, stop=True).then_inc(s_total, 1)
            for n in range(14):
                pe.wait_ge(s_ready, n + 1)
                for b in range(W // P):
                    ins = nc.tensor.transpose(turned[:, b * P:(b + 1) * P], buf[0][:, b * P:(b + 1) * P], k.ident[:])
                ins.then_inc(s_turned, 1)

        @block.vector
        def _(dve):
            v = nc.vector
            ch = Chain(dve, s_step)
            if first:
                v.memset(zero[:], 0)
                v.memset(before[0:1, 0:1], 0)
                v.memset(dst_key[:], N)
                v.memset(buf[1][:].bitcast(I32), N).then_inc(s_pad, 1)
            ch.done(v.memset(pad[:], 0.0))
            v.memset(pad[:, :, REC_S - 1].bitcast(I32), N).then_inc(s_padded, 1)
            if first:
                v.memset(zeros[:], 0.0).then_inc(s_zeros, 1)
            dve.wait_ge(s_pos, 2 if first else 1)
            for m in range(11, 18):
                ch.done(v.tensor_scalar(pbit[:, m - 10:m - 9], prow[:], m - 11, 1, ALU.logical_shift_right, ALU.bitwise_and))
            ch.step(v.memset(sgn[:], 1.0))
            ch.done(v.memset(flip[:], 1.0))
            ch.done(v.tensor_scalar(sgn[:, 1:8], pbit[:, 1:8], -2.0, 1.0, ALU.mult, ALU.add))
            ch.done(v.tensor_tensor(flip[:, 1:9], sgn[:, 1:9], sgn[:, 0:8], ALU.mult))
            if first:
                dve.wait_ge(s_keys, 64)
                for key, rec in ((dst_key[:], dst_rec[:]), (buf[1][:].bitcast(I32), buf[0][:].bitcast(I32))):
                    ch.done(v.tensor_scalar(key, key, float(KEY_BIAS), None, ALU.add))
                    ch.done(v.tensor_scalar(rec, key, IDX_BITS, None, ALU.logical_shift_left))
                    ch.done(v.tensor_tensor(rec, rec, pos[:], ALU.bitwise_or))
                dve.sem_inc(s_rec, 1)
                dve.wait_ge(s_before, 32)
                dve.wait_ge(s_cols, 32)
                ch.done(v.tensor_tensor(before[:], before[:], dsts[:], ALU.is_gt))
                ch.done(v.tensor_reduce(falls[:], before[:], AX, ALU.add))
                dve.sem_inc(s_falls, 1)
                dve.wait_ge(s_total, 1)
                ch.done(v.tensor_scalar(k.unsorted[:], total[0:1, 0:1], 1.0, None, ALU.min))
            else:
                dve.wait_ge(s_keys, 16)
            cur = 0

            def compare(m, d, up_only):
                nonlocal cur
                a, b = buf[cur], buf[1 - cur]
                if up_only:
                    va = a[:].rearrange("p (n s d) -> p s n d", s=2, d=d)
                    vb = b[:].rearrange("p (n s d) -> p s n d", s=2, d=d)
                    ch.step(v.tensor_tensor(vb[:, 0], va[:, 0], va[:, 1], ALU.min))
                    ch.step(v.tensor_tensor(vb[:, 1], va[:, 0], va[:, 1], ALU.max))
                else:
                    for down in range(2):
                        r = 2 ** m
                        va = a[:].rearrange("p (g w r) -> p w g r", w=2, r=r)[:, down].rearrange("p g (n s d) -> p s g n d", s=2, d=d)
                        vb = b[:].rearrange("p (g w r) -> p w g r", w=2, r=r)[:, down].rearrange("p g (n s d) -> p s g n d", s=2, d=d)
                        ch.step(v.tensor_tensor(vb[:, down], va[:, 0], va[:, 1], ALU.min))
                        ch.step(v.tensor_tensor(vb[:, 1 - down], va[:, 0], va[:, 1], ALU.max))
                ch.wait()
                cur = 1 - cur

            turns = 0

            def turn():
                nonlocal cur, turns
                if cur == 1:
                    ch.done(v.tensor_copy(buf[0][:], buf[1][:]))
                dve.sem_inc(s_ready, 1)
                turns += 1
                dve.wait_ge(s_turned, turns)
                ch.done(v.tensor_copy(buf[0][:], turned[:]))
                cur = 0

            for m in range(1, 19):
                if m >= 11:
                    ch.done(v.tensor_scalar(buf[cur][:], buf[cur][:], flip[:, m - 10:m - 9], None, ALU.mult))
                if m >= 12:
                    turn()
                    for b in range(m - 12, -1, -1):
                        compare(m, 2 ** b, True)
                    turn()
                for b in range(min(m, 11) - 1, -1, -1):
                    compare(m, 2 ** b, m >= 11)
            if cur == 1:
                ch.done(v.tensor_copy(buf[0][:], buf[1][:]))
            dve.sem_inc(s_ready, 1)


assert CHUNKS * C == J and PAIRS * 2 == CHUNKS and NT % GRP == 0


def bc(ap, n):
    return ap.unsqueeze(2).to_broadcast([ap.shape[0], ap.shape[1], n])


def rows_of(ap, n):
    return ap.unsqueeze(1).to_broadcast([ap.shape[0], n, ap.shape[1]])


def clear(nc, sems):
    span = range(min(s.num for s in sems), max(s.num for s in sems) + 1)
    nc.gpsimd.dma_reset(span)
    nc.gpsimd.sem_clear(span)
    nc.all_engine_barrier()


class Phase:

    def __init__(self, nc, ctx, tag):
        self.nc, self.ctx, self.tag, self.sems = nc, ctx, tag, []

    def sb(self, name, shape, dt=F32):
        return self.ctx.enter_context(self.nc.sbuf_tensor(f"{self.tag}_{name}", shape, dt))

    def ps(self, name, shape, dt=F32):
        return self.ctx.enter_context(self.nc.psum_tensor(f"{self.tag}_{name}", shape, dt))

    def sem(self, name):
        s = self.ctx.enter_context(self.nc.semaphore(f"{self.tag}_{name}"))
        self.sems.append(s)
        return s

    def block(self):
        self.ctx.callback(clear, self.nc, self.sems)
        return self.ctx.enter_context(self.nc.Block())


def gather(nc, out, table, index):
    return nc.gpsimd.indirect_dma_start(out=out, out_offset=None, in_=table,
                                        in_offset=bass.IndirectOffsetOnAxis(ap=index, axis=0))


def scatter(nc, table, index, rows, last):
    return nc.gpsimd.indirect_dma_start(out=table, out_offset=bass.IndirectOffsetOnAxis(ap=index, axis=0), in_=rows,
                                        in_offset=None, bounds_check=last, oob_is_err=False)


def open_stores(sp, k, s_stored):
    for b in range(2):
        sp.dma_start(k.spare[b:b + 1, :], k.ones[b:b + 1, 0:1]).then_inc(s_stored[b], 16)


def pool_gathers(nc, pool, index, staged, rows, width, table, s_staged, s_rows, used, s_turn):
    with pool.Fori(0, PAIRS) as t:
        for b in range(2):
            for s, n in used[b]:
                pool.wait_ge(s, (t + 1) * n)
            nc.gpsimd.tensor_copy(staged[:, b], index[:, bass.ds((t * 2 + b) * C, C)]).then_inc(s_staged, 1)
            pool.wait_ge(s_staged, t * 2 + b + 1)
            pool.sem_inc(s_turn, 1)
            for c in range(C):
                gather(nc, rows[b][:, c, 0:width], table, staged[:, b, c:c + 1]).then_inc(s_rows[b], 16)


class Projector:

    def __init__(self, ph, ident):
        self.nc, self.ident = ph.nc, ident
        self.pst = [ph.ps(f"turn{b}", [P, GRP, P]) for b in range(2)]
        self.psp = [ph.ps(f"prod{b}", [P, GRP, P]) for b in range(2)]
        self.st = [ph.sb(f"turned{b}", [P, GRP, P]) for b in range(2)]
        self.s_t, self.s_tc, self.s_p, self.s_pc = (ph.sem(n) for n in ("s_turned", "s_turned_copied", "s_product", "s_product_copied"))
        self.npe = self.nact = self.ndve = 0

    def pe(self, pe, src, K, w, M):
        n0, groups = self.npe, NT // GRP
        for g in range(groups + 1):
            if g < groups:
                i = n0 + g
                if i >= 2:
                    pe.wait_ge(self.s_tc, i - 1)
                for k in range(GRP):
                    ins = self.nc.tensor.transpose(self.pst[i % 2][0:K, k, :], src(g * GRP + k), self.ident[:])
                ins.then_inc(self.s_t, 1)
            if g >= 1:
                i = n0 + g - 1
                pe.wait_ge(self.s_tc, i + 1)
                if i >= 2:
                    pe.wait_ge(self.s_pc, i - 1)
                for k in range(GRP):
                    ins = self.nc.tensor.matmul(self.psp[i % 2][:, k, 0:M], self.st[i % 2][0:K, k, :], w, start=True, stop=True)
                ins.then_inc(self.s_p, 1)
        self.npe += groups

    def act(self, act, K):
        for i in range(self.nact, self.nact + NT // GRP):
            act.wait_ge(self.s_t, i + 1)
            if i >= 2:
                act.wait_ge(self.s_p, i - 1)
            self.nc.scalar.activation(self.st[i % 2][0:K], self.pst[i % 2][0:K], ACT.Copy).then_inc(self.s_tc, 1)
        self.nact += NT // GRP

    def dve(self, dve, dst, M):
        for g in range(NT // GRP):
            i = self.ndve + g
            dve.wait_ge(self.s_p, i + 1)
            self.nc.vector.tensor_copy(dst[:, g * GRP:(g + 1) * GRP, 0:M], self.psp[i % 2][:, :, 0:M]).then_inc(self.s_pc, 1)
        self.ndve += NT // GRP
        dve.wait_ge(self.s_pc, self.ndve)


class Norm:

    def __init__(self, ph):
        self.nc = ph.nc
        self.stat = ph.sb("stat", [P, NT])
        self.root = ph.sb("root", [P, NT])
        self.sq = ph.sb("sq", [P, NT, F])
        self.s_var, self.s_root = ph.sem("s_var"), ph.sem("s_root")
        self.nd = self.na = 0

    def rsqrt(self, dve, ch):
        self.nd += 1
        dve.sem_inc(self.s_var, 1)
        dve.wait_ge(self.s_root, self.nd)
        ch.done(self.nc.vector.reciprocal(self.stat[:], self.root[:]))

    def variance(self, ch, centred):
        ch.done(self.nc.vector.tensor_tensor(self.sq[:], centred, centred, ALU.mult))
        ch.done(self.nc.vector.tensor_reduce(self.stat[:], self.sq[:], AX, ALU.add))
        ch.done(self.nc.vector.tensor_scalar(self.stat[:], self.stat[:], 1.0 / F, EPS, ALU.mult, ALU.add))

    def dve(self, dve, ch, x, out, gain=None, bias=None):
        v = self.nc.vector
        ch.done(v.tensor_reduce(self.stat[:], x, AX, ALU.add))
        ch.done(v.tensor_scalar(self.stat[:], self.stat[:], 1.0 / F, None, ALU.mult))
        ch.done(v.tensor_tensor(out, x, bc(self.stat[:], F), ALU.subtract))
        self.variance(ch, out)
        self.rsqrt(dve, ch)
        ch.done(v.tensor_tensor(out, out, bc(self.stat[:], F), ALU.mult))
        if gain is not None:
            ch.done(v.tensor_tensor(out, out, rows_of(gain, NT), ALU.mult))
            ch.done(v.tensor_tensor(out, out, rows_of(bias, NT), ALU.add))

    def act(self, act):
        self.na += 1
        act.wait_ge(self.s_var, self.na)
        self.nc.scalar.activation(self.root[:], self.stat[:], ACT.Sqrt).then_inc(self.s_root, 1)


def constants(nc, k):
    with ExitStack() as ctx:
        ph = Phase(nc, ctx, "const")
        s, s_i = ph.sem("s_filled"), ph.sem("s_iota")
        block = ph.block()

        @block.gpsimd
        def _(pool):
            g = nc.gpsimd
            g.iota(k.iota[:], [[1, P]], base=0, channel_multiplier=0, allow_small_or_imprecise_dtypes=True)
            g.iota(k.rowstart[:], [[0, 1]], base=0, channel_multiplier=J, allow_small_or_imprecise_dtypes=True).then_inc(s_i, 1)
            g.memset(k.ones[:], 1.0)
            g.memset(k.ident[:], 0.0).then_inc(s, 1)
            g.memset(k.below[:], 1.0).then_inc(s, 1)
            g.memset(k.above[:], 1.0).then_inc(s, 1)
            pool.wait_ge(s, 3)
            g.affine_select(out=k.ident[:], in_=k.ident[:], compare_op=ALU.not_equal, fill=1.0, base=0, pattern=[[-1, P]], channel_multiplier=1)
            g.affine_select(out=k.below[:], in_=k.below[:], compare_op=ALU.is_gt, fill=0.0, base=0, pattern=[[-1, P]], channel_multiplier=1)
            g.affine_select(out=k.above[:], in_=k.above[:], compare_op=ALU.is_gt, fill=0.0, base=0, pattern=[[1, P]], channel_multiplier=-1)


def unpack(nc, k, o):
    with ExitStack() as ctx:
        ph = Phase(nc, ctx, f"unpack{o}")
        bits, prev = ph.sb("bits", [P, J], I32), ph.sb("prev", [P, J], I32)
        prevf = ph.sb("prevf", [P, J])
        s_in, s_step = ph.sem("s_in"), ph.sem("s_step")
        keyf, perm, keep, keepr = k.keyf[o], k.perm[o], k.keep[o], k.keepr[o]
        block = ph.block()

        @block.sync
        def _(sp):
            sp.dma_start(bits[:], k.sorted[o, 1:1 + EP].rearrange("(p j) -> p j", p=P)).then_inc(s_in, 16)
            sp.dma_start(prev[:], k.sorted[o, 0:EP].rearrange("(p j) -> p j", p=P)).then_inc(s_in, 16)

        @block.vector
        def _(dve):
            v = nc.vector
            ch = Chain(dve, s_step)
            dve.wait_ge(s_in, 32)
            ch.done(v.tensor_scalar(perm[:], bits[:], (1 << IDX_BITS) - 1, None, ALU.bitwise_and))
            ch.step(v.tensor_scalar(bits[:], bits[:], IDX_BITS, None, ALU.logical_shift_right))
            ch.done(v.tensor_scalar(prev[:], prev[:], IDX_BITS, None, ALU.logical_shift_right))
            ch.step(v.tensor_scalar(keyf[:], bits[:], float(-KEY_BIAS), None, ALU.add))
            ch.done(v.tensor_scalar(prevf[:], prev[:], float(-KEY_BIAS), None, ALU.add))
            ch.done(v.tensor_tensor(keep[:], keyf[:], prevf[:], ALU.is_equal))
            ch.step(v.tensor_copy(k.first[o][:], keyf[:, 0:1]))
            ch.step(v.tensor_copy(k.firstf[o][:], keyf[:, 0:1]))
            ch.step(v.tensor_copy(k.lastf[o][:], keyf[:, J - 1:J]))
            ch.done(v.tensor_copy(keepr[:], keep[:]))
            ch.done(v.memset(keepr[:, 0:1], 0.0))
            if o == 1:
                ch.done(v.tensor_scalar(k.pen[:], keepr[:], -1.0, FAR, ALU.add, ALU.mult))


def edge_records(nc, i, k):
    with ExitStack() as ctx:
        ph = Phase(nc, ctx, "records")
        staged = ph.sb("staged", [P, 2, C], I32)
        rows = [ph.sb(f"rows{b}", [P, C, REC_S]) for b in range(2)]
        quots, rems = ([ph.sb(f"{n}{o}", [P, C]) for o in range(ORDERS)] for n in ("quot", "rem"))
        hot_p = [ph.sb(f"hot_p{o}", [P, C, P], BF16) for o in range(ORDERS)]
        hot_t = [ph.sb(f"hot_t{o}", [P, C, NT], BF16) for o in range(ORDERS)]
        part = [ph.ps(f"part{o}", [P, 512]) for o in range(ORDERS)]
        s_staged, s_step, s_hot, s_part, s_turn = (ph.sem(n) for n in ("s_staged", "s_step", "s_hot", "s_part", "s_turn"))
        s_rows, s_stored, s_kept = ([ph.sem(f"{n}{b}") for b in range(2)] for n in ("s_rows", "s_stored", "s_kept"))
        pad = ph.sb("pad", [P, EF])
        s_pad, s_in, s_out = ph.sem("s_pad"), ph.sem("s_in"), ph.sem("s_out")
        rest = E - (P - 1) * J
        block = ph.block()

        @block.scalar
        def _(act):
            act.dma_start(k.edges_d[0:E], i["edge_attr_16"]).then_inc(s_out, 16)
            act.wait_ge(s_pad, 1)
            for n, r in enumerate((slice(E, E + P), slice(EP - P, EP))):
                act.dma_start(k.edges_d[r], pad[:]).then_inc(s_out, 16)
                act.wait_ge(s_out, 32 + 16 * n)
            for into, src in ((k.weight, i["edge_weight"]), (k.other[0], i["src"])):
                act.dma_start(into[0:P - 1, :], src[0:(P - 1) * J].rearrange("(p j) -> p j", p=P - 1)).then_inc(s_in, 16)
                act.dma_start(into[P - 1:P, 0:rest], src[(P - 1) * J:E].rearrange("(p j) -> p j", p=1)).then_inc(s_in, 16)
            act.wait_ge(s_in, 64)

        @block.gpsimd
        def _(pool):
            pool_gathers(nc, pool, k.perm[1], staged, rows, REC_S, k.raw_s, s_staged, s_rows,
                         [[(s_stored[b], 16), (s_kept[b], 1)] for b in range(2)], s_turn)

        @block.sync
        def _(sp):
            open_stores(sp, k, s_stored)
            with sp.Fori(0, PAIRS) as t:
                for b in range(2):
                    sp.wait_ge(s_rows[b], (t + 1) * (16 * C))
                    sp.dma_start(k.edges_s.rearrange("(p j) w -> p j w", p=P)[:, bass.ds((t * 2 + b) * C, C), :], rows[b][:]).then_inc(s_stored[b], 16)
            for b in range(2):
                sp.wait_ge(s_stored[b], 16 * (PAIRS + 1))

        @block.tensor
        def _(pe):
            with pe.Fori(0, CHUNKS) as n:
                for o in range(ORDERS):
                    pe.wait_ge(s_hot, n * ORDERS + o + 1)
                    for c in range(C):
                        ins = nc.tensor.matmul(part[o][:, 0:NT], hot_p[o][:, c, :], hot_t[o][:, c, :], start=(c == 0), stop=(c == C - 1))
                    ins.then_inc(s_part, 1)

        @block.vector
        def _(dve):
            v = nc.vector
            ch = Chain(dve, s_step)
            for o in range(ORDERS):
                ch.done(v.memset(k.count[o][:], 0.0))
            v.memset(pad[:], 0.0)
            v.memset(k.weight[:], 0.0)
            v.memset(k.other[0][:], N).then_inc(s_pad, 1)
            for b in range(2):
                dve.sem_inc(s_kept[b], 1)
            PER, n0 = 2 * (4 * ORDERS + 1), ch.n
            with dve.Fori(0, PAIRS) as t:
                ch.n, ch.base = n0, t * PER
                for b in range(2):
                    at = bass.ds((t * 2 + b) * C, C)
                    for o in range(ORDERS):
                        quot, rem = quots[o], rems[o]
                        ch.done(v.tensor_scalar(quot[:], k.keyf[o][:, at], float(-(NT // 2)), 1.0 / NT, ALU.add, ALU.mult))
                        ch.done(v.tensor_scalar(quot[:], quot[:], ROUND, -ROUND, ALU.add, ALU.add))
                        ch.done(v.scalar_tensor_tensor(out=rem[:], in0=quot[:], scalar=float(-NT), in1=k.keyf[o][:, at], op0=ALU.mult, op1=ALU.add))
                        v.tensor_tensor(hot_p[o][:], bc(quot[:], P), rows_of(k.iota[:], C), ALU.is_equal)
                        v.tensor_tensor(hot_t[o][:], bc(rem[:], NT), rows_of(k.iota[:, 0:NT], C), ALU.is_equal).then_inc(s_hot, 1)
                    for o in range(ORDERS):
                        dve.wait_ge(s_part, (t * 2 + b) * ORDERS + o + 1)
                        ch.done(v.tensor_tensor(k.count[o][:], k.count[o][:], part[o][:, 0:NT], ALU.add))
                    dve.wait_ge(s_rows[b], (t + 1) * (16 * C))
                    ch.done(v.tensor_copy(k.other[1][:, at], rows[b][:, :, REC_S - 1].bitcast(I32)))
                    dve.sem_inc(s_kept[b], 1)
            assert ch.n - n0 == PER, ch.n - n0


def dst_records(nc, k):
    with ExitStack() as ctx:
        ph = Phase(nc, ctx, "dstrec")
        staged = ph.sb("staged", [P, 2, C], I32)
        rows = [ph.sb(f"rows{b}", [P, C, REC_D]) for b in range(2)]
        s_staged, s_step, s_turn = (ph.sem(n) for n in ("s_staged", "s_step", "s_turn"))
        s_rows, s_stored, s_kept = ([ph.sem(f"{n}{b}") for b in range(2)] for n in ("s_rows", "s_stored", "s_kept"))
        s_here = ph.sem("s_here")
        block = ph.block()

        @block.tensor
        def _(pe):
            pe.sem_inc(s_here, 1)

        @block.scalar
        def _(act):
            act.sem_inc(s_here, 1)

        @block.gpsimd
        def _(pool):
            pool_gathers(nc, pool, k.perm[0], staged, rows, REC_D, k.raw_d, s_staged, s_rows,
                         [[(s_stored[b], 16), (s_kept[b], 1)] for b in range(2)], s_turn)

        @block.sync
        def _(sp):
            open_stores(sp, k, s_stored)
            with sp.Fori(0, PAIRS) as t:
                for b in range(2):
                    sp.wait_ge(s_rows[b], (t + 1) * (16 * C))
                    sp.dma_start(k.edges_d.rearrange("(p j) w -> p j w", p=P)[:, bass.ds((t * 2 + b) * C, C), :], rows[b][:, :, 0:EF]).then_inc(s_stored[b], 16)
            for b in range(2):
                sp.wait_ge(s_stored[b], 16 * (PAIRS + 1))

        @block.vector
        def _(dve):
            v = nc.vector
            ch = Chain(dve, s_step)
            for b in range(2):
                dve.sem_inc(s_kept[b], 1)
            with dve.Fori(0, PAIRS) as t:
                ch.n, ch.base = 0, t * 4
                for b in range(2):
                    at = bass.ds((t * 2 + b) * C, C)
                    dve.wait_ge(s_rows[b], (t + 1) * (16 * C))
                    ch.step(v.tensor_copy(k.weight[:, at], rows[b][:, :, EF]))
                    ch.done(v.tensor_copy(k.other[0][:, at], rows[b][:, :, EF + 1].bitcast(I32)))
                    dve.sem_inc(s_kept[b], 1)
def segments(nc, k, o):
    with ExitStack() as ctx:
        ph = Phase(nc, ctx, f"segments{o}")
        cum, tot, pre = ph.sb("cum", [P, NT]), ph.sb("tot", [P, 1]), ph.sb("pre", [P, 1])
        one = ph.sb("one", [P, NT])
        flag, tmp = ph.sb("flag", [P, NT]), ph.sb("tmp", [P, NT])
        lastpos = ph.sb("lastpos", [P, NT])
        at1, f1, g1 = ph.sb("at1", [P, 1]), ph.sb("f1", [P, 1]), ph.sb("g1", [P, 1])
        diag = ph.sb("diag", [P, P])
        ps1, ps2 = ph.ps("ps1", [P, 512]), ph.ps("ps2", [P, 512])
        s_step, s_tot, s_pre, s_pos, s_put, s_got, s_diag, s_row = (ph.sem(n) for n in ("s_step", "s_tot", "s_pre", "s_pos", "s_put", "s_got", "s_diag", "s_row"))
        block = ph.block()

        @block.tensor
        def _(pe):
            pe.wait_ge(s_tot, 1)
            nc.tensor.matmul(ps1[:, 0:1], k.above[:], tot[:], start=True, stop=True).then_inc(s_pre, 1)
            pe.wait_ge(s_diag, 1)
            nc.tensor.matmul(ps2[:, 0:P], k.ones[:], diag[:], start=True, stop=True).then_inc(s_row, 1)

        @block.sync
        def _(sp):
            sp.wait_ge(s_pos, 1)
            sp.dma_start(k.lastpos[o].rearrange("(p t) a -> p (t a)", p=P), lastpos[:]).then_inc(s_put, 16)

        @block.gpsimd
        def _(pool):
            pool.wait_ge(s_put, 16)
            gather(nc, at1[:, 0:1], k.lastpos[o], k.first[o][:, 0:1]).then_inc(s_got, 16)

        @block.vector
        def _(dve):
            v = nc.vector
            ch = Chain(dve, s_step)
            ch.done(v.memset(one[:], 1.0))
            ch.done(v.tensor_tensor_scan(cum[:], one[:], k.count[o][:], 0.0, ALU.mult, ALU.add))
            ch.done(v.tensor_copy(tot[:], cum[:, NT - 1:NT]))
            dve.sem_inc(s_tot, 1)
            dve.wait_ge(s_pre, 1)
            ch.done(v.tensor_copy(pre[:], ps1[:, 0:1]))
            ch.done(v.tensor_scalar(cum[:], cum[:], pre[:], None, ALU.add))
            ch.step(v.tensor_scalar(flag[:], k.count[o][:], 0.0, None, ALU.is_equal))
            ch.step(v.tensor_tensor(tmp[:], cum[:], k.count[o][:], ALU.subtract))
            ch.done(v.tensor_scalar(lastpos[:], cum[:], -1.0, None, ALU.add))
            dve.sem_inc(s_pos, 1)
            ch.done(v.scalar_tensor_tensor(out=k.start[o][:], in0=flag[:], scalar=float(SKIP), in1=tmp[:], op0=ALU.mult, op1=ALU.add))
            ch.done(v.tensor_scalar(tmp[:], lastpos[:], -1.0, float(EP), ALU.mult, ALU.add))
            ch.done(v.tensor_tensor(tmp[:], tmp[:], flag[:], ALU.mult))
            ch.done(v.tensor_tensor(k.end[o][:], tmp[:], lastpos[:], ALU.add))
            ch.done(v.tensor_scalar(diag[:], k.ident[:], k.lastf[o][:], None, ALU.mult))
            dve.sem_inc(s_diag, 1)
            dve.wait_ge(s_row, 1)
            ch.done(v.tensor_scalar(diag[:], ps2[:, 0:P], k.firstf[o][:], None, ALU.is_equal))
            ch.done(v.tensor_tensor(k.mask[o][:], diag[:], k.below[:], ALU.mult))
            dve.wait_ge(s_got, 16)
            ch.done(v.tensor_tensor(f1[:], at1[:], k.rowstart[:], ALU.subtract))
            ch.done(v.tensor_scalar(f1[:], f1[:], float(J), None, ALU.is_lt))
            ch.done(v.tensor_tensor(f1[:], f1[:], k.keep[o][:, 0:1], ALU.mult))
            ch.done(v.tensor_scalar(g1[:], f1[:], -1.0, 1.0, ALU.mult, ALU.add))
            ch.done(v.tensor_tensor(at1[:], at1[:], f1[:], ALU.mult))
            ch.step(v.scalar_tensor_tensor(out=k.cread[o][:], in0=g1[:], scalar=float(EP), in1=at1[:], op0=ALU.mult, op1=ALU.add))
            ch.done(v.scalar_tensor_tensor(out=k.cwrite[o][:], in0=g1[:], scalar=float(SKIP), in1=at1[:], op0=ALU.mult, op1=ALU.add))


def collect(nc, k, o, res, W, tail, out, softmax, tag):
    with ExitStack() as ctx:
        ph = Phase(nc, ctx, tag)
        here, fixed = ph.sb("here", [P, W]), ph.sb("fixed", [P, W])
        diag, wt, wtT = ph.sb("diag", [P, P]), ph.sb("wt", [P, P]), ph.sb("wtT", [P, P])
        cm, m2, ex = ph.sb("cm", [P, 1]), ph.sb("m2", [P, 1]), ph.sb("ex", [P, 2])
        psr, pst, psc = ph.ps("psr", [P, 512]), ph.ps("pst", [P, 512]), ph.ps("psc", [P, 512])
        s_step, s_here, s_diag, s_row, s_arg, s_exp, s_w, s_wT, s_wTc, s_c, s_fixed, s_put, s_got = (
            ph.sem(n) for n in ("s_step", "s_here", "s_diag", "s_row", "s_arg", "s_exp", "s_w", "s_wT", "s_wTc", "s_c", "s_fixed", "s_put", "s_got"))
        with nc.Block() as block:
            @block.gpsimd
            def _(pool):
                gather(nc, here[:], res, k.cread[o][:, 0:1]).then_inc(s_here, 16)
                pool.wait_ge(s_fixed, 1)
                scatter(nc, res, k.cwrite[o][:, 0:1], fixed[:], EP - 1).then_inc(s_put, 16)
                pool.wait_ge(s_put, 16)
                for t in range(NT):
                    gather(nc, out[:, t, :], res, k.end[o][:, t:t + 1]).then_inc(s_got, 16)
                pool.wait_ge(s_got, 16 * NT)

            @block.tensor
            def _(pe):
                if softmax:
                    pe.wait_ge(s_diag, 1)
                    nc.tensor.matmul(psr[:, 0:P], k.ones[:], diag[:], start=True, stop=True).then_inc(s_row, 1)
                pe.wait_ge(s_w, 1)
                nc.tensor.transpose(pst[:, 0:P], wt[:], k.ident[:]).then_inc(s_wT, 1)
                pe.wait_ge(s_wTc, 1)
                nc.tensor.matmul(psc[:, 0:W], wtT[:], tail, start=True, stop=True).then_inc(s_c, 1)

            @block.scalar
            def _(act):
                if softmax:
                    act.wait_ge(s_arg, 1)
                    nc.scalar.activation(wt[:], wt[:], ACT.Exp).then_inc(s_exp, 1)
                    act.wait_ge(s_arg, 2)
                    nc.scalar.activation(ex[:], ex[:], ACT.Exp).then_inc(s_exp, 1)

            @block.vector
            def _(dve):
                v = nc.vector
                ch = Chain(dve, s_step)
                if softmax:
                    ch.done(v.tensor_scalar(diag[:], k.ident[:], tail[:, F + 1:F + 2], None, ALU.mult))
                    dve.sem_inc(s_diag, 1)
                    ch.done(v.tensor_scalar(wt[:], k.mask[o][:], -1.0, FAR, ALU.add, ALU.mult))
                    dve.wait_ge(s_row, 1)
                    ch.done(v.tensor_tensor(wt[:], wt[:], psr[:, 0:P], ALU.add))
                    ch.done(v.tensor_reduce(cm[:], wt[:], AX, ALU.max))
                    ch.done(v.tensor_scalar(wt[:], wt[:], cm[:], None, ALU.subtract))
                    dve.sem_inc(s_arg, 1)
                    dve.wait_ge(s_exp, 1)
                    ch.done(v.tensor_tensor(wt[:], wt[:], k.mask[o][:], ALU.mult))
                else:
                    ch.done(v.tensor_copy(wt[:], k.mask[o][:]))
                dve.sem_inc(s_w, 1)
                dve.wait_ge(s_wT, 1)
                ch.done(v.tensor_copy(wtT[:], pst[:, 0:P]))
                dve.sem_inc(s_wTc, 1)
                dve.wait_ge(s_c, 1)
                dve.wait_ge(s_here, 16)
                if softmax:
                    ch.done(v.tensor_tensor(m2[:], here[:, F + 1:F + 2], cm[:], ALU.max))
                    ch.step(v.tensor_tensor(ex[:, 0:1], here[:, F + 1:F + 2], m2[:], ALU.subtract))
                    ch.done(v.tensor_tensor(ex[:, 1:2], cm[:], m2[:], ALU.subtract))
                    dve.sem_inc(s_arg, 1)
                    dve.wait_ge(s_exp, 2)
                    ch.done(v.tensor_scalar(here[:], here[:], ex[:, 0:1], None, ALU.mult))
                    ch.done(v.scalar_tensor_tensor(out=fixed[:], in0=psc[:, 0:W], scalar=ex[:, 1:2], in1=here[:], op0=ALU.mult, op1=ALU.add))
                    ch.done(v.tensor_copy(fixed[:, F + 1:F + 2], m2[:]))
                else:
                    ch.done(v.tensor_tensor(fixed[:], here[:], psc[:, 0:W], ALU.add))
                dve.sem_inc(s_fixed, 1)

        clear(nc, ph.sems)


def load_nodes(sp, ins, into, width, sem):
    full, rest = N // NT, N % NT
    sp.dma_start(into[0:full], ins[0:full * NT].rearrange("(p t) f -> p t f", t=NT)).then_inc(sem, 16)
    sp.dma_start(into[full:full + 1, 0:rest], ins[full * NT:N].rearrange("(p t) f -> p t f", p=1)).then_inc(sem, 16)


def scan_columns(nc, out, keep, val, before, width):
    for f in range(width):
        ins = nc.vector.tensor_tensor_scan(out[:, :, f], keep, val[:, :, f], before[:, f:f + 1], ALU.mult, ALU.add)
    return ins


def stream(sp, load, store):
    for b in range(2):
        load(0, b)
    with sp.Fori(0, PAIRS - 1) as t:
        for b in range(2):
            store(t, b)
            load(t + 1, b)
    for b in range(2):
        store(PAIRS - 1, b)


def store_sums(sp, k, res, sums, s_sums, s_stored):
    open_stores(sp, k, s_stored)

    def store(t, b):
        sp.wait_ge(s_sums[b], t + 1)
        sp.dma_start(res[0:EP].rearrange("(p j) w -> p j w", p=P)[:, bass.ds((t * 2 + b) * C, C), :], sums[b][:]).then_inc(s_stored[b], 16)
    return store


def node_inputs(nc, k, i):
    with ExitStack() as ctx:
        ph = Phase(nc, ctx, "nodes")
        emb, embT, adapt = ph.sb("emb", [P, G]), ph.sb("embT", [G, P]), ph.sb("adapt", [G, G])
        both = ph.sb("both", [P, 2 * G])
        z = ph.sb("z", [P, NT, 1], I32)
        zrow = ph.sb("zrow", [P, NT, 2 * G])
        mult = ph.sb("mult", [P, NT, 1])
        table = ph.sb("table", [P, NT, F + G + 1])
        fill = ph.sb("fill", [P, NT, FILL_S])
        low = ph.sb("low", [P, NT])
        neutral = ph.sb("neutral", [1, ACC])
        ps = ph.ps("ps", [P, 512])
        s_in, s_zero, s_step, s_t, s_tc, s_m, s_both, s_z, s_tab, s_out, s_fill, s_low, s_log = (
            ph.sem(n) for n in ("s_in", "s_zero", "s_step", "s_t", "s_tc", "s_m", "s_both", "s_z", "s_tab", "s_out", "s_fill", "s_low", "s_log"))
        NIN = 16 * 8
        NE = i["L0_gnn_emb"].shape[0]
        block = ph.block()

        @block.sync
        def _(sp):
            sp.wait_ge(s_zero, 1)
            load_nodes(sp, i["x"], k.x, F, s_in)
            load_nodes(sp, column(i["node_type_119"]), z, 1, s_in)
            load_nodes(sp, column(i["node_vec"]), mult, 1, s_in)
            sp.dma_start(emb[0:NE, :], i["L0_gnn_emb"]).then_inc(s_in, 16)
            sp.dma_start(adapt[:], i["L0_gnn_adapt"]).then_inc(s_in, 16)
            sp.wait_ge(s_both, 1)
            sp.dma_start(k.by_type, both[:]).then_inc(s_out, 16)
            sp.wait_ge(s_tab, 1)
            sp.dma_start(k.table0.rearrange("(p t) w -> p t w", p=P), table[:]).then_inc(s_out, 16)
            sp.dma_start(k.fillrows.rearrange("(p t) w -> p t w", p=P), fill[:]).then_inc(s_out, 16)
            sp.dma_start(k.acc[EP:EP + 1, :], neutral[:]).then_inc(s_out, 16)
            sp.dma_start(k.sum[EP:EP + 1, :], neutral[:, 0:F]).then_inc(s_out, 16)
            sp.wait_ge(s_out, 16 * 5)

        @block.tensor
        def _(pe):
            pe.wait_ge(s_in, NIN)
            nc.tensor.transpose(ps[0:G, 0:P], emb[:], k.ident[:]).then_inc(s_t, 1)
            pe.wait_ge(s_tc, 1)
            nc.tensor.matmul(ps[:, P:P + G], embT[:], adapt[:], start=True, stop=True).then_inc(s_m, 1)

        @block.gpsimd
        def _(pool):
            pool.wait_ge(s_in, NIN)
            pool.wait_ge(s_out, 16)
            for t in range(NT):
                gather(nc, zrow[:, t, :], k.by_type, z[:, t, :]).then_inc(s_z, 16)
            pool.wait_ge(s_tab, 1)
            for t in range(NT):
                scatter(nc, k.fill_s, k.start[1][:, t:t + 1], fill[:, t, :], EP - 1).then_inc(s_fill, 16)
            pool.wait_ge(s_fill, 16 * NT)

        @block.scalar
        def _(act):
            act.wait_ge(s_low, 1)
            nc.scalar.activation(k.logm[:], low[:], ACT.Ln).then_inc(s_log, 1)

        @block.vector
        def _(dve):
            v = nc.vector
            ch = Chain(dve, s_step)
            for m in (k.x, z, mult, emb, neutral):
                v.memset(m[:], 0)
            ch.done(v.memset(fill[:], 0.0))
            ch.done(v.memset(neutral[:, F + 1:F + 2], -FAR))
            dve.sem_inc(s_zero, 1)
            dve.wait_ge(s_t, 1)
            ch.done(v.tensor_copy(embT[:], ps[0:G, 0:P]))
            dve.sem_inc(s_tc, 1)
            dve.wait_ge(s_m, 1)
            ch.step(v.tensor_copy(both[:, 0:G], emb[:]))
            ch.done(v.tensor_copy(both[:, G:], ps[:, P:P + G]))
            dve.sem_inc(s_both, 1)
            dve.wait_ge(s_in, NIN)
            ch.done(v.tensor_scalar(low[:], mult[:, :, 0], 1.0, None, ALU.max))
            dve.sem_inc(s_low, 1)
            ch.step(v.tensor_copy(table[:, :, 0:F], k.x[:]))
            ch.step(v.tensor_copy(table[:, :, F + G], mult[:, :, 0]))
            dve.wait_ge(s_z, 16 * NT)
            ch.step(v.tensor_copy(table[:, :, F:F + G], zrow[:, :, G:]))
            ch.done(v.tensor_copy(fill[:, :, 0:G], zrow[:, :, 0:G]))
            dve.sem_inc(s_tab, 1)
            dve.wait_ge(s_log, 1)


def first_pass(nc, k, i):
    W = F + G + 1
    with ExitStack() as ctx:
        ph = Phase(nc, ctx, "first")
        staged = ph.sb("staged", [P, 2, C], I32)
        rows = [ph.sb(f"rows{b}", [P, C, W]) for b in range(2)]
        fin = [ph.sb(f"fin{b}", [P, C, FILL_S]) for b in range(2)]
        edge = [ph.sb(f"edge{b}", [P, C, REC_S]) for b in range(2)]
        fo = [ph.sb(f"fo{b}", [P, C, G]) for b in range(2)]
        sums = [ph.sb(f"sums{b}", [P, C, ACC]) for b in range(2)]
        init = ph.sb("init", [P, FILL_S])
        val = ph.sb("val", [P, C, F + 1])
        dot, gate = ph.sb("dot", [P, C, G]), ph.sb("gate", [P, C, F])
        near, phase_, turn, cw, wgt = (ph.sb(n, [P, C]) for n in ("near", "phase", "turn", "cw", "wgt"))
        w1, w2, b1 = ph.sb("w1", [RBF, F]), ph.sb("w2", [F + 1, F]), ph.sb("b1", [F, 1])
        half = ph.sb("half", [P, 1])
        eT = [ph.sb(f"eT{b}", [RBF, COLS * P]) for b in range(2)]
        act1 = [ph.sb(f"act1{b}", [64, COLS * P]) for b in range(2)]
        ps_t, ps_1, ps_2 = ([ph.ps(f"{n}{b}", [P, 512]) for b in range(2)] for n in ("ps_t", "ps_1", "ps_2"))
        s_w, s_ones, s_init, s_staged, s_step, s_turn, s_pe_turn = (ph.sem(n) for n in ("s_w", "s_ones", "s_init", "s_staged", "s_step", "s_turn", "s_pe_turn"))
        s_rows, s_load, s_used, s_sums, s_stored = ([ph.sem(f"{n}{b}") for b in range(2)] for n in ("s_rows", "s_load", "s_used", "s_sums", "s_stored"))
        s_t, s_tc, s_1, s_1a, s_2, s_2c, s_arg, s_cos = (ph.sem(n) for n in ("s_t", "s_tc", "s_1", "s_1a", "s_2", "s_2c", "s_arg", "s_cos"))
        cols = lambda g: min(COLS, C - g * COLS)
        block = ph.block()

        @block.gpsimd
        def _(pool):
            gather(nc, init[:], k.fillrows, k.first[1][:, 0:1]).then_inc(s_init, 16)
            pool.wait_ge(s_init, 16)
            pool_gathers(nc, pool, k.other[1], staged, rows, W, k.table0, s_staged, s_rows,
                         [[(s_used[b], 1)] for b in range(2)], s_turn)

        @block.sync
        def _(sp):
            sp.wait_ge(s_ones, 1)
            sp.dma_start(w1[:], i["L0_gnn_F1W"]).then_inc(s_w, 16)
            sp.dma_start(w2[0:F, :], i["L0_gnn_F2W"]).then_inc(s_w, 16)
            sp.dma_start(w2[F:F + 1, :], i["L0_gnn_F2b"].rearrange("(a n) -> a n", a=1)).then_inc(s_w, 16)
            sp.dma_start(b1[:], column(i["L0_gnn_F1b"])).then_inc(s_w, 16)
            def load(t, b):
                at = bass.ds((t * 2 + b) * C, C)
                sp.wait_ge(s_used[b], t + 1)
                sp.dma_start(edge[b][:], k.edges_s.rearrange("(p j) w -> p j w", p=P)[:, at, :]).then_inc(s_load[b], 16)
                sp.dma_start(fin[b][:], k.fill_s.rearrange("(p j) w -> p j w", p=P)[:, at, :]).then_inc(s_load[b], 16)

            stream(sp, load, store_sums(sp, k, k.acc, sums, s_sums, s_stored))
            for b in range(2):
                sp.wait_ge(s_stored[b], 16 * (PAIRS + 1))

        @block.tensor
        def _(pe):
            pe.wait_ge(s_w, 64)
            with pe.Fori(0, PAIRS) as t:
                for b in range(2):
                    pe.wait_ge(s_load[b], (t + 1) * 32)
                    for s in range(STEPS + 2):
                        n = (t * 2 + b) * STEPS + s
                        q = (b * STEPS + s) % 2
                        if s < STEPS:
                            pe.wait_ge(s_tc, n + 1)
                            pe.sem_inc(s_pe_turn, 1)
                            for c in range(cols(s)):
                                ins = nc.tensor.transpose(ps_t[q][0:RBF, c * P:(c + 1) * P], edge[b][:, s * COLS + c, 0:RBF], k.ident[:])
                            ins.then_inc(s_t, 1)
                        if 1 <= s < STEPS + 1:
                            g = s - 1
                            pe.wait_ge(s_tc, n + 2)
                            pe.wait_ge(s_1a, n)
                            pe.sem_inc(s_pe_turn, 1)
                            w = cols(g) * P
                            nc.tensor.matmul(ps_1[1 - q][0:F, 0:w], w1[:], eT[1 - q][:, 0:w], start=True, stop=True).then_inc(s_1, 1)
                        if s >= 2:
                            g = s - 2
                            pe.wait_ge(s_1a, n + 1)
                            pe.wait_ge(s_2c, n - 1)
                            for c in range(cols(g)):
                                ins = nc.tensor.matmul(ps_2[q][:, c * F:(c + 1) * F], act1[q][0:F + 1, c * P:(c + 1) * P], w2[:], start=True, stop=True)
                            ins.then_inc(s_2, 1)

        @block.scalar
        def _(act):
            act.sem_inc(s_tc, 2)
            act.sem_inc(s_1a, 2)
            act.wait_ge(s_w, 64)
            with act.Fori(0, PAIRS) as t:
                for b in range(2):
                    ch0 = (t * 2 + b) * STEPS
                    act.wait_ge(s_arg, t * 2 + b + 1)
                    nc.scalar.activation(cw[:], phase_[:], ACT.Sin, bias=half[:], scale=-np.pi / 6.0).then_inc(s_cos, 1)
                    for g in range(STEPS + 1):
                        if g < STEPS:
                            w = cols(g) * P
                            act.wait_ge(s_t, ch0 + g + 1)
                            q = (b * STEPS + g) % 2
                            nc.scalar.activation(eT[q][:, 0:w], ps_t[q][0:RBF, 0:w], ACT.Copy).then_inc(s_tc, 1)
                        if g >= 1:
                            w = cols(g - 1) * P
                            act.wait_ge(s_1, ch0 + g)
                            q = (b * STEPS + g - 1) % 2
                            nc.scalar.activation(act1[q][0:F, 0:w], ps_1[q][0:F, 0:w], ACT.Silu, bias=b1[:]).then_inc(s_1a, 1)

        @block.vector
        def _(dve):
            v = nc.vector
            ch = Chain(dve, s_step)
            v.memset(half[:], float(np.pi / 2))
            for m in (*act1,):
                v.memset(m[:], 1.0)
            v.memset(sums[0][:], 0.0)
            ch.done(v.memset(sums[1][:], 0.0))
            dve.sem_inc(s_ones, 1)
            dve.sem_inc(s_2c, 2)
            for b in range(2):
                dve.sem_inc(s_used[b], 1)
            dve.wait_ge(s_init, 16)
            ch.done(v.tensor_copy(fo[1][:, C - 1, :], init[:, 0:G]))
            PER, n0 = 24, ch.n
            with dve.Fori(0, PAIRS) as t:
                ch.n, ch.base = n0, t * PER
                for b in range(2):
                    at = bass.ds((t * 2 + b) * C, C)
                    dve.wait_ge(s_load[b], (t + 1) * 32)
                    d = edge[b][:, :, RBF]
                    ch.step(v.tensor_scalar(near[:], d, 6.0, 0.5, ALU.is_lt, ALU.mult))
                    ch.done(v.tensor_scalar(turn[:], d, 1.0 / 12.0, ROUND, ALU.mult, ALU.add))
                    ch.done(v.tensor_scalar(turn[:], turn[:], -ROUND, -12.0, ALU.add, ALU.mult))
                    ch.done(v.tensor_tensor(turn[:], turn[:], d, ALU.add))
                    ch.done(v.scalar_tensor_tensor(out=phase_[:], in0=turn[:], scalar=-1.0, in1=turn[:], op0=ALU.mult, op1=ALU.max))
                    dve.sem_inc(s_arg, 1)
                    ch.done(scan_columns(nc, fo[b], k.keep[1][:, at], fin[b][:], fo[1 - b][:, C - 1, :], G))
                    dve.wait_ge(s_rows[b], (t + 1) * (16 * C))
                    ch.done(v.tensor_tensor(dot[:], fo[b][:], rows[b][:, :, F:F + G], ALU.mult))
                    ch.done(v.tensor_reduce(wgt[:], dot[:], AX, ALU.add))
                    for g in range(STEPS):
                        dve.wait_ge(s_2, (t * 2 + b) * STEPS + g + 1)
                        c0, w = g * COLS, cols(g)
                        v.tensor_tensor(gate[:, c0:c0 + w, :], ps_2[(b * STEPS + g) % 2][:, 0:w * F].rearrange("p (c f) -> p c f", f=F),
                                        bc(wgt[:, c0:c0 + w], F), ALU.add).then_inc(s_2c, 1)
                    dve.wait_ge(s_2c, (t * 2 + b + 1) * STEPS + 2)
                    dve.wait_ge(s_cos, t * 2 + b + 1)
                    ch.done(v.tensor_scalar(cw[:], cw[:], 1.0, None, ALU.add))
                    ch.done(v.tensor_tensor(cw[:], cw[:], near[:], ALU.mult))
                    ch.step(v.tensor_tensor(cw[:], cw[:], rows[b][:, :, W - 1], ALU.mult))
                    ch.done(v.tensor_tensor(gate[:], gate[:], rows[b][:, :, 0:F], ALU.mult))
                    v.tensor_copy(val[:, :, F], rows[b][:, :, W - 1])
                    v.tensor_tensor(val[:, :, 0:F], gate[:], bc(cw[:], F), ALU.mult).then_inc(s_used[b], 1)
                    dve.wait_ge(s_used[b], t + 2)
                    dve.wait_ge(s_stored[b], (t + 1) * 16)
                    scan_columns(nc, sums[b], k.keepr[1][:, at], val[:], sums[1 - b][:, C - 1, :], F + 1).then_inc(s_sums[b], 1)
                    dve.wait_ge(s_sums[b], t + 1)
            assert ch.n - n0 == PER, ch.n - n0
            dve.wait_ge(s_sums[1], PAIRS)
            v.tensor_copy(k.tail[:], sums[1][:, C - 1, :]).then_inc(s_step, 1)


def after_first(nc, k, i):
    with ExitStack() as ctx:
        ph = Phase(nc, ctx, "afterfirst")
        norm = Norm(ph)
        gain, bias = ph.sb("gain", [P, F]), ph.sb("bias", [P, F])
        tot, t1 = ph.sb("tot", [P, NT]), ph.sb("t1", [P, NT, F])
        s_step, s_w = ph.sem("s_step"), ph.sem("s_w")
        block = ph.block()

        @block.sync
        def _(sp):
            sp.dma_start(gain[:], i["L0_gnn_gn"].partition_broadcast(P)).then_inc(s_w, 16)
            sp.dma_start(bias[:], i["L0_gnn_bn"].partition_broadcast(P)).then_inc(s_w, 16)

        @block.scalar
        def _(act):
            norm.act(act)

        @block.vector
        def _(dve):
            v = nc.vector
            ch = Chain(dve, s_step)
            ch.done(v.tensor_scalar(tot[:], k.agg[:, :, F], 1e-8, None, ALU.max))
            ch.done(v.reciprocal(tot[:], tot[:]))
            ch.done(v.tensor_tensor(t1[:], k.agg[:, :, 0:F], bc(tot[:], F), ALU.mult))
            ch.done(v.tensor_tensor(t1[:], t1[:], k.x[:], ALU.add))
            dve.wait_ge(s_w, 32)
            norm.dve(dve, ch, t1[:], k.h[:], gain[:], bias[:])


def layer_tables(nc, k, i, layer):
    with ExitStack() as ctx:
        ph = Phase(nc, ctx, "tables")
        proj_, norm = Projector(ph, k.ident), Norm(ph)
        wqk, wu = ph.sb("wqk", [F, 2 * F]), ph.sb("wu", [F, F + 1])
        mean, gk = ph.sb("mean", [F, 1]), ph.sb("gk", [F, 1])
        gq, bq = ph.sb("gq", [P, F]), ph.sb("bq", [P, F])
        proj, q, uc = ph.sb("proj", [P, NT, 2 * F]), ph.sb("q", [P, NT, F]), ph.sb("uc", [P, NT, F + 1])
        table, fill = ph.sb("table", [P, NT, ACC]), ph.sb("fill", [P, NT, FILL_S])
        s_w, s_step, s_wt, s_wtc, s_ready, s_tab, s_out, s_fill, s_q, s_placed = (
            ph.sem(n) for n in ("s_w", "s_step", "s_wt", "s_wtc", "s_ready", "s_tab", "s_out", "s_fill", "s_q", "s_placed"))
        of = lambda name: i[f"L0_gnn_{name}"][bass.ds(layer, 1)]
        row = lambda name: of(name).to_broadcast([P, F])
        with nc.Block() as block:
            @block.sync
            def _(sp):
                sp.dma_start(wqk[:, 0:F], of("Wq").rearrange("l a b -> (l a) b")).then_inc(s_w, 16)
                sp.dma_start(wqk[:, F:], of("Wk").rearrange("l a b -> (l a) b")).then_inc(s_w, 16)
                sp.dma_start(gk[:], of("gk").rearrange("l (f a) -> (l f) a", a=1)).then_inc(s_w, 16)
                sp.dma_start(wu[:, F:F + 1], of("bk").rearrange("l (f a) -> (l f) a", a=1)).then_inc(s_w, 16)
                sp.dma_start(gq[:], row("gq")).then_inc(s_w, 16)
                sp.dma_start(bq[:], row("bq")).then_inc(s_w, 16)
                sp.wait_ge(s_tab, 1)
                sp.dma_start(k.table1.rearrange("(p t) w -> p t w", p=P), table[:]).then_inc(s_out, 16)
                sp.wait_ge(s_fill, 1)
                sp.dma_start(k.fillrows.rearrange("(p t) w -> p t w", p=P), fill[:]).then_inc(s_out, 16)
                sp.wait_ge(s_out, 32)

            @block.tensor
            def _(pe):
                pe.wait_ge(s_ready, 1)
                nc.tensor.transpose(proj_.psp[1][0:F, 0, 0:F], wqk[:, F:], k.ident[0:F, 0:F]).then_inc(s_wt, 1)
                pe.wait_ge(s_wtc, 1)
                proj_.pe(pe, lambda t: k.h[:, t, :], F, wqk[:], 2 * F)
                pe.wait_ge(s_q, 1)
                proj_.pe(pe, lambda t: q[:, t, :], F, wu[:], F + 1)

            @block.scalar
            def _(act):
                proj_.act(act, F)
                norm.act(act)
                norm.act(act)
                proj_.act(act, F)

            @block.gpsimd
            def _(pool):
                pool.wait_ge(s_fill, 1)
                for t in range(NT):
                    scatter(nc, k.fill_s, k.start[1][:, t:t + 1], fill[:, t, :], EP - 1).then_inc(s_placed, 16)
                pool.wait_ge(s_placed, 16 * NT)

            @block.vector
            def _(dve):
                v = nc.vector
                ch = Chain(dve, s_step)
                dve.wait_ge(s_w, 96)
                ch.done(v.tensor_reduce(mean[:], wqk[:, F:], AX, ALU.add))
                ch.done(v.tensor_scalar(mean[:], mean[:], 1.0 / F, None, ALU.mult))
                ch.done(v.tensor_scalar(wqk[:, F:], wqk[:, F:], mean[:], None, ALU.subtract))
                dve.sem_inc(s_ready, 1)
                dve.wait_ge(s_wt, 1)
                ch.done(v.tensor_scalar(wu[:, 0:F], proj_.psp[1][0:F, 0, 0:F], gk[:], None, ALU.mult))
                dve.sem_inc(s_wtc, 1)
                proj_.dve(dve, proj, 2 * F)
                norm.variance(ch, proj[:, :, F:])
                norm.rsqrt(dve, ch)
                ch.step(v.tensor_copy(table[:, :, 0:F], k.h[:]))
                ch.step(v.tensor_copy(table[:, :, F], norm.stat[:]))
                ch.done(v.tensor_copy(table[:, :, F + 1], k.logm[:]))
                dve.sem_inc(s_tab, 1)
                norm.dve(dve, ch, proj[:, :, 0:F], q[:], gq[:], bq[:])
                dve.sem_inc(s_q, 1)
                proj_.dve(dve, uc, F + 1)
                ch.step(v.tensor_copy(fill[:, :, 0:F], uc[:, :, 0:F]))
                ch.step(v.tensor_scalar(fill[:, :, F:F + RBF], q[:, :, 0:RBF], 0.1, None, ALU.mult))
                ch.done(v.tensor_copy(fill[:, :, FILL_S - 1], uc[:, :, F]))
                dve.sem_inc(s_fill, 1)

        clear(nc, ph.sems)


def attend(nc, k):
    with ExitStack() as ctx:
        ph = Phase(nc, ctx, "attend")
        staged = ph.sb("staged", [P, 2, C], I32)
        rows = [ph.sb(f"rows{b}", [P, C, ACC]) for b in range(2)]
        fin = [ph.sb(f"fin{b}", [P, C, FILL_S]) for b in range(2)]
        edge = [ph.sb(f"edge{b}", [P, C, REC_S]) for b in range(2)]
        fo = [ph.sb(f"fo{b}", [P, C, FILL_S]) for b in range(2)]
        sums = [ph.sb(f"sums{b}", [P, C, ACC]) for b in range(2)]
        init = ph.sb("init", [P, FILL_S])
        val = ph.sb("val", [P, C, F + 1])
        dot_h, dot_e = ph.sb("dot_h", [P, C, F]), ph.sb("dot_e", [P, C, RBF])
        sh, se = ph.sb("sh", [P, C]), ph.sb("se", [P, C])
        top = [ph.sb(f"top{b}", [P, 1 + C]) for b in range(2)]
        arg, ex = ph.sb("arg", [P, 2, C]), ph.sb("ex", [P, 2, C])
        s_init, s_staged, s_step, s_arg, s_exp, s_turn = (ph.sem(n) for n in ("s_init", "s_staged", "s_step", "s_arg", "s_exp", "s_turn"))
        s_rows, s_load, s_used, s_sums, s_stored = ([ph.sem(f"{n}{b}") for b in range(2)] for n in ("s_rows", "s_load", "s_used", "s_sums", "s_stored"))
        with nc.Block() as block:
            @block.gpsimd
            def _(pool):
                gather(nc, init[:], k.fillrows, k.first[1][:, 0:1]).then_inc(s_init, 16)
                pool.wait_ge(s_init, 16)
                pool_gathers(nc, pool, k.other[1], staged, rows, ACC, k.table1, s_staged, s_rows,
                             [[(s_used[b], 1)] for b in range(2)], s_turn)

            @block.sync
            def _(sp):
                def load(t, b):
                    at = bass.ds((t * 2 + b) * C, C)
                    sp.wait_ge(s_used[b], t + 1)
                    sp.dma_start(edge[b][:], k.edges_s.rearrange("(p j) w -> p j w", p=P)[:, at, :]).then_inc(s_load[b], 16)
                    sp.dma_start(fin[b][:], k.fill_s.rearrange("(p j) w -> p j w", p=P)[:, at, :]).then_inc(s_load[b], 16)

                stream(sp, load, store_sums(sp, k, k.acc, sums, s_sums, s_stored))
                for b in range(2):
                    sp.wait_ge(s_stored[b], 16 * (PAIRS + 1))

            @block.scalar
            def _(act):
                with act.Fori(0, PAIRS) as t:
                    for b in range(2):
                        act.wait_ge(s_arg, t * 2 + b + 1)
                        nc.scalar.activation(ex[:], arg[:], ACT.Exp).then_inc(s_exp, 1)

            @block.vector
            def _(dve):
                v = nc.vector
                ch = Chain(dve, s_step)
                v.memset(top[1][:], 0.0)
                for b in range(2):
                    dve.sem_inc(s_used[b], 1)
                ch.done(v.memset(sums[1][:, C - 1, :], 0.0))
                dve.wait_ge(s_init, 16)
                ch.done(v.tensor_copy(fo[1][:, C - 1, :], init[:]))
                PER, n0 = 28, ch.n
                with dve.Fori(0, PAIRS) as t:
                    ch.n, ch.base = n0, t * PER
                    for b in range(2):
                        at = bass.ds((t * 2 + b) * C, C)
                        dve.wait_ge(s_load[b], (t + 1) * 32)
                        ch.done(scan_columns(nc, fo[b], k.keep[1][:, at], fin[b][:], fo[1 - b][:, C - 1, :], FILL_S))
                        ch.done(v.tensor_tensor(dot_e[:], fo[b][:, :, F:F + RBF], edge[b][:, :, 0:RBF], ALU.mult))
                        ch.done(v.tensor_reduce(se[:], dot_e[:], AX, ALU.add))
                        dve.wait_ge(s_rows[b], (t + 1) * (16 * C))
                        ch.done(v.tensor_tensor(dot_h[:], fo[b][:, :, 0:F], rows[b][:, :, 0:F], ALU.mult))
                        ch.done(v.tensor_reduce(sh[:], dot_h[:], AX, ALU.add))
                        ch.done(v.tensor_tensor(sh[:], sh[:], rows[b][:, :, F], ALU.mult))
                        ch.done(v.tensor_tensor(sh[:], sh[:], fo[b][:, :, FILL_S - 1], ALU.add))
                        ch.done(v.tensor_tensor(sh[:], sh[:], se[:], ALU.add))
                        ch.done(v.tensor_tensor(sh[:], sh[:], rows[b][:, :, F + 1], ALU.add))
                        ch.step(v.tensor_copy(top[b][:, 0:1], top[1 - b][:, C:C + 1]))
                        ch.done(v.tensor_tensor_scan(top[b][:, 1:], k.pen[:, at], sh[:], top[1 - b][:, C:C + 1], ALU.add, ALU.max))
                        ch.done(v.tensor_tensor(arg[:, 0], top[b][:, 0:C], k.pen[:, at], ALU.add))
                        ch.step(v.tensor_tensor(arg[:, 0], arg[:, 0], top[b][:, 1:], ALU.subtract))
                        ch.done(v.tensor_tensor(arg[:, 1], sh[:], top[b][:, 1:], ALU.subtract))
                        v.tensor_scalar(arg[:, 1], arg[:, 1], 20.0, None, ALU.min).then_inc(s_arg, 1)
                        dve.wait_ge(s_exp, t * 2 + b + 1)
                        v.tensor_copy(val[:, :, F], ex[:, 1])
                        v.tensor_tensor(val[:, :, 0:F], rows[b][:, :, 0:F], bc(ex[:, 1], F), ALU.mult).then_inc(s_used[b], 1)
                        dve.wait_ge(s_used[b], t + 2)
                        dve.wait_ge(s_stored[b], (t + 1) * 16)
                        v.tensor_copy(sums[b][:, :, F + 1], top[b][:, 1:])
                        scan_columns(nc, sums[b], ex[:, 0], val[:], sums[1 - b][:, C - 1, :], F + 1).then_inc(s_sums[b], 1)
                        dve.wait_ge(s_sums[b], t + 1)
                assert ch.n - n0 == PER, ch.n - n0
                dve.wait_ge(s_sums[1], PAIRS)
                v.tensor_copy(k.tail[:], sums[1][:, C - 1, :]).then_inc(s_arg, 1)

        clear(nc, ph.sems)


def layer_update(nc, k, i, layer):
    with ExitStack() as ctx:
        ph = Phase(nc, ctx, "update")
        proj_, norm = Projector(ph, k.ident), Norm(ph)
        wm, wt, wb = ph.sb("wm", [F, F]), ph.sb("wt", [F, F]), ph.sb("wb", [F, F])
        left, eye, wz = ph.sb("left", [F, 2 * F]), ph.sb("eye", [F, 2 * F]), ph.sb("wz", [2 * F, F])
        go, bo = ph.sb("go", [P, F]), ph.sb("bo", [P, F])
        ha, z, lz = ph.sb("ha", [P, NT, 2 * F]), ph.sb("z", [P, NT, F]), ph.sb("lz", [P, NT, F])
        den = ph.sb("den", [P, NT])
        s_w, s_step, s_wt, s_wtc, s_prod, s_ready = (ph.sem(n) for n in ("s_w", "s_step", "s_wt", "s_wtc", "s_prod", "s_ready"))
        of = lambda name: i[f"L0_gnn_{name}"][bass.ds(layer, 1)]
        with nc.Block() as block:
            @block.sync
            def _(sp):
                sp.dma_start(wm[:], of("Wm").rearrange("l a b -> (l a) b")).then_inc(s_w, 16)
                sp.dma_start(wt[:], of("Wu")[:, 0:F].rearrange("l a b -> (l a) b")).then_inc(s_w, 16)
                sp.dma_start(wb[:], of("Wu")[:, F:2 * F].rearrange("l a b -> (l a) b")).then_inc(s_w, 16)
                sp.dma_start(go[:], of("go").to_broadcast([P, F])).then_inc(s_w, 16)
                sp.dma_start(bo[:], of("bo").to_broadcast([P, F])).then_inc(s_w, 16)

            @block.tensor
            def _(pe):
                pe.wait_ge(s_w, 80)
                nc.tensor.transpose(proj_.psp[1][0:F, 0, 0:F], wm[:], k.ident[0:F, 0:F]).then_inc(s_wt, 1)
                pe.wait_ge(s_wtc, 1)
                nc.tensor.matmul(proj_.psp[1][0:2 * F, 0, 0:F], eye[:], wt[:], start=True, stop=False)
                nc.tensor.matmul(proj_.psp[1][0:2 * F, 0, 0:F], left[:], wb[:], start=False, stop=True).then_inc(s_prod, 1)
                pe.wait_ge(s_ready, 1)
                proj_.pe(pe, lambda t: ha[:, t, :], 2 * F, wz[:], F)

            @block.scalar
            def _(act):
                proj_.act(act, 2 * F)
                norm.act(act)

            @block.vector
            def _(dve):
                v = nc.vector
                ch = Chain(dve, s_step)
                v.memset(left[:], 0.0)
                ch.done(v.memset(eye[:], 0.0))
                ch.done(v.tensor_copy(eye[:, 0:F], k.ident[0:F, 0:F]))
                dve.wait_ge(s_wt, 1)
                ch.done(v.tensor_copy(left[:, F:], proj_.psp[1][0:F, 0, 0:F]))
                dve.sem_inc(s_wtc, 1)
                ch.done(v.tensor_scalar(den[:], k.agg[:, :, F], 1e-10, None, ALU.add))
                ch.done(v.reciprocal(den[:], den[:]))
                ch.step(v.tensor_tensor(ha[:, :, F:], k.agg[:, :, 0:F], bc(den[:], F), ALU.mult))
                ch.done(v.tensor_copy(ha[:, :, 0:F], k.h[:]))
                dve.wait_ge(s_prod, 1)
                ch.done(v.tensor_copy(wz[:], proj_.psp[1][0:2 * F, 0, 0:F]))
                dve.sem_inc(s_ready, 1)
                proj_.dve(dve, z, F)
                ch.done(v.tensor_scalar(lz[:], z[:], 0.01, None, ALU.mult))
                ch.done(v.tensor_tensor(z[:], z[:], lz[:], ALU.max))
                ch.done(v.tensor_tensor(z[:], z[:], k.h[:], ALU.add))
                dve.wait_ge(s_w, 80)
                norm.dve(dve, ch, z[:], k.h[:], go[:], bo[:])

        clear(nc, ph.sems)


def next_tables(nc, k, stage, out):
    with ExitStack() as ctx:
        ph = Phase(nc, ctx, f"next{stage}")
        norm = Norm(ph)
        t1, t2 = ph.sb("t1", [P, NT, F]), ph.sb("t2", [P, NT, F])
        cnt = ph.sb("cnt", [P, NT])
        s_step, s_tab, s_out, s_w = (ph.sem(n) for n in ("s_step", "s_tab", "s_out", "s_w"))
        y = k.y
        block = ph.block()

        @block.sync
        def _(sp):
            sp.wait_ge(s_tab, 1)
            if stage == 3:
                full, rest = N // NT, N % NT
                sp.dma_start(out[0:full * NT].rearrange("(p t) f -> p t f", t=NT), k.x[0:full]).then_inc(s_out, 16)
                sp.dma_start(out[full * NT:N].rearrange("(p t) f -> p t f", p=1), k.x[full:full + 1, 0:rest]).then_inc(s_out, 16)
                sp.wait_ge(s_out, 32)
            else:
                sp.dma_start(k.table2.rearrange("(p t) f -> p t f", p=P), y[:]).then_inc(s_out, 16)
                sp.wait_ge(s_out, 16)

        @block.gpsimd
        def _(pool):
            if stage == 0:
                pool.wait_ge(s_tab, 1)
                for t in range(NT):
                    scatter(nc, k.fill_d, k.start[0][:, t:t + 1], y[:, t, :], EP - 1).then_inc(s_w, 16)
                pool.wait_ge(s_w, 16 * NT)

        @block.scalar
        def _(act):
            norm.act(act)
            if stage in (1, 2):
                norm.act(act)

        @block.vector
        def _(dve):
            v = nc.vector
            ch = Chain(dve, s_step)
            if stage == 0:
                ch.done(v.tensor_tensor(t1[:], k.x[:], k.h[:], ALU.add))
            elif stage == 1:
                ch.done(v.tensor_tensor(t1[:], bc(k.count[0][:], F), rows_of(k.b3[:], NT), ALU.mult))
                ch.done(v.tensor_tensor(t1[:], t1[:], k.agg2[:], ALU.add))
                ch.done(v.tensor_scalar(cnt[:], k.count[0][:], 1.0, None, ALU.max))
                ch.done(v.reciprocal(cnt[:], cnt[:]))
                ch.done(v.tensor_tensor(t1[:], t1[:], bc(cnt[:], F), ALU.mult))
                ch.done(v.tensor_tensor(t1[:], t1[:], k.x[:], ALU.add))
                ch.done(v.tensor_tensor(t1[:], t1[:], k.x[:], ALU.add))
            else:
                src = k.agg2
                if stage == 3:
                    ch.done(v.tensor_tensor(t2[:], k.agg2[:], y[:], ALU.add))
                    src = t2
                ch.done(v.tensor_tensor(t1[:], src[:], bc(k.dinv[:], F), ALU.mult))
                ch.done(v.tensor_tensor(t1[:], t1[:], k.x[:], ALU.add))
            norm.dve(dve, ch, t1[:], k.x[:])
            if stage == 0:
                ch.done(v.tensor_copy(y[:], k.x[:]))
            elif stage in (1, 2):
                if stage == 1:
                    ch.done(v.tensor_scalar(norm.stat[:], k.count[1][:], 1.0, None, ALU.max))
                else:
                    ch.done(v.tensor_scalar(norm.stat[:], k.count[1][:], 1.0, None, ALU.add))
                norm.rsqrt(dve, ch)
                ch.done(v.tensor_copy(k.dinv[:], norm.stat[:]))
                ch.done(v.tensor_tensor(y[:], k.x[:], bc(k.dinv[:], F), ALU.mult))
            dve.sem_inc(s_tab, 1)


def sum_pass(nc, k, weighted):
    with ExitStack() as ctx:
        ph = Phase(nc, ctx, f"sum{int(weighted)}")
        staged = ph.sb("staged", [P, 2, C], I32)
        rows = [ph.sb(f"rows{b}", [P, C, F]) for b in range(2)]
        sums = [ph.sb(f"sums{b}", [P, C, F]) for b in range(2)]
        val = ph.sb("val", [P, C, F])
        s_go, s_staged, s_step, s_turn = (ph.sem(n) for n in ("s_go", "s_staged", "s_step", "s_turn"))
        s_rows, s_used, s_sums, s_stored = ([ph.sem(f"{n}{b}") for b in range(2)] for n in ("s_rows", "s_used", "s_sums", "s_stored"))
        block = ph.block()

        @block.gpsimd
        def _(pool):
            pool.wait_ge(s_go, 1)
            pool_gathers(nc, pool, k.other[0], staged, rows, F, k.table2, s_staged, s_rows,
                         [[(s_used[b], 1)] for b in range(2)], s_turn)

        @block.sync
        def _(sp):
            sp.sem_inc(s_go, 1)
            store = store_sums(sp, k, k.sum, sums, s_sums, s_stored)
            with sp.Fori(0, PAIRS) as t:
                for b in range(2):
                    store(t, b)
            for b in range(2):
                sp.wait_ge(s_stored[b], 16 * (PAIRS + 1))

        @block.vector
        def _(dve):
            v = nc.vector
            ch = Chain(dve, s_step)
            for b in range(2):
                dve.sem_inc(s_used[b], 1)
            ch.done(v.memset(sums[1][:, C - 1, :], 0.0))
            PER, n0 = 2 * int(weighted), ch.n
            with dve.Fori(0, PAIRS) as t:
                ch.n, ch.base = n0, t * PER
                for b in range(2):
                    at = bass.ds((t * 2 + b) * C, C)
                    dve.wait_ge(s_rows[b], (t + 1) * (16 * C))
                    src = rows[b]
                    if weighted:
                        ch.done(v.tensor_tensor(val[:], rows[b][:], bc(k.weight[:, at], F), ALU.mult))
                        src = val
                    dve.wait_ge(s_stored[b], (t + 1) * 16)
                    scan_columns(nc, sums[b], k.keepr[0][:, at], src[:], sums[1 - b][:, C - 1, :], F).then_inc(s_sums[b], 1)
                    dve.wait_ge(s_sums[b], t + 1)
                    dve.sem_inc(s_used[b], 1)
            dve.wait_ge(s_sums[1], PAIRS)
            v.tensor_copy(k.tail[:, 0:F], sums[1][:, C - 1, :]).then_inc(s_go, 1)


def mlp_pass(nc, k, i):
    X = 2 * F + EF
    with ExitStack() as ctx:
        ph = Phase(nc, ctx, "mlp")
        staged = ph.sb("staged", [P, 2, C], I32)
        xin = [ph.sb(f"xin{b}", [P, C, X]) for b in range(2)]
        fin = [ph.sb(f"fin{b}", [P, C, F]) for b in range(2)]
        edge = [ph.sb(f"edge{b}", [P, C, EF]) for b in range(2)]
        sums = [ph.sb(f"sums{b}", [P, C, F]) for b in range(2)]
        val = [ph.sb(f"val{b}", [P, C, F]) for b in range(2)]
        init = ph.sb("init", [P, F])
        w1, w2, w3 = ph.sb("w1", [X, HID]), ph.sb("w2", [HID, HID]), ph.sb("w3", [HID, F])
        b1, b2 = ph.sb("b1", [HID, 1]), ph.sb("b2", [HID, 1])
        xT, h1, h2 = ([ph.sb(f"{n}{b}", [P, COLS * P]) for b in range(2)] for n in ("xT", "h1", "h2"))
        ps_t, ps_1, ps_2, ps_3 = ([ph.ps(f"{n}{b}", [P, 512]) for b in range(2)] for n in ("ps_t", "ps_1", "ps_2", "ps_3"))
        s_w, s_init, s_staged, s_step, s_join, s_turn = (ph.sem(n) for n in ("s_w", "s_init", "s_staged", "s_step", "s_join", "s_turn"))
        s_rows, s_load, s_used, s_sums, s_stored = ([ph.sem(f"{n}{b}") for b in range(2)] for n in ("s_rows", "s_load", "s_used", "s_sums", "s_stored"))
        s_t, s_tc, s_1, s_1a, s_2, s_2a, s_3, s_3c = (ph.sem(n) for n in ("s_t", "s_tc", "s_1", "s_1a", "s_2", "s_2a", "s_3", "s_3c"))
        cols = lambda g: min(COLS, C - g * COLS)
        block = ph.block()

        @block.gpsimd
        def _(pool):
            gather(nc, init[:], k.table2, k.first[0][:, 0:1]).then_inc(s_init, 16)
            pool.wait_ge(s_init, 16)
            pool_gathers(nc, pool, k.other[0], staged, xin, F, k.table2, s_staged, s_rows,
                         [[(s_used[b], 1)] for b in range(2)], s_turn)

        @block.sync
        def _(sp):
            for to, name in ((w1, "W1"), (w2, "W2"), (w3, "W3")):
                sp.dma_start(to[:], i[f"L1_gnn_{name}"]).then_inc(s_w, 16)
            sp.dma_start(b1[:], column(i["L1_gnn_b1"])).then_inc(s_w, 16)
            sp.dma_start(b2[:], column(i["L1_gnn_b2"])).then_inc(s_w, 16)
            sp.dma_start(k.b3[:], i["L1_gnn_b3"].partition_broadcast(P)).then_inc(s_w, 16)

            def load(t, b):
                at = bass.ds((t * 2 + b) * C, C)
                sp.wait_ge(s_used[b], t + 1)
                sp.dma_start(edge[b][:], k.edges_d.rearrange("(p j) w -> p j w", p=P)[:, at, :]).then_inc(s_load[b], 16)
                sp.dma_start(fin[b][:], k.fill_d.rearrange("(p j) w -> p j w", p=P)[:, at, :]).then_inc(s_load[b], 16)

            stream(sp, load, store_sums(sp, k, k.sum, sums, s_sums, s_stored))
            for b in range(2):
                sp.wait_ge(s_stored[b], 16 * (PAIRS + 1))

        @block.tensor
        def _(pe):
            pe.wait_ge(s_w, 96)
            with pe.Fori(0, PAIRS) as t:
                for b in range(2):
                    pe.wait_ge(s_rows[b], (t + 1) * (16 * C))
                    pe.wait_ge(s_join, t * 2 + b + 1)
                    for s in range(STEPS + 3):
                        n = (t * 2 + b) * STEPS + s
                        q = (b * STEPS + s) % 2
                        if s < STEPS:
                            pe.wait_ge(s_tc, n + 1)
                            for c in range(cols(s)):
                                ins = nc.tensor.transpose(ps_t[q][0:X, c * P:(c + 1) * P], xin[b][:, s * COLS + c, :], k.ident[:])
                            ins.then_inc(s_t, 1)
                        if 1 <= s <= STEPS:
                            w = cols(s - 1) * P
                            pe.wait_ge(s_tc, n + 2)
                            pe.wait_ge(s_1a, n)
                            nc.tensor.matmul(ps_1[1 - q][:, 0:w], w1[:], xT[1 - q][0:X, 0:w], start=True, stop=True).then_inc(s_1, 1)
                        if 2 <= s <= STEPS + 1:
                            w = cols(s - 2) * P
                            pe.wait_ge(s_1a, n + 1)
                            pe.wait_ge(s_2a, n - 1)
                            nc.tensor.matmul(ps_2[q][:, 0:w], w2[:], h1[q][:, 0:w], start=True, stop=True).then_inc(s_2, 1)
                        if s >= 3:
                            pe.wait_ge(s_2a, n)
                            pe.wait_ge(s_3c, n - 2)
                            for c in range(cols(s - 3)):
                                ins = nc.tensor.matmul(ps_3[1 - q][:, c * F:(c + 1) * F], h2[1 - q][:, c * P:(c + 1) * P], w3[:], start=True, stop=True)
                            ins.then_inc(s_3, 1)

        @block.scalar
        def _(act):
            act.sem_inc(s_1a, 2)
            act.sem_inc(s_2a, 2)
            act.sem_inc(s_tc, 2)
            act.wait_ge(s_w, 96)
            with act.Fori(0, PAIRS) as t:
                for b in range(2):
                    for s in range(STEPS + 2):
                        n = (t * 2 + b) * STEPS + s
                        q = (b * STEPS + s) % 2
                        if s < STEPS:
                            w = cols(s) * P
                            act.wait_ge(s_t, n + 1)
                            nc.scalar.activation(xT[q][0:X, 0:w], ps_t[q][0:X, 0:w], ACT.Copy).then_inc(s_tc, 1)
                        if 1 <= s <= STEPS:
                            w = cols(s - 1) * P
                            act.wait_ge(s_1, n)
                            nc.scalar.activation(h1[1 - q][:, 0:w], ps_1[1 - q][:, 0:w], ACT.Relu, bias=b1[:]).then_inc(s_1a, 1)
                        if s >= 2:
                            w = cols(s - 2) * P
                            act.wait_ge(s_2, n - 1)
                            nc.scalar.activation(h2[q][:, 0:w], ps_2[q][:, 0:w], ACT.Relu, bias=b2[:]).then_inc(s_2a, 1)

        @block.vector
        def _(dve):
            v = nc.vector
            ch = Chain(dve, s_step)
            dve.sem_inc(s_3c, 2)
            for b in range(2):
                dve.sem_inc(s_used[b], 1)
            ch.done(v.memset(sums[1][:, C - 1, :], 0.0))
            dve.wait_ge(s_init, 16)
            ch.done(v.tensor_copy(xin[1][:, C - 1, F:2 * F], init[:]))
            with dve.Fori(0, PAIRS) as t:
                for b in range(2):
                    at = bass.ds((t * 2 + b) * C, C)
                    dve.wait_ge(s_load[b], (t + 1) * 32)
                    v.tensor_copy(xin[b][:, :, 2 * F:], edge[b][:, :, 0:EF])
                    scan_columns(nc, xin[b][:, :, F:2 * F], k.keep[0][:, at], fin[b][:], xin[1 - b][:, C - 1, F:2 * F], F).then_inc(s_join, 1)
                    for g in range(STEPS):
                        c0, w = g * COLS, cols(g)
                        dve.wait_ge(s_3, (t * 2 + b) * STEPS + g + 1)
                        v.tensor_copy(val[b][:, c0:c0 + w, :], ps_3[(b * STEPS + g) % 2][:, 0:w * F].rearrange("p (c f) -> p c f", f=F)).then_inc(s_3c, 1)
                    dve.wait_ge(s_3c, (t * 2 + b + 1) * STEPS + 2)
                    dve.sem_inc(s_used[b], 1)
                    dve.wait_ge(s_stored[b], (t + 1) * 16)
                    scan_columns(nc, sums[b], k.keepr[0][:, at], val[b][:], sums[1 - b][:, C - 1, :], F).then_inc(s_sums[b], 1)
                    dve.wait_ge(s_sums[b], t + 1)
            dve.wait_ge(s_sums[1], PAIRS)
            v.tensor_copy(k.tail[:, 0:F], sums[1][:, C - 1, :]).then_inc(s_step, 1)


class Shared:
    pass


def program(nc, i, out):
    k = Shared()
    dram = lambda name, shape, dt=F32: nc.dram_tensor(name, shape, dt).ap()
    k.sorted = dram("sorted_records", [ORDERS, 1 + SORT_N], I32)
    k.raw_s, k.raw_d = dram("raw_s", [EP, REC_S]), dram("raw_d", [EP, REC_D])
    k.edges_s, k.edges_d = dram("edges_s", [EP, REC_S]), dram("edges_d", [EP, EF])
    k.fill_s, k.fill_d = dram("fill_s", [EP, FILL_S]), dram("fill_d", [EP, F])
    k.lastpos = [dram(f"lastpos{o}", [NP, 1]) for o in range(ORDERS)]
    k.by_type = dram("by_type", [P, 2 * G])
    k.table0, k.table1, k.table2 = dram("table0", [NP, F + G + 1]), dram("table1", [NP, ACC]), dram("table2", [NP, F])
    k.fillrows = dram("fillrows", [NP, FILL_S])
    k.spare = dram("spare", [2, 1])
    k.acc, k.sum = dram("acc_rows", [EP + 1, ACC]), dram("sum_rows", [EP + 1, F])
    with ExitStack() as ctx:
        sb = lambda n, s, d=F32: ctx.enter_context(nc.sbuf_tensor(n, s, d))
        k.ident, k.ones, k.iota = sb("ident", [P, P]), sb("ones", [P, P]), sb("iota", [P, P])
        k.below, k.above, k.rowstart = sb("below", [P, P]), sb("above", [P, P]), sb("rowstart", [P, 1])
        constants(nc, k)
        k.unsorted = sb("unsorted", [1, 1], I32)
        sort_edges(nc, i, k, 1, first=True)
        unsorted = nc.values_load(k.unsorted[0:1, 0:1], min_val=0, max_val=1)
        with nc.If(unsorted > 0):
            sort_edges(nc, i, k, 0, first=False)
        k.keep = [sb(f"keep{o}", [P, J]) for o in range(ORDERS)]
        k.keepr = [sb(f"keepr{o}", [P, J]) for o in range(ORDERS)]
        k.pen, k.weight = sb("pen", [P, J]), sb("weight", [P, J])
        k.other = [sb(f"other{o}", [P, J], I32) for o in range(ORDERS)]
        k.first = [sb(f"first{o}", [P, 1], I32) for o in range(ORDERS)]
        k.firstf, k.lastf = ([sb(f"{n}{o}", [P, 1]) for o in range(ORDERS)] for n in ("firstf", "lastf"))
        k.count = [sb(f"count{o}", [P, NT]) for o in range(ORDERS)]
        k.start, k.end = ([sb(f"{n}{o}", [P, NT], I32) for o in range(ORDERS)] for n in ("start", "end"))
        k.cread, k.cwrite = ([sb(f"{n}{o}", [P, 1], I32) for o in range(ORDERS)] for n in ("cread", "cwrite"))
        k.mask = [sb(f"mask{o}", [P, P]) for o in range(ORDERS)]
        with ExitStack() as own:
            k.keyf = [own.enter_context(nc.sbuf_tensor(f"keyf{o}", [P, J], F32)) for o in range(ORDERS)]
            k.perm = [own.enter_context(nc.sbuf_tensor(f"perm{o}", [P, J], I32)) for o in range(ORDERS)]
            for o in range(ORDERS):
                unpack(nc, k, o)
            edge_records(nc, i, k)
            with nc.If(unsorted > 0):
                dst_records(nc, k)
            for o in range(ORDERS):
                segments(nc, k, o)
        k.x, k.h, k.y = sb("x", [P, NT, F]), sb("h", [P, NT, F]), sb("y", [P, NT, F])
        k.logm, k.dinv, k.b3 = sb("logm", [P, NT]), sb("dinv", [P, NT]), sb("b3", [P, F])
        k.tail = sb("tail", [P, ACC])
        with ExitStack() as own:
            k.agg = own.enter_context(nc.sbuf_tensor("agg", [P, NT, ACC], F32))
            node_inputs(nc, k, i)
            first_pass(nc, k, i)
            collect(nc, k, 1, k.acc, ACC, k.tail[:], k.agg, False, "collect_first")
            after_first(nc, k, i)
            with nc.Fori(0, LAYERS) as layer:
                layer_tables(nc, k, i, layer)
                attend(nc, k)
                collect(nc, k, 1, k.acc, ACC, k.tail[:], k.agg, True, "collect_layer")
                layer_update(nc, k, i, layer)
        k.agg2 = sb("agg2", [P, NT, F])
        next_tables(nc, k, 0, out)
        mlp_pass(nc, k, i)
        collect(nc, k, 0, k.sum, F, k.tail[:, 0:F], k.agg2, False, "collect_mlp")
        next_tables(nc, k, 1, out)
        sum_pass(nc, k, True)
        collect(nc, k, 0, k.sum, F, k.tail[:, 0:F], k.agg2, False, "collect_weighted")
        next_tables(nc, k, 2, out)
        sum_pass(nc, k, False)
        collect(nc, k, 0, k.sum, F, k.tail[:, 0:F], k.agg2, False, "collect_plain")
        next_tables(nc, k, 3, out)


_INS = ["x", "src", "dst", "edge_attr_16", "edge_attr_40", "edge_weight", "node_type_119", "node_vec",
        "L0_gnn_Wq", "L0_gnn_gq", "L0_gnn_bq", "L0_gnn_Wk", "L0_gnn_gk", "L0_gnn_bk", "L0_gnn_Wm", "L0_gnn_Wu",
        "L0_gnn_go", "L0_gnn_bo", "L0_gnn_F1W", "L0_gnn_F1b", "L0_gnn_F2W", "L0_gnn_F2b", "L0_gnn_gn", "L0_gnn_bn",
        "L0_gnn_emb", "L0_gnn_adapt", "L1_gnn_W1", "L1_gnn_b1", "L1_gnn_W2", "L1_gnn_b2", "L1_gnn_W3", "L1_gnn_b3"]


def kernel(**inputs):
    import numpy as _np
    import concourse.bacc as _bacc
    from concourse import mybir as _mybir
    from concourse.bass_utils import run_bass_kernel_spmd as _run

    nc = _bacc.Bacc("TRN2", target_bir_lowering=False, num_devices=1)
    arrays, args = {}, {}
    for name in _INS:
        a = _np.ascontiguousarray(inputs[name])
        arrays[f"in_{name}_dram"] = a
        args[name] = nc.dram_tensor(f"in_{name}_dram", a.shape, _mybir.dt.from_np(a.dtype), kind="ExternalInput").ap()
    out = nc.dram_tensor("out_0_dram", (N, F), F32, kind="ExternalOutput").ap()
    program(nc, args, out)
    r = _run(nc, [arrays], core_ids=[0])
    return r.results[0]["out_0_dram"]
```
